# Optimizing a Trainium2 kernel written in Bass

```python
import numpy as np
import jax
import jax.numpy as jnp

def _softmax(x, axis=-1):
    return jax.nn.softmax(x, axis=axis)

def _gelu(x):
    return jax.nn.gelu(x, approximate=True)

def _silu(x):
    return jax.nn.silu(x)

def _sigmoid(x):
    return jax.nn.sigmoid(x)

def _layernorm(x, axis=-1, eps=1e-05):
    m = jnp.mean(x, axis=axis, keepdims=True)
    v = jnp.var(x, axis=axis, keepdims=True)
    return (x - m) / jnp.sqrt(v + eps)

def _scatter_add(tgt, idx, src, axis=0):
    return tgt.at[idx].add(src)

def _segment_sum(src, seg, n):
    return jax.ops.segment_sum(src, seg, n)
kernel_name = 'mk_adaln_ffn_d2_seqx_r8_12a081'

def setup_inputs(seed: int=0):
    np.random.seed(seed)
    _w = jnp.asarray

    def _rec_inputs():
        import jax
        import jax.numpy as jnp
        _rk = jax.random.key(seed)
        x = 7.22e-05 + 1 * jax.random.normal(jax.random.fold_in(_rk, 1), (8, 128, 512), jnp.float32)
        _lenS = 128 - jax.random.randint(jax.random.fold_in(_rk, 7), (8,), 0, max(1, 128 // 4) + 1, jnp.int32)
        _lenS2 = 128 - jax.random.randint(jax.random.fold_in(_rk, 8), (8,), 0, max(1, 128 // 4) + 1, jnp.int32)
        itok_B_2_6 = jax.random.randint(jax.random.fold_in(_rk, 11), (8,), 2, 7, jnp.int32)
        itok_B_0_23 = jax.random.randint(jax.random.fold_in(_rk, 12), (8,), 0, 24, jnp.int32)
        return (x, itok_B_2_6, itok_B_0_23)
    x, itok_B_2_6, itok_B_0_23 = _rec_inputs()

    def _L0_cond_setup():
        import jax, jax.numpy as jnp
        import numpy as np
        B, N, H, F = (4, 64, 512, 1376)
        L, R, RANK = (1, 16, 16)
        SCALE = 0.5
        key = jax.random.key(seed)
        ks = jax.random.split(key, 12)
        nrm = lambda k, shape, fan: jax.random.normal(k, shape, jnp.float32) * fan ** (-0.5)
        inp = {'x': jax.random.normal(ks[0], (B, N, H), jnp.float32), 'W_gate': nrm(ks[1], (F, H), H), 'W_up': nrm(ks[2], (F, H), H), 'W_down': nrm(ks[3], (H, F), F), 'A_gate': nrm(ks[4], (L, R, RANK, H), H), 'B_gate': nrm(ks[5], (L, R, F, RANK), RANK), 'A_up': nrm(ks[6], (L, R, RANK, H), H), 'B_up': nrm(ks[7], (L, R, F, RANK), RANK), 'A_down': nrm(ks[8], (L, R, RANK, F), F), 'B_down': nrm(ks[9], (L, R, H, RANK), RANK), 'lora_indices': jax.random.randint(ks[10], (B,), 0, R), 'layer_idx': 0}
        return inp
    _L0_cond_all = _L0_cond_setup()
    _L0_cond_in = {k: v for k, v in _L0_cond_all.items() if k in ('W_gate', 'W_up', 'W_down', 'A_gate', 'B_gate', 'A_up', 'B_up', 'A_down', 'B_down')}
    del _L0_cond_all

    def _L0_ffn_setup():
        import jax, jax.numpy as jnp
        import numpy as np
        B, S, H, I, R = (4, 32, 512, 1792, 4)

        def _anemll_linear(x, w, su, sv):
            w_eff = w * (su @ sv)
            return jnp.einsum('bsh,oh->bso', x, w_eff)
        key = jax.random.key(seed)
        ks = jax.random.split(key, 10)
        sd = 0.02
        return {'x': jax.random.normal(ks[0], (B, S, H), dtype=jnp.float32), 'gate_w': jax.random.normal(ks[1], (I, H), dtype=jnp.float32) * sd, 'gate_su': jax.random.normal(ks[2], (I, R), dtype=jnp.float32) * 0.5, 'gate_sv': jax.random.normal(ks[3], (R, H), dtype=jnp.float32) * 0.5, 'up_w': jax.random.normal(ks[4], (I, H), dtype=jnp.float32) * sd, 'up_su': jax.random.normal(ks[5], (I, R), dtype=jnp.float32) * 0.5, 'up_sv': jax.random.normal(ks[6], (R, H), dtype=jnp.float32) * 0.5, 'down_w': jax.random.normal(ks[7], (H, I), dtype=jnp.float32) * sd, 'down_su': jax.random.normal(ks[8], (H, R), dtype=jnp.float32) * 0.5, 'down_sv': jax.random.normal(ks[9], (R, I), dtype=jnp.float32) * 0.5}
    _L0_ffn_all = _L0_ffn_setup()
    _L0_ffn_in = {k: v for k, v in _L0_ffn_all.items() if k in ('gate_w', 'gate_su', 'gate_sv', 'up_w', 'up_su', 'up_sv', 'down_w', 'down_su', 'down_sv')}
    del _L0_ffn_all

    def _L1_cond_setup():
        import jax, jax.numpy as jnp
        import numpy as np
        R = 16
        ALPHA = 32
        SCALING = ALPHA / R
        SLOTS = 32
        IN_F = 512
        OUT_F = 512
        B, T = (8, 128)
        key = jax.random.key(seed)
        k1, k2, k3, k4, k5, k6 = jax.random.split(key, 6)
        x = jax.random.normal(k1, (B, T, IN_F), dtype=jnp.float32)
        adapter_mapping = jax.random.randint(k2, (B,), 0, SLOTS, dtype=jnp.int32)
        W = jax.random.normal(k3, (OUT_F, IN_F), dtype=jnp.float32) * 0.02
        b = jax.random.normal(k4, (OUT_F,), dtype=jnp.float32) * 0.02
        lora_As = jax.random.normal(k5, (SLOTS, IN_F, R), dtype=jnp.float32) * 0.02
        lora_Bs = jax.random.normal(k6, (SLOTS, R, OUT_F), dtype=jnp.float32) * 0.02
        return {'x': x, 'adapter_mapping': adapter_mapping, 'W': W, 'b': b, 'lora_As': lora_As, 'lora_Bs': lora_Bs}
    _L1_cond_all = _L1_cond_setup()
    _L1_cond_in = {k: v for k, v in _L1_cond_all.items() if k in ('W', 'b', 'lora_As', 'lora_Bs')}
    del _L1_cond_all

    def _L1_ffn_setup():
        import jax, jax.numpy as jnp
        import numpy as np
        H = 512
        I = 1792
        G = 128

        def dequant(q, s, g=G):
            O, In = q.shape
            return (q.reshape(O, In // g, g).astype(s.dtype) * s[:, :, None]).reshape(O, In)
        key = jax.random.key(seed)
        ks = jax.random.split(key, 7)
        x = jax.random.normal(ks[0], (2, 256, H), dtype=jnp.float32)

        def mk_qlinear(kq, ksc, out_d, in_d):
            q = jax.random.randint(kq, (out_d, in_d), -8, 8, dtype=jnp.int32)
            s = jax.random.uniform(ksc, (out_d, in_d // G), dtype=jnp.float32, minval=0.005, maxval=0.02)
            return (q, s)
        gate_q, gate_s = mk_qlinear(ks[1], ks[2], I, H)
        up_q, up_s = mk_qlinear(ks[3], ks[4], I, H)
        down_q, down_s = mk_qlinear(ks[5], ks[6], H, I)
        return {'x': x, 'gate_q': gate_q, 'gate_s': gate_s, 'up_q': up_q, 'up_s': up_s, 'down_q': down_q, 'down_s': down_s}
    _L1_ffn_all = _L1_ffn_setup()
    _L1_ffn_in = {k: v for k, v in _L1_ffn_all.items() if k in ('gate_q', 'gate_s', 'up_q', 'up_s', 'down_q', 'down_s')}
    del _L1_ffn_all
    return {'x': x, 'itok_B_2_6': itok_B_2_6, 'itok_B_0_23': itok_B_0_23, 'L0_cond_W_gate': _L0_cond_in['W_gate'], 'L0_cond_W_up': _L0_cond_in['W_up'], 'L0_cond_W_down': _L0_cond_in['W_down'], 'L0_cond_A_gate': _L0_cond_in['A_gate'], 'L0_cond_B_gate': _L0_cond_in['B_gate'], 'L0_cond_A_up': _L0_cond_in['A_up'], 'L0_cond_B_up': _L0_cond_in['B_up'], 'L0_cond_A_down': _L0_cond_in['A_down'], 'L0_cond_B_down': _L0_cond_in['B_down'], 'L0_ffn_gate_w': _L0_ffn_in['gate_w'], 'L0_ffn_gate_su': _L0_ffn_in['gate_su'], 'L0_ffn_gate_sv': _L0_ffn_in['gate_sv'], 'L0_ffn_up_w': _L0_ffn_in['up_w'], 'L0_ffn_up_su': _L0_ffn_in['up_su'], 'L0_ffn_up_sv': _L0_ffn_in['up_sv'], 'L0_ffn_down_w': _L0_ffn_in['down_w'], 'L0_ffn_down_su': _L0_ffn_in['down_su'], 'L0_ffn_down_sv': _L0_ffn_in['down_sv'], 'L1_cond_W': _L1_cond_in['W'], 'L1_cond_b': _L1_cond_in['b'], 'L1_cond_lora_As': _L1_cond_in['lora_As'], 'L1_cond_lora_Bs': _L1_cond_in['lora_Bs'], 'L1_ffn_gate_q': _L1_ffn_in['gate_q'], 'L1_ffn_gate_s': _L1_ffn_in['gate_s'], 'L1_ffn_up_q': _L1_ffn_in['up_q'], 'L1_ffn_up_s': _L1_ffn_in['up_s'], 'L1_ffn_down_q': _L1_ffn_in['down_q'], 'L1_ffn_down_s': _L1_ffn_in['down_s']}

def reference(x, itok_B_2_6, itok_B_0_23, L0_cond_W_gate, L0_cond_W_up, L0_cond_W_down, L0_cond_A_gate, L0_cond_B_gate, L0_cond_A_up, L0_cond_B_up, L0_cond_A_down, L0_cond_B_down, L0_ffn_gate_w, L0_ffn_gate_su, L0_ffn_gate_sv, L0_ffn_up_w, L0_ffn_up_su, L0_ffn_up_sv, L0_ffn_down_w, L0_ffn_down_su, L0_ffn_down_sv, L1_cond_W, L1_cond_b, L1_cond_lora_As, L1_cond_lora_Bs, L1_ffn_gate_q, L1_ffn_gate_s, L1_ffn_up_q, L1_ffn_up_s, L1_ffn_down_q, L1_ffn_down_s):
    import jax
    import jax.numpy as jnp

    def _L0_cond_ref(x, W_gate, W_up, W_down, A_gate, B_gate, A_up, B_up, A_down, B_down, lora_indices, layer_idx):
        import jax, jax.numpy as jnp
        import numpy as np
        B, N, H, F = (4, 64, 512, 1376)
        L, R, RANK = (1, 16, 16)
        SCALE = 0.5

        def lora_add(base, inp, A, B):
            Ab = A[layer_idx][lora_indices]
            Bb = B[layer_idx][lora_indices]
            t = jnp.einsum('bri,bni->bnr', Ab, inp)
            return base + jnp.einsum('bor,bnr->bno', Bb, t) * SCALE
        gate = lora_add(jnp.einsum('bnh,fh->bnf', x, W_gate), x, A_gate, B_gate)
        up = lora_add(jnp.einsum('bnh,fh->bnf', x, W_up), x, A_up, B_up)
        act = jax.nn.silu(gate) * up
        down = lora_add(jnp.einsum('bnf,hf->bnh', act, W_down), act, A_down, B_down)
        return down

    def _L0_ffn_ref(x, gate_w, gate_su, gate_sv, up_w, up_su, up_sv, down_w, down_su, down_sv):
        import jax, jax.numpy as jnp
        import numpy as np
        B, S, H, I, R = (4, 32, 512, 1792, 4)

        def _anemll_linear(x, w, su, sv):
            w_eff = w * (su @ sv)
            return jnp.einsum('bsh,oh->bso', x, w_eff)
        a = _anemll_linear(x, gate_w, gate_su, gate_sv)
        b = _anemll_linear(x, up_w, up_su, up_sv)
        d = jax.nn.silu(a) * b
        return _anemll_linear(d, down_w, down_su, down_sv)

    def _L1_cond_ref(x, adapter_mapping, W, b, lora_As, lora_Bs):
        import jax, jax.numpy as jnp
        import numpy as np
        R = 16
        ALPHA = 32
        SCALING = ALPHA / R
        SLOTS = 32
        IN_F = 512
        OUT_F = 512
        B, T = (8, 128)
        base_out = jnp.einsum('bti,oi->bto', x, W) + b
        A = lora_As[adapter_mapping]
        Bm = lora_Bs[adapter_mapping]
        lora_h = jnp.einsum('bti,bir->btr', x, A)
        lora_out = jnp.einsum('btr,bro->bto', lora_h, Bm)
        return base_out + lora_out * SCALING

    def _L1_ffn_ref(x, gate_q, gate_s, up_q, up_s, down_q, down_s):
        import jax, jax.numpy as jnp
        import numpy as np
        H = 512
        I = 1792
        G = 128

        def dequant(q, s, g=G):
            O, In = q.shape
            return (q.reshape(O, In // g, g).astype(s.dtype) * s[:, :, None]).reshape(O, In)
        Wg = dequant(gate_q, gate_s)
        Wu = dequant(up_q, up_s)
        Wd = dequant(down_q, down_s)
        gate_score = jax.nn.silu(jnp.einsum('bsh,ih->bsi', x, Wg))
        intermediate = gate_score * jnp.einsum('bsh,ih->bsi', x, Wu)
        return jnp.einsum('bsi,hi->bsh', intermediate, Wd)
    x = x + _L0_ffn_ref(_L0_cond_ref(x, L0_cond_W_gate, L0_cond_W_up, L0_cond_W_down, L0_cond_A_gate, L0_cond_B_gate, L0_cond_A_up, L0_cond_B_up, L0_cond_A_down, L0_cond_B_down, itok_B_2_6, 0), L0_ffn_gate_w, L0_ffn_gate_su, L0_ffn_gate_sv, L0_ffn_up_w, L0_ffn_up_su, L0_ffn_up_sv, L0_ffn_down_w, L0_ffn_down_su, L0_ffn_down_sv)
    x = x + _L1_ffn_ref(_L1_cond_ref(x, itok_B_0_23, L1_cond_W, L1_cond_b, L1_cond_lora_As, L1_cond_lora_Bs), L1_ffn_gate_q, L1_ffn_gate_s, L1_ffn_up_q, L1_ffn_up_s, L1_ffn_down_q, L1_ffn_down_s)
    return x

_drawn_inputs = setup_inputs


def setup_inputs(seed=0):
    import zlib

    import numpy as np

    out = dict(_drawn_inputs(seed))
    spreads = {}
    factors = {}
    for name, (base, spread) in spreads.items():
        noise = np.random.default_rng([zlib.crc32(name.encode()), seed]).standard_normal(out[name].shape)
        drawn = base * np.exp(spread * noise) if base else spread * noise
        out[name] = jnp.asarray(drawn.astype(out[name].dtype))
    for name, factor in factors.items():
        out[name] = (out[name] * factor).astype(out[name].dtype)
    return out
```

```python
from collections import namedtuple
from contextlib import ExitStack

import concourse.bass as bass
from concourse import mybir

F32 = mybir.dt.float32
F32R = mybir.dt.float32r
I32 = mybir.dt.int32
ALU = mybir.AluOpType
ACT = mybir.ActivationFunctionType

P = 128
H = 512
HK = H // P
TOK = 1024
CT = 512
CH = TOK // CT
NB = 8
BC = NB // CH
R = 16
RB = BC * R
F0 = 1376
F1 = 1792
F0_TAIL = F0 - F0 // P * P
SR = 4
WT = 1024
PACK = F1 + H

Phase = namedtuple("Phase", "name kind layer part tiles first t0 g0 d0 m0 raw0 loads prep")


def plan_phases():
    steps = [
        ("cond gate/up a", "gate_up", "cond", 0, 6, 0, 1, "split"),
        ("cond down a", "down", "cond", 0, HK, 0, 1, "split"),
        ("cond gate/up b", "gate_up", "cond", 1, 5, 6, 1, "split"),
        ("cond down b", "down", "cond", 1, HK, 6, 2, "split"),
        ("ffn0 gate/up a", "gate_up", "ffn0", 0, 7, 0, 1, "scale"),
        ("ffn0 down a", "down", "ffn0", 0, HK, 0, 1, "scale"),
        ("ffn0 gate/up b", "gate_up", "ffn0", 1, 7, 7, 1, "scale"),
        ("ffn0 down b", "down", "ffn0", 1, HK, 7, 1, "scale"),
        ("cond1", "down", "cond1", 0, HK, 0, 1, "split"),
        ("ffn1 gate/up a", "gate_up", "ffn1", 0, 7, 0, 2, "dequant"),
        ("ffn1 down a", "down", "ffn1", 0, HK, 0, 2, "dequant"),
        ("ffn1 gate/up b", "gate_up", "ffn1", 1, 7, 7, 2, "dequant"),
        ("ffn1 down b", "down", "ffn1", 1, HK, 7, 2, "dequant"),
    ]
    t0, g0, d0, m0, raw0 = 0, CH, 0, 0, [0, 0]
    phases = []
    for name, kind, layer, part, tiles, first, loads, prep in steps:
        phases.append(Phase(name, kind, layer, part, tiles, first, t0, g0, d0, m0, tuple(raw0), loads, prep))
        for j in range(tiles):
            raw0[(t0 + j) % 2] += 16 * loads
        t0 += tiles
        if kind == "gate_up":
            g0 += CH * tiles
        else:
            d0 += CH * tiles
        if prep == "scale":
            m0 += tiles
    return phases


def adaln_ffn(nc, d, out):
    phases = plan_phases()
    following = dict(zip(phases, phases[1:]))
    named = {ph.name: ph for ph in phases}
    with ExitStack() as ctx:
        at = {}

        def place(name, shape, dt, offset):
            return nc.alloc_sbuf_tensor_at(name, shape, dt, offset=offset)

        def region(name, size):
            at[name] = at["top"]
            at["top"] += size

        def sem(name):
            return ctx.enter_context(nc.semaphore(name))

        KB = 1024
        at["top"] = (nc.sbuf_base + 63) // 64 * 64
        ACT_TILES = 7
        for name, size in (("h", 32 * KB), ("xp", 16 * KB), ("act_hi", ACT_TILES * 4 * KB), ("act_lo", ACT_TILES * 4 * KB),
                           ("w", 24 * KB), ("gated", 4 * KB), ("lora0", 11 * KB + (2 * F0 + H) * CH * 4),
                           ("t", 16 * KB), ("mask", 2 * KB), ("pack", 4 * (F1 + 3 * H)), ("lora_b1", 4 * KB), ("small", 192)):
            region(name, size)

        h_hi = place("h_hi", [P, HK, TOK], F32R, at["h"])
        h_lo = place("h_lo", [P, HK, TOK], F32R, at["h"] + 16 * KB)
        xp = place("xp", [P, HK, TOK], F32, at["xp"])
        act_hi = place("act_hi", [P, ACT_TILES, TOK], F32R, at["act_hi"])
        act_lo = place("act_lo", [P, ACT_TILES, TOK], F32R, at["act_lo"])
        w_hi = place("w_hi", [P, 2, WT], F32R, at["w"])
        w_lo = place("w_lo", [P, 2, WT], F32R, at["w"] + 8 * KB)
        w_raw = place("w_raw", [P, 2, WT], F32, at["w"] + 16 * KB)
        gated = place("gated", [P, CH, CT], F32, at["gated"])
        NKD = (F0 + P - 1) // P
        BW = 2 * F0 + H
        a_dn_hi = place("a_dn_hi", [P, NKD, NB, R], F32R, at["lora0"])
        a_dn_lo = place("a_dn_lo", [P, NKD, NB, R], F32R, at["lora0"] + NKD * NB * R * 4)
        b_split = place("b_split", [P, CH, BW], F32R, at["lora0"] + 11 * KB)
        y_hi = place("y_hi", [P, HK, TOK], F32R, at["lora0"])
        y_lo = place("y_lo", [P, HK, TOK], F32R, at["lora0"] + 16 * KB)
        a1_hi = place("a1_hi", [P, HK, NB, R], F32R, at["lora0"] + 32 * KB)
        a1_lo = place("a1_lo", [P, HK, NB, R], F32R, at["lora0"] + 34 * KB)
        a1_raw = place("a1_raw", [P, NB, HK * R], F32, at["lora0"])
        b1_raw = place("b1_raw", [P, CH, H], F32, at["lora0"] + 2 * KB)
        b1_split = place("b1_split", [P, CH, H], F32R, at["lora_b1"])
        t_hi = place("t_hi", [P, 2, TOK], F32R, at["t"])
        t_lo = place("t_lo", [P, 2, TOK], F32R, at["t"] + 8 * KB)
        s_bc = [place(f"s_bc{i}", [P, WT], F32, at["t"] + 8 * KB * i + 4 * KB) for i in range(2)]
        seg_mask = place("seg_mask", [P, CT], F32, at["mask"])
        pack_long = place("pack_long", [P, F1], F32R, at["pack"])
        pack_short = place("pack_short", [P, 3, H], F32R, at["pack"] + 4 * F1)
        b_raw = [place(f"b_raw{c}", [P, BW], F32, at[("act_hi", "act_lo")[c]]) for c in range(CH)]
        a_dn_raw = place("a_dn_raw", [P, NB, NKD * R], F32, at["act_hi"] + 4 * BW)
        a_gu_raw = place("a_gu_raw", [P, NB, 2 * HK * R], F32, at["act_hi"] + 4 * BW + 4 * NB * NKD * R)
        pack_raw = place("pack_raw", [P, PACK], F32, at["act_lo"] + 4 * BW)
        pack_signed = place("pack_signed", [P, F1], F32, at["act_lo"])
        pack_hi = place("pack_hi", [P, PACK], F32R, at["act_hi"])
        a_gu_hi = place("a_gu_hi", [P, 2 * HK, NB, R], F32R, at["act_hi"] + 24 * KB)
        a_gu_lo = place("a_gu_lo", [P, 2 * HK, NB, R], F32R, at["act_lo"] + 24 * KB)
        small = at["small"]
        ids0 = place("ids0", [1, NB], I32, small)
        ids1 = place("ids1", [1, NB], I32, small + 32)
        bias = place("bias", [P, HK], F32, small + 64)
        row_id = place("row_id", [P, 4], I32, small + 96)
        sel = place("sel", [P, 12], F32, small + 128)
        assert small + 192 <= nc.sbuf_usable_end

        ps_gate = [ctx.enter_context(nc.psum_tensor(f"ps_gate{c}", [P, CT], F32)) for c in range(CH)]
        ps_up = [ctx.enter_context(nc.psum_tensor(f"ps_up{c}", [P, CT], F32)) for c in range(CH)]
        ps_down = [ctx.enter_context(nc.psum_tensor(f"ps_down{c}", [P, CT], F32)) for c in range(CH)]
        ps_m = ctx.enter_context(nc.psum_tensor("ps_m", [P, WT], F32))

        raw_in = [sem(f"raw_in{s}") for s in range(2)]
        x_in = [sem(f"x_in{k}") for k in range(HK)]
        x_again = sem("x_again")
        ids_in = sem("ids_in")
        bias_in = sem("bias_in")
        a_gu_in, a_dn_in, b_in = sem("a_gu_in"), sem("a_dn_in"), sem("b_in")
        a1_in, b1_in = sem("a1_in"), sem("b1_in")
        pack_zero, pack_in = sem("pack_zero"), sem("pack_in")
        mask_step, mask_ready = sem("mask_step"), sem("mask_ready")
        rows_ready = sem("rows_ready")
        sel_step = sem("sel_step")
        x_hi_done, x_ready = sem("x_hi_done"), sem("x_ready")
        a_gu_hi_done, a_gu_ready = sem("a_gu_hi_done"), sem("a_gu_ready")
        a_dn_hi_done, a_dn_ready = sem("a_dn_hi_done"), sem("a_dn_ready")
        b_hi_done, b_ready = sem("b_hi_done"), sem("b_ready")
        a1_hi_done, a1_ready = sem("a1_hi_done"), sem("a1_ready")
        b1_hi_done, b1_ready = sem("b1_hi_done"), sem("b1_ready")
        pack_hi_done, pack_step, pack_ready = sem("pack_hi_done"), sem("pack_step"), sem("pack_ready")
        m_ready = sem("m_ready")
        w_prod = sem("w_prod")
        w_hi_done, w_ready = sem("w_hi_done"), sem("w_ready")
        gate_ready, up_ready = sem("gate_ready"), sem("up_ready")
        silu_done, prod_done = sem("silu_done"), sem("prod_done")
        act_hi_done, act_ready = sem("act_hi_done"), sem("act_ready")
        down_ready = sem("down_ready")
        sum_done = sem("sum_done")
        h_hi_done, h_ready = sem("h_hi_done"), sem("h_ready")
        t_dn_ready, t_masked, t_hi_done, t_lo_done = sem("t_dn_ready"), sem("t_masked"), sem("t_hi_done"), sem("t_lo_done")
        t_rep = [sem(f"t_rep{c}") for c in range(CH)]
        out_done = sem("out_done")

        def chunk(c):
            return slice(c * CT, (c + 1) * CT)

        def ds(start, size):
            return bass.ds(start, size)

        def widths(ph, i, jj):
            if ph.layer == "cond" and ph.part == 1 and isinstance(i, int) and 2 * i + jj == ph.tiles - 1:
                return F0_TAIL
            return P

        def k_rows(ph, k):
            return F0_TAIL if ph.name == "cond down b" and k == k_count(ph) - 1 else P

        def k_count(ph):
            return {"cond": (6, 5)[ph.part], "cond1": HK}.get(ph.layer, ACT_TILES)

        def columns(ph):
            return WT if ph.kind == "gate_up" else k_count(ph) * P

        def slot(ph, jj, i):
            return (ph.t0 + jj) % 2

        def raw_count(ph, i, jj):
            return ph.raw0[slot(ph, jj, i)] + 16 * ph.loads * (i + jj // 2 + 1)

        def tile_steps(eng, ph, step, in_loop=True, peeled=0):
            looped = (ph.tiles - 1) // 2 if ph.kind == "gate_up" and in_loop else peeled
            for j in range(2 * peeled):
                step(j // 2, j % 2, ph, (j + 1) // 2, (j + 1) % 2)
            if looped > peeled:
                with eng.Fori(peeled, looped) as i:
                    for jj in range(2):
                        step(i, jj, ph, i, jj + 1)
            for j in range(2 * looped, ph.tiles):
                if j + 1 < ph.tiles:
                    step(j // 2, j % 2, ph, j // 2, j % 2 + 1)
                else:
                    step(j // 2, j % 2, following.get(ph), 0, 0)

        def w_prod_count(ph, i, jj):
            scaled = sum(p.tiles for p in phases if p.prep == "scale")
            if ph.prep == "scale":
                return ph.m0 + 2 * i + jj + 1
            return scaled + ph.t0 - named["ffn1 gate/up a"].t0 + 2 * i + jj + 1

        def h_seen(ph):
            return {"ffn0 down b": CH * HK, "cond1": 2 * CH * HK}.get(ph.name, 0)

        block = ctx.enter_context(nc.Block())

        @block.sync
        def _(sp):
            def load_tile(ph, i, jj):
                s = slot(ph, jj, i)
                if not (isinstance(i, int) and ph.t0 + 2 * i + jj < 2):
                    sp.wait_ge(w_ready, ph.t0 + 2 * i + jj - 1)
                n = columns(ph)
                if ph.kind == "gate_up":
                    f = ph.first + 2 * i + jj
                    if widths(ph, i, jj) == F0_TAIL:
                        sp.dma_start(w_raw[:, s, :].rearrange("p (g f) -> p g f", f=P)[:, :, 0:F0_TAIL],
                                     d["cond_gu_tail"].rearrange("p (g f) -> p g f", f=F0_TAIL)).then_inc(raw_in[s], 16)
                        return
                    src = {"cond": d["cond_gu"], "ffn0": d["ffn0_gu"], "ffn1": d["ffn1_gu"]}[ph.layer]
                    dst = w_raw[:, s, :]
                    if ph.prep == "dequant":
                        dst = dst.bitcast(I32)
                    sp.dma_start(dst, src[ds(f, 1)].rearrange("a p n -> (a p) n")).then_inc(raw_in[s], 16)
                    if ph.prep == "dequant":
                        sp.dma_start(s_bc[s][:, :], d["ffn1_gu_s"][ds(f, 1), :].partition_broadcast(P)).then_inc(raw_in[s], 16)
                    return
                o = 2 * i + jj
                if ph.layer == "cond":
                    src = d[("cond_dn_a", "cond_dn_b")[ph.part]]
                    main = src.shape[2]
                    sp.dma_start(w_raw[:, s, 0:main], src[o]).then_inc(raw_in[s], 16)
                    if ph.part:
                        sp.dma_start(w_raw[0:F0_TAIL, s, main:n], d["cond_dn_tail"][o]).then_inc(raw_in[s], 16)
                elif ph.layer == "cond1":
                    sp.dma_start(w_raw[:, s, 0:n], d["cond1_w"][o]).then_inc(raw_in[s], 16)
                elif ph.layer == "ffn0":
                    sp.dma_start(w_raw[:, s, 0:n], d["ffn0_dn"][ph.part, o]).then_inc(raw_in[s], 16)
                else:
                    sp.dma_start(w_raw[:, s, 0:n].bitcast(I32), d["ffn1_dn"][ph.part, o]).then_inc(raw_in[s], 16)
                    sp.dma_start(s_bc[s][:, 0:n], d["ffn1_dn_s"][ph.part, o:o + 1, :].partition_broadcast(P)).then_inc(raw_in[s], 16)

            for k in range(HK):
                sp.dma_start(xp[:, k, :], d["x"][k]).then_inc(x_in[k], 16)
            first = phases[0]
            for ph in phases:
                if ph.name == "cond1":
                    sp.dma_start(bias[:, :], d["cond1_b"]).then_inc(bias_in, 16)
                if ph.name == "ffn0 down a":
                    sp.wait_ge(h_ready, CH * HK)
                    sp.dma_start(xp[:, :, :], d["x"].rearrange("k p n -> p k n")).then_inc(x_again, 16)
                start = 0
                if ph is first:
                    load_tile(ph, 0, 0)
                    load_tile(ph, 0, 1)
                    start = 1
                pairs = ph.tiles // 2
                if ph.kind == "gate_up":
                    last_pair = pairs
                    with sp.Fori(start, last_pair) as i:
                        load_tile(ph, i, 0)
                        load_tile(ph, i, 1)
                    if ph.tiles % 2:
                        load_tile(ph, pairs, 0)
                else:
                    for o in range(ph.tiles):
                        load_tile(ph, o // 2, o % 2)
            last = phases[-1]
            for o in range(HK):
                for c in range(CH):
                    sp.wait_ge(sum_done, last.d0 + CH * o + c + 1)
                    sp.dma_start(out[o][:, chunk(c)], xp[:, o, chunk(c)]).then_inc(out_done, 16)
            sp.wait_ge(out_done, 16 * CH * HK)

        @block.gpsimd
        def _(pool):
            pool.dma_start(ids0[:, :], d["ids0"]).then_inc(ids_in, 16)
            pool.dma_start(ids1[:, :], d["ids1"]).then_inc(ids_in, 16)
            nc.gpsimd.iota(row_id[:, 0:1], [[0, 1]], base=0, channel_multiplier=1).then_inc(rows_ready, 1)
            nc.gpsimd.memset(pack_raw[:, :], 0.0).then_inc(pack_zero, 1)
            pool.wait_ge(ids_in, 32)
            for b in range(NB):
                e = pool.value_load(ids0[0:1, b:b + 1], min_val=0, max_val=d["a_gu"].shape[0] - 1)
                pool.dma_start(a_gu_raw[:, b, :], d["a_gu"][ds(e, 1)].rearrange("a p n -> (a p) n")).then_inc(a_gu_in, 16)
            segs = seg_mask[0:RB, :].rearrange("p (s n) -> p s n", s=BC)
            nc.gpsimd.memset(seg_mask[0:RB, :], 1.0).then_inc(mask_step, 1)
            pool.wait_ge(mask_step, 1)
            nc.gpsimd.affine_select(out=segs, in_=segs, compare_op=ALU.is_ge, fill=0.0, base=0,
                                    pattern=[[-R, BC], [0, P]], channel_multiplier=1).then_inc(mask_step, 1)
            pool.wait_ge(mask_step, 2)
            nc.gpsimd.affine_select(out=segs, in_=segs, compare_op=ALU.is_ge, fill=0.0, base=R - 1,
                                    pattern=[[R, BC], [0, P]], channel_multiplier=-1).then_inc(mask_ready, 1)
            for b in range(NB):
                e = pool.value_load(ids0[0:1, b:b + 1], min_val=0, max_val=d["a_gu"].shape[0] - 1)
                for rep in range(2):
                    row = rep * RB + b % BC * R
                    pool.dma_start(b_raw[b // BC][row:row + R, :], d["b0"][ds(e, 1)].rearrange("a r n -> (a r) n")).then_inc(b_in, 16)
            pool.wait_ge(pack_zero, 1)
            for q in range(3):
                for v in range(4):
                    row = 32 * q + SR * v
                    pool.dma_start(pack_raw[row:row + SR, :], d["factors"][q]).then_inc(pack_in, 16)
            for b in range(NB):
                e = pool.value_load(ids0[0:1, b:b + 1], min_val=0, max_val=d["a_gu"].shape[0] - 1)
                full = (NKD - 1) * R
                pool.dma_start(a_dn_raw[:, b, 0:full], d["a_dn"][ds(e, 1)].rearrange("a p n -> (a p) n")).then_inc(a_dn_in, 16)
                pool.dma_start(a_dn_raw[0:F0_TAIL, b, full:full + R],
                               d["a_dn_tail"][ds(e, 1)].rearrange("a p n -> (a p) n")).then_inc(a_dn_in, 16)
            pool.wait_ge(down_ready, 2 * CH * HK)
            for b in range(NB):
                e = pool.value_load(ids1[0:1, b:b + 1], min_val=0, max_val=d["a1"].shape[0] - 1)
                pool.dma_start(a1_raw[:, b, :], d["a1"][ds(e, 1)].rearrange("a p n -> (a p) n")).then_inc(a1_in, 16)
                for rep in range(2):
                    row = rep * RB + b % BC * R
                    pool.dma_start(b1_raw[row:row + R, b // BC, :], d["b1"][ds(e, 1)].rearrange("a r n -> (a r) n")).then_inc(b1_in, 16)

        @block.scalar
        def _(act):
            def tile_hi(ph, i, jj):
                s, n = slot(ph, jj, i), columns(ph)
                if ph.prep == "split":
                    act.wait_ge(raw_in[s], raw_count(ph, i, jj))
                else:
                    act.wait_ge(w_prod, w_prod_count(ph, i, jj))
                nc.scalar.activation(w_hi[:, s, 0:n], w_raw[:, s, 0:n], ACT.Copy).then_inc(w_hi_done, 1)

            def copy_t(c, parts):
                for t in (t_hi, t_lo):
                    act.dma_start(t[RB:2 * RB, 0:parts, chunk(c)].bitcast(F32), t[0:RB, 0:parts, chunk(c)].bitcast(F32)).then_inc(t_rep[c], 16)

            def gate_up_tile(ph, i, jj):
                m = widths(ph, i, jj)
                for c in range(CH):
                    n = ph.g0 + CH * (2 * i + jj) + c
                    act.wait_ge(gate_ready, n + 1)
                    act.wait_ge(act_ready, n - 1)
                    nc.scalar.activation(gated[0:m, c, :], ps_gate[c][0:m, :], ACT.Silu).then_inc(silu_done, 1)
                    act.wait_ge(prod_done, n + 1)
                    nc.scalar.activation(act_hi[0:m, ds(2 * i + jj, 1), chunk(c)].rearrange("p a n -> p (a n)"),
                                         gated[0:m, c, :], ACT.Copy).then_inc(act_hi_done, 1)

            def down_tile(ph, o):
                for c in range(CH):
                    if ph.name in ("cond down b", "ffn0 down b"):
                        act.wait_ge(sum_done, ph.d0 + CH * o + c + 1)
                        nc.scalar.activation(h_hi[:, o, chunk(c)], xp[:, o, chunk(c)], ACT.Copy).then_inc(h_hi_done, 1)
                    elif ph.name == "cond1":
                        act.wait_ge(sum_done, ph.d0 + CH * o + c + 1)
                        nc.scalar.activation(y_hi[:, o, chunk(c)], gated[:, c, :], ACT.Copy).then_inc(h_hi_done, 1)

            def t_from_gated(base):
                for c in range(CH):
                    act.wait_ge(t_masked, base + c + 1)
                    nc.scalar.activation(t_hi[0:RB, 0, chunk(c)], gated[0:RB, c, :], ACT.Copy).then_inc(t_hi_done, 1)
                for c in range(CH):
                    act.wait_ge(t_lo_done, base + c + 1)
                    copy_t(c, 1)

            for k in range(HK):
                act.wait_ge(x_in[k], 16)
                nc.scalar.activation(h_hi[:, k, :], xp[:, k, :], ACT.Copy).then_inc(x_hi_done, 1)
            act.wait_ge(a_gu_in, 16 * NB)
            nc.scalar.activation(a_gu_hi[:, :, :, :], a_gu_raw[:, :, :].rearrange("p b (k r) -> p k b r", r=R),
                                 ACT.Copy).then_inc(a_gu_hi_done, 1)
            tile_hi(phases[0], 0, 0)
            for c in range(CH):
                act.wait_ge(prod_done, c + 1)
                nc.scalar.activation(t_hi[0:RB, :, chunk(c)], xp[0:RB, 2 * c:2 * c + 2, 0:CT], ACT.Copy).then_inc(act_hi_done, 1)
                if c == 0:
                    act.wait_ge(b_in, 16 * 2 * NB)
                    for cc in range(CH):
                        nc.scalar.activation(b_split[0:RB, cc, :], b_raw[cc][0:RB, :], ACT.Copy).then_inc(b_hi_done, 1)
                    for cc in range(CH):
                        nc.scalar.activation(b_split[RB:2 * RB, cc, :], b_raw[cc][RB:2 * RB, :], ACT.Copy).then_inc(b_hi_done, 1)
                act.wait_ge(act_ready, c + 1)
                copy_t(c, 2)
            act.wait_ge(pack_in, 16 * 12)
            act.wait_ge(b_ready, CH)
            nc.scalar.activation(pack_hi[:, :], pack_raw[:, :], ACT.Copy).then_inc(pack_hi_done, 1)
            act.wait_ge(a_dn_in, 16 * 2 * NB)
            k_full = NKD - 1
            nc.scalar.activation(a_dn_hi[:, 0:k_full, :, :], a_dn_raw[:, :, 0:k_full * R].rearrange("p b (k r) -> p k b r", r=R),
                                 ACT.Copy).then_inc(a_dn_hi_done, 1)
            nc.scalar.activation(a_dn_hi[0:F0_TAIL, k_full, :, :], a_dn_raw[0:F0_TAIL, :, k_full * R:NKD * R],
                                 ACT.Copy).then_inc(a_dn_hi_done, 1)

            for ph in phases:
                if ph.name == "ffn0 down b":
                    act.wait_ge(a1_in, 16 * NB)
                    nc.scalar.activation(a1_hi[:, :, :, :], a1_raw[:, :, :].rearrange("p b (k r) -> p k b r", r=R),
                                         ACT.Copy).then_inc(a1_hi_done, 1)
                    act.wait_ge(b1_in, 16 * 2 * NB)
                    nc.scalar.activation(b1_split[:, :, :], b1_raw[:, :, :], ACT.Copy).then_inc(b1_hi_done, 1)

                def step(i, jj, nxt, ni, njj, ph=ph):
                    if nxt is not None:
                        if ph.kind == "gate_up":
                            act.wait_ge(up_ready, ph.g0 + CH * (2 * i + jj))
                        tile_hi(nxt, ni, njj)
                    if ph.kind == "gate_up":
                        gate_up_tile(ph, i, jj)
                    else:
                        if ph.name == "cond down b" and 2 * i + jj == 0:
                            t_from_gated(0)
                        if ph.name == "cond1" and 2 * i + jj == 0:
                            t_from_gated(CH)
                        down_tile(ph, 2 * i + jj)

                if ph.kind == "gate_up" and ph.d0 > 0:
                    act.wait_ge(down_ready, ph.d0)
                if ph.kind == "down":
                    def step_down(i, jj, nxt, ni, njj, ph=ph, step=step):
                        o = 2 * i + jj
                        if o == 0:
                            if ph.g0 > CH and ph.name != "cond1":
                                act.wait_ge(up_ready, ph.g0)
                            else:
                                act.wait_ge(down_ready, ph.d0)
                        else:
                            act.wait_ge(down_ready, ph.d0 + CH * o)
                        step(i, jj, nxt, ni, njj)
                    tile_steps(act, ph, step_down)
                else:
                    tile_steps(act, ph, step)

        @block.vector
        def _(dve):
            chain = [0]

            def link(ins):
                chain[0] += 1
                ins.then_inc(sel_step, 1)
                dve.wait_ge(sel_step, chain[0])

            def lo(out_, value, hi):
                return nc.vector.tensor_tensor(out_, value, hi.bitcast(F32), ALU.subtract)

            def tile_lo(ph, i, jj):
                s, n = slot(ph, jj, i), columns(ph)
                if ph.prep == "scale":
                    dve.wait_ge(raw_in[s], raw_count(ph, i, jj))
                    dve.wait_ge(m_ready, ph.m0 + 2 * i + jj + 1)
                    nc.vector.tensor_tensor(w_raw[:, s, 0:n], w_raw[:, s, 0:n], ps_m[:, 0:n], ALU.mult).then_inc(w_prod, 1)
                elif ph.prep == "dequant":
                    dve.wait_ge(raw_in[s], raw_count(ph, i, jj))
                    nc.vector.tensor_tensor(w_raw[:, s, 0:n], w_raw[:, s, 0:n].bitcast(I32), s_bc[s][:, 0:n],
                                            ALU.mult).then_inc(w_prod, 1)
                dve.wait_ge(w_hi_done, ph.t0 + 2 * i + jj + 1)
                lo(w_lo[:, s, 0:n], w_raw[:, s, 0:n], w_hi[:, s, 0:n]).then_inc(w_ready, 1)

            def gate_up_tile(ph, i, jj):
                m = widths(ph, i, jj)
                for c in range(CH):
                    n = ph.g0 + CH * (2 * i + jj) + c
                    dve.wait_ge(silu_done, n + 1)
                    dve.wait_ge(up_ready, n + 1)
                    nc.vector.tensor_tensor(gated[0:m, c, :], gated[0:m, c, :], ps_up[c][0:m, :], ALU.mult).then_inc(prod_done, 1)
                    dve.wait_ge(act_hi_done, n + 1)
                    j = ds(2 * i + jj, 1)
                    lo(act_lo[0:m, j, chunk(c)].rearrange("p a n -> p (a n)"), gated[0:m, c, :],
                       act_hi[0:m, j, chunk(c)].rearrange("p a n -> p (a n)")).then_inc(act_ready, 1)

            def down_tile(ph, o):
                for c in range(CH):
                    n = ph.d0 + CH * o + c
                    here = xp[:, o, chunk(c)]
                    dve.wait_ge(down_ready, n + 1)
                    if ph.name == "cond down a":
                        nc.vector.tensor_copy(here, ps_down[c][:, :]).then_inc(sum_done, 1)
                    elif ph.name == "cond1":
                        nc.vector.tensor_scalar(gated[:, c, :], ps_down[c][:, :], bias[:, o:o + 1], None, ALU.add).then_inc(sum_done, 1)
                    else:
                        nc.vector.tensor_tensor(here, here, ps_down[c][:, :], ALU.add).then_inc(sum_done, 1)
                    hs = h_seen(ph) + CH * o + c + 1
                    if ph.name in ("cond down b", "ffn0 down b"):
                        dve.wait_ge(h_hi_done, hs)
                        lo(h_lo[:, o, chunk(c)], here, h_hi[:, o, chunk(c)]).then_inc(h_ready, 1)
                    elif ph.name == "cond1":
                        dve.wait_ge(h_hi_done, hs)
                        lo(y_lo[:, o, chunk(c)], gated[:, c, :], y_hi[:, o, chunk(c)]).then_inc(h_ready, 1)

            def t_from_psum(base, scale):
                for c in range(CH):
                    dve.wait_ge(t_dn_ready, base + c + 1)
                    nc.vector.scalar_tensor_tensor(out=gated[0:RB, c, :], in0=ps_m[0:RB, chunk(c)], scalar=scale,
                                                   in1=seg_mask[0:RB, :], op0=ALU.mult, op1=ALU.mult).then_inc(t_masked, 1)
                for c in range(CH):
                    dve.wait_ge(t_hi_done, base + c + 1)
                    lo(t_lo[0:RB, 0, chunk(c)], gated[0:RB, c, :], t_hi[0:RB, 0, chunk(c)]).then_inc(t_lo_done, 1)

            dve.wait_ge(rows_ready, 1)
            link(nc.vector.tensor_scalar(row_id[:, 1:2], row_id[:, 0:1], 2, 1, ALU.logical_shift_right, ALU.bitwise_and))
            link(nc.vector.tensor_scalar(row_id[:, 2:3], row_id[:, 0:1], 3, 1, ALU.logical_shift_right, ALU.bitwise_and))
            link(nc.vector.tensor_scalar(row_id[:, 3:4], row_id[:, 0:1], 5, None, ALU.logical_shift_right))
            link(nc.vector.tensor_copy(sel[:, 0:1], row_id[:, 1:2]))
            link(nc.vector.tensor_copy(sel[:, 2:3], row_id[:, 2:3]))
            link(nc.vector.tensor_copy(sel[:, 10:11], row_id[:, 3:4]))
            for a in (0, 2):
                link(nc.vector.tensor_scalar(sel[:, a + 1:a + 2], sel[:, a:a + 1], -2.0, 1.0, ALU.mult, ALU.add))
            for q in range(3):
                link(nc.vector.tensor_scalar(sel[:, 11:12], sel[:, 10:11], float(q), None, ALU.is_equal))
                for a in range(2):
                    link(nc.vector.tensor_tensor(sel[:, 4 + 2 * q + a:5 + 2 * q + a], sel[:, 2 + a:3 + a], sel[:, 11:12], ALU.mult))

            for k in range(HK):
                dve.wait_ge(x_hi_done, k + 1)
                lo(h_lo[:, k, :], xp[:, k, :], h_hi[:, k, :]).then_inc(x_ready, 1)
            dve.wait_ge(a_gu_hi_done, 1)
            lo(a_gu_lo[:, :, :, :], a_gu_raw[:, :, :].rearrange("p b (k r) -> p k b r", r=R), a_gu_hi[:, :, :, :]).then_inc(a_gu_ready, 1)
            tile_lo(phases[0], 0, 0)
            dve.wait_ge(mask_ready, 1)
            for c in range(CH):
                for g, (ready, ps, done) in enumerate(((gate_ready, ps_gate, silu_done), (up_ready, ps_up, prod_done))):
                    dve.wait_ge(ready, c + 1)
                    nc.vector.scalar_tensor_tensor(out=xp[0:RB, 2 * c + g, 0:CT], in0=ps[c][0:RB, :], scalar=0.5,
                                                   in1=seg_mask[0:RB, :], op0=ALU.mult, op1=ALU.mult).then_inc(done, 1)
                dve.wait_ge(act_hi_done, c + 1)
                lo(t_lo[0:RB, :, chunk(c)], xp[0:RB, 2 * c:2 * c + 2, 0:CT], t_hi[0:RB, :, chunk(c)]).then_inc(act_ready, 1)
                if c == 0:
                    for cc in range(CH):
                        dve.wait_ge(b_hi_done, CH + cc + 1)
                        lo(b_split[RB:2 * RB, cc, :], b_raw[cc][RB:2 * RB, :], b_split[RB:2 * RB, cc, :]).then_inc(b_ready, 1)
            dve.wait_ge(pack_hi_done, 1)
            step_n = 0
            for k_, (col, n, dst, a) in enumerate([(0, F1, pack_long[:, :], 0)] + [(F1, H, pack_short[:, q, :], 4 + 2 * q) for q in range(3)]):
                if step_n:
                    dve.wait_ge(pack_ready, step_n)
                signed = pack_signed[:, 0:n]
                nc.vector.tensor_scalar(signed, pack_hi[:, col:col + n].bitcast(F32), sel[:, a + 1:a + 2], None, ALU.mult).then_inc(pack_step, 1)
                step_n += 1
                dve.wait_ge(pack_step, step_n)
                nc.vector.scalar_tensor_tensor(out=dst, in0=pack_raw[:, col:col + n], scalar=sel[:, a:a + 1], in1=signed,
                                               op0=ALU.mult, op1=ALU.add).then_inc(pack_ready, 1)
            k_full = NKD - 1
            dve.wait_ge(a_dn_hi_done, 2)
            lo(a_dn_lo[:, 0:k_full, :, :], a_dn_raw[:, :, 0:k_full * R].rearrange("p b (k r) -> p k b r", r=R),
               a_dn_hi[:, 0:k_full, :, :]).then_inc(a_dn_ready, 1)
            lo(a_dn_lo[0:F0_TAIL, k_full, :, :], a_dn_raw[0:F0_TAIL, :, k_full * R:NKD * R],
               a_dn_hi[0:F0_TAIL, k_full, :, :]).then_inc(a_dn_ready, 1)

            for ph in phases:
                if ph.name == "ffn0 down b":
                    dve.wait_ge(a1_hi_done, 1)
                    lo(a1_lo[:, :, :, :], a1_raw[:, :, :].rearrange("p b (k r) -> p k b r", r=R), a1_hi[:, :, :, :]).then_inc(a1_ready, 1)
                    dve.wait_ge(b1_hi_done, 1)
                    lo(b1_split[RB:2 * RB, :, :], b1_raw[RB:2 * RB, :, :], b1_split[RB:2 * RB, :, :]).then_inc(b1_ready, 1)
                if ph.name == "ffn0 down a":
                    dve.wait_ge(x_again, 16)
                if ph.name == "cond1":
                    dve.wait_ge(bias_in, 16)

                def step(i, jj, nxt, ni, njj, ph=ph):
                    if nxt is not None:
                        tile_lo(nxt, ni, njj)
                    if ph.kind == "gate_up":
                        gate_up_tile(ph, i, jj)
                    else:
                        if ph.name == "cond down b" and 2 * i + jj == 0:
                            t_from_psum(0, 0.5)
                        if ph.name == "cond1" and 2 * i + jj == 0:
                            t_from_psum(CH, 2.0)
                        down_tile(ph, 2 * i + jj)

                tile_steps(dve, ph, step)

        @block.tensor
        def _(pe):
            def sums(ps, m, s, col, ks, rhs_hi, rhs_lo, rows=lambda k: P, before=lambda k: None, start=True, stop=False):
                last = None
                for n, k in enumerate(ks):
                    before(k)
                    r = rows(k)
                    cols = slice(col + k * P, col + k * P + m)
                    nc.tensor.matmul(ps[0:m, :], w_hi[0:r, s, cols], rhs_hi(k, r), start=start and n == 0, stop=False)
                    nc.tensor.matmul(ps[0:m, :], w_hi[0:r, s, cols], rhs_lo(k, r), start=False, stop=False)
                    last = nc.tensor.matmul(ps[0:m, :], w_lo[0:r, s, cols], rhs_hi(k, r), start=False,
                                            stop=stop and n == len(ks) - 1)
                return last

            def adapters(ps, m, b, g, c):
                nc.tensor.matmul(ps[0:m, :], b, t_hi[:, g, chunk(c)], start=False, stop=False)
                return nc.tensor.matmul(ps[0:m, :], b, t_lo[:, g, chunk(c)], start=False, stop=True)

            def adapter_t(ps, a_hi_, a_lo_, ks, c, rhs_hi, rhs_lo, rows=lambda k: P, start=True, stop=True):
                last = None
                for n, k in enumerate(ks):
                    r = rows(k)
                    a_h = a_hi_(k)[0:r, c * BC:(c + 1) * BC, :].rearrange("p b r -> p (b r)")
                    a_l = a_lo_(k)[0:r, c * BC:(c + 1) * BC, :].rearrange("p b r -> p (b r)")
                    nc.tensor.matmul(ps, a_h, rhs_hi(k, r), start=start and n == 0, stop=False)
                    nc.tensor.matmul(ps, a_h, rhs_lo(k, r), start=False, stop=False)
                    last = nc.tensor.matmul(ps, a_l, rhs_hi(k, r), start=False, stop=stop and n == len(ks) - 1)
                return last

            def scales(ph, i, jj):
                n = ph.m0 + 2 * i + jj
                if not (isinstance(i, int) and n == 0):
                    pe.wait_ge(w_prod, n)
                else:
                    pe.wait_ge(pack_ready, 4)
                last = None
                if ph.kind == "gate_up":
                    for g in range(2):
                        for k in range(HK):
                            q = g * HK + k
                            last = nc.tensor.matmul(ps_m[:, q * P:(q + 1) * P], pack_short[:, g, k * P:(k + 1) * P],
                                                    pack_long[:, ds((ph.first + 2 * i + jj) * P, P)], start=True, stop=True)
                else:
                    o = 2 * i + jj
                    for k in range(k_count(ph)):
                        last = nc.tensor.matmul(ps_m[:, k * P:(k + 1) * P], pack_long[:, (ph.first + k) * P:(ph.first + k + 1) * P],
                                                pack_short[:, 2, o * P:(o + 1) * P], start=True, stop=True)
                last.then_inc(m_ready, 1)

            def net_input(ph):
                return (y_hi, y_lo) if ph.layer == "ffn1" else (h_hi, h_lo)

            def gate_up_tile(ph, i, jj):
                s, m = slot(ph, jj, i), widths(ph, i, jj)
                hi, lo = net_input(ph)
                pe.wait_ge(w_ready, ph.t0 + 2 * i + jj + 1)
                for c in range(CH):
                    n = ph.g0 + CH * (2 * i + jj) + c
                    for g, (ps, read, ready) in enumerate(((ps_gate, silu_done, gate_ready), (ps_up, prod_done, up_ready))):
                        pe.wait_ge(read, n - 1)

                        def input_ready(k, c=c, g=g):
                            if g == 0 and ph.layer != "cond" and ph.part == 0 and jj == 0 and isinstance(i, int) and i == 0:
                                pe.wait_ge(h_ready, {"ffn0": 0, "ffn1": 2 * CH * HK}[ph.layer] + CH * k + c + 1)

                        last = sums(ps[c], m, s, g * HK * P, range(HK), lambda k, r, c=c: hi[0:r, k, chunk(c)],
                                    lambda k, r, c=c: lo[0:r, k, chunk(c)], before=input_ready, stop=ph.layer != "cond")
                        if ph.layer == "cond":
                            pe.wait_ge(t_rep[c], 32)
                            pe.wait_ge(b_ready, CH)
                            b0 = g * F0 + (ph.first + 2 * i + jj) * P
                            last = adapters(ps[c], m, b_split[:, c, b0:b0 + m], g, c)
                        last.then_inc(ready, 1)

            def down_base(ph, o, c):
                n, s = ph.d0 + CH * o + c, slot(ph, o, 0)
                if c == 0:
                    pe.wait_ge(w_ready, ph.t0 + o + 1)
                if n >= 2:
                    pe.wait_ge(sum_done, n - 1)
                g0 = ph.g0 - CH * k_count(ph)

                def input_ready(k):
                    if o > 0:
                        return
                    if ph.layer == "cond1":
                        pe.wait_ge(h_ready, CH * HK + CH * k + c + 1)
                    else:
                        pe.wait_ge(act_ready, g0 + CH * k + c + 1)

                hi, lo = (h_hi, h_lo) if ph.layer == "cond1" else (act_hi, act_lo)
                return sums(ps_down[c], P, s, 0, range(k_count(ph)), lambda k, r: hi[0:r, k, chunk(c)],
                            lambda k, r: lo[0:r, k, chunk(c)], rows=lambda k: k_rows(ph, k), before=input_ready,
                            stop=not has_adapters(ph))

            def has_adapters(ph):
                return ph.name in ("cond down b", "cond1")

            def down_adapters(ph, o, c):
                if ph.name == "cond1":
                    pe.wait_ge(b1_ready, 1)
                    pe.wait_ge(t_rep[c], 3 * 32)
                    return adapters(ps_down[c], P, b1_split[:, c, o * P:(o + 1) * P], 0, c)
                pe.wait_ge(t_rep[c], 2 * 32)
                return adapters(ps_down[c], P, b_split[:, c, 2 * F0 + o * P:2 * F0 + (o + 1) * P], 0, c)

            def t_down(ph, c):
                ks = range(k_count(ph))
                pe.wait_ge(a_dn_ready, 2)
                pe.wait_ge(act_ready, ph.g0 - CH + c + 1)
                last = adapter_t(ps_m[0:RB, chunk(c)], lambda k: a_dn_hi[:, ph.first + k], lambda k: a_dn_lo[:, ph.first + k], ks, c,
                                 lambda k, r: act_hi[0:r, k, chunk(c)], lambda k, r: act_lo[0:r, k, chunk(c)],
                                 rows=lambda k: k_rows(ph, k), start=ph.part == 0, stop=ph.part == 1)
                if ph.part == 1:
                    last.then_inc(t_dn_ready, 1)

            pe.wait_ge(a_gu_ready, 1)
            for c in range(CH):
                for g, (ps, ready) in enumerate(((ps_gate, gate_ready), (ps_up, up_ready))):
                    pe.wait_ge(x_ready, HK)
                    adapter_t(ps[c][0:RB, :], lambda k, g=g: a_gu_hi[:, g * HK + k], lambda k, g=g: a_gu_lo[:, g * HK + k],
                              range(HK), c, lambda k, r, c=c: h_hi[:, k, chunk(c)],
                              lambda k, r, c=c: h_lo[:, k, chunk(c)]).then_inc(ready, 1)

            for ph in phases:
                if ph.name == "cond1":
                    pe.wait_ge(a1_ready, 1)
                    for c in range(CH):
                        pe.wait_ge(h_ready, 2 * CH * HK - CH + c + 1)
                        adapter_t(ps_m[0:RB, chunk(c)], lambda k: a1_hi[:, k], lambda k: a1_lo[:, k], range(HK), c,
                                  lambda k, r, c=c: h_hi[:, k, chunk(c)],
                                  lambda k, r, c=c: h_lo[:, k, chunk(c)]).then_inc(t_dn_ready, 1)

                def step(i, jj, nxt, ni, njj, ph=ph):
                    if nxt is not None and nxt.prep == "scale":
                        scales(nxt, ni, njj)
                    if ph.kind == "gate_up":
                        gate_up_tile(ph, i, jj)
                        return
                    o = 2 * i + jj
                    if not has_adapters(ph):
                        for c in range(CH):
                            down_base(ph, o, c).then_inc(down_ready, 1)
                    elif o == 0:
                        down_base(ph, o, 0)
                        if ph.name == "cond down b":
                            for c in range(CH):
                                t_down(ph, c)
                        down_base(ph, o, 1)
                        for c in range(CH):
                            down_adapters(ph, o, c).then_inc(down_ready, 1)
                    else:
                        for c in range(CH):
                            down_base(ph, o, c)
                            down_adapters(ph, o, c).then_inc(down_ready, 1)

                first_read = ph.kind == "gate_up" and ph.layer != "cond" and ph.part == 0
                tile_steps(pe, ph, step, in_loop=ph.layer != "cond", peeled=1 if first_read else 0)
                if ph.name == "cond down a":
                    for c in range(CH):
                        t_down(ph, c)


def _lay_out(i):
    import numpy as np

    def tiles(w, k, f):
        o, n = w.shape
        return w.T.reshape(n // P, P, o // f, f).transpose(2, 1, 0, 3)

    def gate_up(g, u, f=P):
        return np.concatenate([tiles(g, HK, f), tiles(u, HK, f)], axis=2).reshape(-1, P, 2 * HK * f)

    def down(w, parts):
        return np.stack([tiles(w[:, a:b], 0, P).reshape(HK, P, -1) for a, b in parts])

    full = F0 // P * P
    cut = 6 * P
    half = F1 // 2
    cg, cu, cd = i["L0_cond_W_gate"], i["L0_cond_W_up"], i["L0_cond_W_down"]
    a = np.stack([i["L0_cond_A_gate"][0], i["L0_cond_A_up"][0]], axis=1)
    n_id = a.shape[0]
    a_dn = i["L0_cond_A_down"][0].transpose(0, 2, 1)
    b0 = np.concatenate([i["L0_cond_B_gate"][0], i["L0_cond_B_up"][0], i["L0_cond_B_down"][0]], axis=1)
    factors = np.stack([
        np.concatenate([i["L0_ffn_gate_su"].T, i["L0_ffn_gate_sv"]], axis=1),
        np.concatenate([i["L0_ffn_up_su"].T, i["L0_ffn_up_sv"]], axis=1),
        np.concatenate([i["L0_ffn_down_sv"], i["L0_ffn_down_su"].T], axis=1)])
    s_gu = np.concatenate([i[f"L1_ffn_{n}_s"].reshape(F1 // P, P, HK).transpose(0, 2, 1) for n in ("gate", "up")], axis=1)
    s_dn = i["L1_ffn_down_s"].reshape(HK, P, 2, half // P).transpose(2, 0, 3, 1)
    a1 = i["L1_cond_lora_As"]
    arrays = {
        "x": i["x"].reshape(TOK, H).T.reshape(HK, P, TOK),
        "ids0": i["itok_B_2_6"].reshape(1, NB),
        "ids1": i["itok_B_0_23"].reshape(1, NB),
        "cond_gu": gate_up(cg[:full], cu[:full]),
        "cond_gu_tail": gate_up(cg[full:], cu[full:], F0_TAIL)[0],
        "cond_dn_a": down(cd, [(0, cut)])[0],
        "cond_dn_b": down(cd, [(cut, full)])[0],
        "cond_dn_tail": cd[:, full:].T.reshape(F0_TAIL, HK, P).transpose(1, 0, 2),
        "a_gu": a.reshape(n_id, 2, R, HK, P).transpose(0, 4, 1, 3, 2).reshape(n_id, P, 2 * HK * R),
        "a_dn": a_dn[:, :full].reshape(n_id, full // P, P, R).transpose(0, 2, 1, 3).reshape(n_id, P, -1),
        "a_dn_tail": a_dn[:, full:],
        "b0": b0.transpose(0, 2, 1),
        "factors": factors,
        "ffn0_gu": gate_up(i["L0_ffn_gate_w"], i["L0_ffn_up_w"]),
        "ffn0_dn": down(i["L0_ffn_down_w"], [(0, half), (half, F1)]),
        "cond1_w": tiles(i["L1_cond_W"], HK, P).reshape(HK, P, H),
        "cond1_b": i["L1_cond_b"].reshape(HK, P).T,
        "a1": a1.reshape(-1, HK, P, R).transpose(0, 2, 1, 3).reshape(-1, P, HK * R),
        "b1": i["L1_cond_lora_Bs"],
        "ffn1_gu": gate_up(i["L1_ffn_gate_q"], i["L1_ffn_up_q"]),
        "ffn1_dn": down(i["L1_ffn_down_q"], [(0, half), (half, F1)]),
        "ffn1_gu_s": s_gu.reshape(F1 // P, WT),
        "ffn1_dn_s": s_dn.reshape(2, HK, half),
    }
    return {k: np.ascontiguousarray(v) for k, v in arrays.items()}


def kernel(**inputs):
    import numpy as np
    import concourse.bacc as bacc
    from concourse.bass_utils import run_bass_kernel_spmd

    arrays = _lay_out({k: np.asarray(v) for k, v in inputs.items()})
    nc = bacc.Bacc("TRN2", target_bir_lowering=False, num_devices=1)
    d = {k: nc.dram_tensor(f"in_{k}", v.shape, mybir.dt.from_np(v.dtype), kind="ExternalInput").ap() for k, v in arrays.items()}
    out = nc.dram_tensor("out_t", (HK, P, TOK), F32, kind="ExternalOutput").ap()
    adaln_ffn(nc, d, out)
    r = run_bass_kernel_spmd(nc, [{f"in_{k}": v for k, v in arrays.items()}], core_ids=[0])
    got = r.results[0]["out_t"]
    return np.ascontiguousarray(got.reshape(H, TOK).T.reshape(NB, TOK // NB, H))
```

```python
from collections import namedtuple
from contextlib import ExitStack

import concourse.bass as bass
from concourse import mybir

F32 = mybir.dt.float32
F32R = mybir.dt.float32r
I32 = mybir.dt.int32
ALU = mybir.AluOpType
ACT = mybir.ActivationFunctionType

P = 128
H = 512
HK = H // P
TOK = 1024
CT = 512
CH = TOK // CT
NB = 8
BC = NB // CH
R = 16
RB = BC * R
F0 = 1376
F1 = 1792
F0_TAIL = F0 - F0 // P * P
NKD = (F0 + P - 1) // P
SR = 4
WT = 1024
DQ = 384
ACT_TILES = 7
KQ = ACT_TILES - DQ // P
UQ = HK - DQ // P
GQ = HK + UQ
assert UQ == 1
PACK = F1 + H
BW = 2 * F0 + H
BP = 512
NBP = (BW + BP - 1) // BP

Phase = namedtuple("Phase", "name kind layer part tiles first t0 g0 d0 m0 q0 a0 f0 raw0 loads prep")


def plan_phases():
    steps = [
        ("cond gate/up a", "gate_up", "cond", 0, 6, 0, 1, "split"),
        ("cond down a", "down", "cond", 0, HK, 0, 1, "split"),
        ("cond gate/up b", "gate_up", "cond", 1, 5, 6, 1, "split"),
        ("cond down b", "down", "cond", 1, HK, 6, 2, "split"),
        ("ffn0 gate/up a", "gate_up", "ffn0", 0, 7, 0, 1, "scale"),
        ("ffn0 down a", "down", "ffn0", 0, HK, 0, 1, "scale"),
        ("ffn0 gate/up b", "gate_up", "ffn0", 1, 7, 7, 1, "scale"),
        ("ffn0 down b", "down", "ffn0", 1, HK, 7, 1, "scale"),
        ("cond1", "down", "cond1", 0, HK, 0, 1, "split"),
        ("ffn1 gate/up a", "gate_up", "ffn1", 0, 7, 0, 3, "dequant"),
        ("ffn1 down a", "down", "ffn1", 0, HK, 0, 2, "dequant"),
        ("ffn1 gate/up b", "gate_up", "ffn1", 1, 7, 7, 3, "dequant"),
        ("ffn1 down b", "down", "ffn1", 1, HK, 7, 2, "dequant"),
    ]
    t0, g0, d0, m0, q0, a0, f0, raw0 = 0, 0, 0, 0, 0, 0, 0, [-16, 0]
    phases = []
    for name, kind, layer, part, tiles, first, loads, prep in steps:
        phases.append(Phase(name, kind, layer, part, tiles, first, t0, g0, d0, m0, q0, a0, f0, tuple(raw0), loads, prep))
        for j in range(tiles):
            raw0[(t0 + j) % 2] += 16 * loads
        t0 += tiles
        if kind == "gate_up":
            g0 += CH * tiles
        else:
            d0 += CH * tiles
        if prep == "scale":
            m0 += tiles
        if prep == "dequant" and kind == "gate_up":
            q0 += CH * tiles * GQ
            a0 += CH * tiles * (HK - 1)
            f0 += CH * tiles
        if prep == "dequant" and kind == "down":
            q0 += CH * tiles * KQ
            a0 += CH * tiles * KQ
    return phases


def adaln_ffn(nc, d, out):
    phases = plan_phases()
    following = dict(zip(phases, phases[1:]))
    named = {ph.name: ph for ph in phases}
    with ExitStack() as ctx:
        at = {}

        def place(name, shape, dt, offset):
            return nc.alloc_sbuf_tensor_at(name, shape, dt, offset=offset)

        def region(name, size):
            at[name] = at["top"]
            at["top"] += size

        def sem(name):
            return ctx.enter_context(nc.semaphore(name))

        KB = 1024
        at["top"] = (nc.sbuf_base + 63) // 64 * 64
        for name, size in (("h", 32 * KB), ("xp", 16 * KB), ("act_hi", ACT_TILES * 4 * KB), ("act_lo", ACT_TILES * 4 * KB),
                           ("w", 24 * KB), ("gated", 4 * KB), ("lora0", 11 * KB + BW * CH * 4),
                           ("t", 16 * KB), ("mask", 2 * KB), ("pack", 4 * (F1 + 3 * H)), ("lora_b1", 4 * KB), ("small", 704)):
            region(name, size)

        h_hi = place("h_hi", [P, HK, TOK], F32R, at["h"])
        h_lo = place("h_lo", [P, HK, TOK], F32R, at["h"] + 16 * KB)
        xp = place("xp", [P, HK, TOK], F32, at["xp"])
        act_hi = place("act_hi", [P, ACT_TILES, TOK], F32R, at["act_hi"])
        act_lo = place("act_lo", [P, ACT_TILES, TOK], F32R, at["act_lo"])
        w_hi = place("w_hi", [P, 2, WT], F32R, at["w"])
        w_lo = place("w_lo", [P, 2, WT], F32R, at["w"] + 8 * KB)
        w_raw = place("w_raw", [P, 2, WT], F32, at["w"] + 16 * KB)
        gated = place("gated", [P, CH, CT], F32, at["gated"])
        a_dn = place("a_dn", [P, NKD, CH, 2 * RB], F32R, at["lora0"])
        b_split = place("b_split", [P, CH, BW], F32R, at["lora0"] + 11 * KB)
        b_raw = place("b_raw", [P, CH, BW], F32, at["lora0"] + 11 * KB)
        y_hi = place("y_hi", [P, HK, TOK], F32R, at["lora0"])
        y_lo = place("y_lo", [P, HK, TOK], F32R, at["lora0"] + 16 * KB)
        a1 = place("a1", [P, HK, CH, 2 * RB], F32R, at["lora0"] + 32 * KB)
        a1_raw = place("a1_raw", [P, NB, HK * R], F32, at["lora0"])
        b1_raw = place("b1_raw", [P, CH, H], F32, at["lora0"] + 2 * KB)
        b1_split = place("b1_split", [P, CH, H], F32R, at["lora_b1"])
        t_hi = place("t_hi", [P, 2, TOK], F32R, at["t"])
        t_lo = place("t_lo", [P, 2, TOK], F32R, at["t"] + 8 * KB)
        s_bc = [place(f"s_bc{i}", [P, DQ], F32, at["t"] + 4 * KB + 4 * DQ * i) for i in range(2)]
        gate_sum = place("gate_sum", [P, 2, CH, CT], F32, at["h"])
        up_sum = place("up_sum", [P, 2, CH, CT], F32, at["h"] + 8 * KB)
        seg_mask = place("seg_mask", [P, CT], F32, at["mask"])
        pack_long = place("pack_long", [P, F1], F32R, at["pack"])
        pack_short = place("pack_short", [P, 3, H], F32R, at["pack"] + 4 * F1)
        a_dn_raw = place("a_dn_raw", [P, NB, NKD * R], F32, at["xp"])
        pack_raw = place("pack_raw", [P, PACK], F32, at["xp"] + 4 * NB * NKD * R)
        a_gu_raw = place("a_gu_raw", [P, NB, HK * 2 * R], F32, at["act_hi"] + 20 * KB)
        a_gu_hi = place("a_gu_hi", [P, HK, CH, 2, BC, R], F32R, at["act_lo"] + 16 * KB)
        a_gu_lo = place("a_gu_lo", [P, HK, CH, 2, BC, R], F32R, at["act_lo"] + 20 * KB)
        b_hi = place("b_hi", [P, CH, BP], F32R, at["act_hi"] + 24 * KB)
        short_hi = place("short_hi", [P, H], F32R, at["act_lo"] + 24 * KB)
        short_part = place("short_part", [P, H], F32, at["act_lo"] + 26 * KB)
        small = at["small"]
        ids0 = place("ids0", [1, NB], I32, small)
        ids1 = place("ids1", [1, NB], I32, small + 32)
        bias = place("bias", [P, HK], F32, small + 64)
        row_id = place("row_id", [P, 4], I32, small + 96)
        sel = place("sel", [P, 12], F32, small + 128)
        s_group_in = place("s_group_in", [P, 2, GQ], F32, small + 192)
        s_group = place("s_group", [P, 2, GQ], F32, small + 256)
        s_down = place("s_down", [P, HK * (F1 // P)], F32, small + 320)
        assert small + 704 <= nc.sbuf_usable_end

        ps_gate = [ctx.enter_context(nc.psum_tensor(f"ps_gate{c}", [P, CT], F32)) for c in range(CH)]
        ps_up = [ctx.enter_context(nc.psum_tensor(f"ps_up{c}", [P, CT], F32)) for c in range(CH)]
        ps_down = [ctx.enter_context(nc.psum_tensor(f"ps_down{c}", [P, CT], F32)) for c in range(CH)]
        ps_m = ctx.enter_context(nc.psum_tensor("ps_m", [P, WT], F32))
        group_banks = [ps_gate[0][:, :], ps_gate[1][:, :], ps_m[:, 0:CT], ps_m[:, CT:WT], ps_up[0][:, :], ps_up[1][:, :]]

        raw_in = [sem(f"raw_in{s}") for s in range(2)]
        w_first_in = [sem(f"w_first_in{g}") for g in range(2)]
        x_in = [[sem(f"x_in{c}{k}") for k in range(HK)] for c in range(CH)]
        start_hi, start_lo = sem("start_hi"), sem("start_lo")
        x_again = sem("x_again")
        ids_in = [sem(f"ids_in{layer}") for layer in range(2)]
        bias_in, s_in = sem("bias_in"), sem("s_in")
        a_gu_in, b_in = ([sem(f"{n}{c}") for c in range(CH)] for n in ("a_gu_in", "b_in"))
        a_dn_in = sem("a_dn_in")
        a1_in, b1_in = sem("a1_in"), sem("b1_in")
        pack_zero, pack_in = sem("pack_zero"), sem("pack_in")
        mask_step, mask_ready = sem("mask_step"), sem("mask_ready")
        rows_ready = sem("rows_ready")
        sel_step = sem("sel_step")
        a_gu_hi_done, a_gu_ready = sem("a_gu_hi_done"), sem("a_gu_ready")
        a_dn_hi_done, a_dn_ready = sem("a_dn_hi_done"), sem("a_dn_ready")
        b_hi_done, b_ready = sem("b_hi_done"), sem("b_ready")
        a1_hi_done, a1_ready = sem("a1_hi_done"), sem("a1_ready")
        b1_hi_done, b1_ready = sem("b1_hi_done"), sem("b1_ready")
        pack_hi_done, pack_step, pack_ready = sem("pack_hi_done"), sem("pack_step"), sem("pack_ready")
        m_ready = sem("m_ready")
        w_prod = sem("w_prod")
        w_hi_done, w_ready = sem("w_hi_done"), sem("w_ready")
        gate_ready, up_ready = sem("gate_ready"), sem("up_ready")
        silu_done, prod_done = sem("silu_done"), sem("prod_done")
        act_hi_done, act_ready = sem("act_hi_done"), sem("act_ready")
        down_ready = sem("down_ready")
        group_ready = sem("group_ready")
        first_scaled = sem("first_scaled")
        group_added = sem("group_added")
        up_scaled, up_added = sem("up_scaled"), sem("up_added")
        sum_done = sem("sum_done")
        h_hi_done, h_ready = sem("h_hi_done"), sem("h_ready")
        t_sums, t_lo_rows, t_masked = sem("t_sums"), sem("t_lo_rows"), sem("t_masked")
        t_added, t_hi_done, t_lo_done = sem("t_added"), sem("t_hi_done"), sem("t_lo_done")
        out_done = sem("out_done")

        def chunk(c):
            return slice(c * CT, (c + 1) * CT)

        def ds(start, size):
            return bass.ds(start, size)

        def widths(ph, i, jj):
            if ph.layer == "cond" and ph.part == 1 and isinstance(i, int) and 2 * i + jj == ph.tiles - 1:
                return F0_TAIL
            return P

        def k_rows(ph, k):
            return F0_TAIL if ph.name == "cond down b" and k == k_count(ph) - 1 else P

        def k_count(ph):
            return {"cond": (6, 5)[ph.part], "cond1": HK}.get(ph.layer, ACT_TILES)

        def columns(ph):
            return WT if ph.kind == "gate_up" else k_count(ph) * P

        def slot(ph, jj, i):
            return (ph.t0 + jj) % 2

        def raw_count(ph, i, jj):
            return ph.raw0[slot(ph, jj, i)] + 16 * ph.loads * (i + jj // 2 + 1)

        def b_col(ph, j, g):
            f = ph.first + j
            return f * 2 * P + g * (F0_TAIL if f == NKD - 1 else P)

        def unit_banks(ph, i, jj, c):
            if ph is phases[0] and isinstance(i, int) and 2 * i + jj == 1 and c == 0:
                return ps_down
            return ps_gate[c], ps_up[c]

        def down_group(o, k, c):
            return CH * (KQ * o + k) + c

        def q_cols(ph):
            return slice(0, WT - DQ) if ph.kind == "gate_up" else slice(DQ, DQ + KQ * P)

        def dq_cols(ph):
            return slice(WT - DQ, WT) if ph.kind == "gate_up" else slice(0, DQ)

        start = [("w", 0)] + [("x", 0, k) for k in range(HK)] + [("w", 1)] + [("x", 1, k) for k in range(HK)]

        def started(*item):
            return start.index(item) + 1

        def tile_steps(eng, ph, step, in_loop=True, peeled=0):
            if ph.kind == "down":
                peeled, in_loop = 0, False
            looped = (ph.tiles - 1) // 2 if in_loop else peeled
            for j in range(2 * peeled):
                step(j // 2, j % 2, ph, (j + 1) // 2, (j + 1) % 2)
            if looped > peeled:
                with eng.Fori(peeled, looped) as i:
                    for jj in range(2):
                        step(i, jj, ph, i, jj + 1)
            for j in range(2 * looped, ph.tiles):
                if j + 1 < ph.tiles:
                    step(j // 2, j % 2, ph, j // 2, j % 2 + 1)
                else:
                    step(j // 2, j % 2, following.get(ph), 0, 0)

        def w_prod_count(ph, i, jj):
            scaled = sum(p.tiles for p in phases if p.prep == "scale")
            if ph.prep == "scale":
                return ph.m0 + 2 * i + jj + 1
            return scaled + ph.t0 - named["ffn1 gate/up a"].t0 + 2 * i + jj + 1

        def h_seen(ph):
            return {"ffn0 down b": CH * HK, "cond1": 2 * CH * HK}.get(ph.name, 0)

        def load_a_gu(eng, b):
            e = eng.value_load(ids0[0:1, b:b + 1], min_val=0, max_val=d["a_gu"].shape[0] - 1)
            eng.dma_start(a_gu_raw[:, b, :], d["a_gu"][ds(e, 1)].rearrange("a p n -> (a p) n")).then_inc(a_gu_in[b // BC], 16)

        def load_b(eng, b):
            e = eng.value_load(ids0[0:1, b:b + 1], min_val=0, max_val=d["b0"].shape[0] - 1)
            row = RB + b % BC * R
            eng.dma_start(b_raw[row:row + R, b // BC, :], d["b0"][ds(e, 1)].rearrange("a r n -> (a r) n")).then_inc(b_in[b // BC], 16)

        block = ctx.enter_context(nc.Block())

        @block.sync
        def _(sp):
            def load_tile(ph, i, jj):
                s = slot(ph, jj, i)
                if not isinstance(i, int) or ph.t0 + 2 * i + jj > 2:
                    sp.wait_ge(w_ready, ph.t0 + 2 * i + jj - 2)
                elif ph.t0 + 2 * i + jj == 2:
                    sp.wait_ge(start_lo, started("w", 1))
                n = columns(ph)
                if ph.kind == "gate_up":
                    f = ph.first + 2 * i + jj
                    if widths(ph, i, jj) == F0_TAIL:
                        sp.dma_start(w_raw[:, s, :].rearrange("p (g f) -> p g f", f=P)[:, :, 0:F0_TAIL],
                                     d["cond_gu_tail"].rearrange("p (g f) -> p g f", f=F0_TAIL)).then_inc(raw_in[s], 16)
                        return
                    src = {"cond": d["cond_gu"], "ffn0": d["ffn0_gu"], "ffn1": d["ffn1_gu"]}[ph.layer]
                    dst = w_raw[:, s, :]
                    if ph.prep == "dequant":
                        dst = dst.bitcast(I32)
                    sp.dma_start(dst, src[ds(f, 1)].rearrange("a p n -> (a p) n")).then_inc(raw_in[s], 16)
                    if ph.prep == "dequant":
                        sp.dma_start(s_group_in[:, s, :], d["ffn1_group_s"][ds(f, 1)].rearrange("a p n -> (a p) n")).then_inc(raw_in[s], 16)
                        sp.dma_start(s_bc[s][:, :], d["ffn1_up_s"][ds(f, 1), :].partition_broadcast(P)).then_inc(raw_in[s], 16)
                    return
                o = 2 * i + jj
                if ph.layer == "cond":
                    src = d[("cond_dn_a", "cond_dn_b")[ph.part]]
                    main = src.shape[2]
                    sp.dma_start(w_raw[:, s, 0:main], src[o]).then_inc(raw_in[s], 16)
                    if ph.part:
                        sp.dma_start(w_raw[0:F0_TAIL, s, main:n], d["cond_dn_tail"][o]).then_inc(raw_in[s], 16)
                elif ph.layer == "cond1":
                    sp.dma_start(w_raw[:, s, 0:n], d["cond1_w"][o]).then_inc(raw_in[s], 16)
                elif ph.layer == "ffn0":
                    sp.dma_start(w_raw[:, s, 0:n], d["ffn0_dn"][ph.part, o]).then_inc(raw_in[s], 16)
                else:
                    sp.dma_start(w_raw[:, s, 0:n].bitcast(I32), d["ffn1_dn"][ph.part, o]).then_inc(raw_in[s], 16)
                    sp.dma_start(s_bc[s][:, :], d["ffn1_dn_s"][ph.part, o:o + 1, :].partition_broadcast(P)).then_inc(raw_in[s], 16)

            sp.dma_start(ids0[:, :], d["ids0"]).then_inc(ids_in[0], 16)
            for item in start:
                if item[0] == "w":
                    half = slice(item[1] * HK * P, (item[1] + 1) * HK * P)
                    sp.dma_start(w_raw[:, 0, half], d["cond_gu"][0][:, half]).then_inc(w_first_in[item[1]], 16)
                else:
                    _, c, k = item
                    sp.dma_start(xp[:, k, chunk(c)], d["x"][k][:, chunk(c)]).then_inc(x_in[c][k], 16)
            sp.wait_ge(ids_in[0], 16)
            for b in range(BC, NB):
                load_a_gu(sp, b)
            load_tile(phases[0], 0, 1)
            for b in range(BC, NB):
                load_b(sp, b)
            sp.dma_start(ids1[:, :], d["ids1"]).then_inc(ids_in[1], 16)
            for ph in phases:
                if ph.name == "cond1":
                    sp.dma_start(bias[:, :], d["cond1_b"]).then_inc(bias_in, 16)
                    sp.dma_start(s_down[:, :], d["ffn1_down_s"]).then_inc(s_in, 16)
                if ph.name == "ffn0 down a":
                    sp.wait_ge(h_ready, CH * HK)
                    sp.dma_start(xp[:, :, :], d["x"].rearrange("k p n -> p k n")).then_inc(x_again, 16)
                unloaded = 0
                if ph is phases[0]:
                    for j in range(2, 4):
                        load_tile(ph, j // 2, j % 2)
                    unloaded = 2
                pairs = ph.tiles // 2
                if ph.kind == "gate_up":
                    with sp.Fori(unloaded, pairs) as i:
                        load_tile(ph, i, 0)
                        load_tile(ph, i, 1)
                    if ph.tiles % 2:
                        load_tile(ph, pairs, 0)
                else:
                    for o in range(ph.tiles):
                        load_tile(ph, o // 2, o % 2)
            last = phases[-1]
            for o in range(HK):
                for c in range(CH):
                    sp.wait_ge(group_added, last.a0 + down_group(o, KQ - 1, c) + 1)
                    sp.dma_start(out[o][:, chunk(c)], xp[:, o, chunk(c)]).then_inc(out_done, 16)
            sp.wait_ge(out_done, 16 * CH * HK)

        @block.gpsimd
        def _(pool):
            pool.wait_ge(ids_in[0], 16)
            for b in range(BC):
                load_a_gu(pool, b)
            for b in range(BC):
                load_b(pool, b)
            nc.gpsimd.memset(seg_mask[:, :], 1.0).then_inc(mask_step, 1)
            pool.wait_ge(mask_step, 1)
            for n in range(2):
                segs = seg_mask[n * RB:(n + 1) * RB, :].rearrange("p (s n) -> p s n", s=BC)
                nc.gpsimd.affine_select(out=segs, in_=segs, compare_op=ALU.is_ge, fill=0.0, base=0,
                                        pattern=[[-R, BC], [0, P]], channel_multiplier=1).then_inc(mask_step, 1)
                pool.wait_ge(mask_step, n + 2)
                nc.gpsimd.affine_select(out=segs, in_=segs, compare_op=ALU.is_ge, fill=0.0, base=R - 1,
                                        pattern=[[R, BC], [0, P]], channel_multiplier=-1).then_inc(mask_ready, 1)
                pool.wait_ge(mask_ready, n + 1)
            nc.gpsimd.iota(row_id[:, 0:1], [[0, 1]], base=0, channel_multiplier=1).then_inc(rows_ready, 1)
            pool.wait_ge(start_lo, len(start))
            for b in range(NB):
                e = pool.value_load(ids0[0:1, b:b + 1], min_val=0, max_val=d["a_dn"].shape[0] - 1)
                full = (NKD - 1) * R
                pool.dma_start(a_dn_raw[:, b, 0:full], d["a_dn"][ds(e, 1)].rearrange("a p n -> (a p) n")).then_inc(a_dn_in, 16)
                pool.dma_start(a_dn_raw[0:F0_TAIL, b, full:full + R],
                               d["a_dn_tail"][ds(e, 1)].rearrange("a p n -> (a p) n")).then_inc(a_dn_in, 16)
            nc.gpsimd.memset(pack_raw[:, :], 0.0).then_inc(pack_zero, 1)
            pool.wait_ge(pack_zero, 1)
            for q in range(3):
                for v in range(4):
                    row = 32 * q + SR * v
                    pool.dma_start(pack_raw[row:row + SR, :], d["factors"][q]).then_inc(pack_in, 16)
            pool.wait_ge(ids_in[1], 16)
            pool.wait_ge(down_ready, 2 * CH * HK)
            for b in range(NB):
                e = pool.value_load(ids1[0:1, b:b + 1], min_val=0, max_val=d["a1"].shape[0] - 1)
                pool.dma_start(a1_raw[:, b, :], d["a1"][ds(e, 1)].rearrange("a p n -> (a p) n")).then_inc(a1_in, 16)
                row = RB + b % BC * R
                pool.dma_start(b1_raw[row:row + R, b // BC, :], d["b1"][ds(e, 1)].rearrange("a r n -> (a r) n")).then_inc(b1_in, 16)

            def tile_lo(ph, i, jj):
                s, n = slot(ph, jj, i), dq_cols(ph)
                pool.wait_ge(w_hi_done, ph.t0 + 2 * i + jj)
                nc.gpsimd.tensor_tensor(w_lo[:, s, n], w_raw[:, s, n], w_hi[:, s, n].bitcast(F32), ALU.subtract).then_inc(w_ready, 1)

            def unit_lo(ph, i, jj, c):
                pool.wait_ge(act_hi_done, ph.g0 + CH * (2 * i + jj) + c + 1)
                j = ds(2 * i + jj, 1)
                nc.gpsimd.tensor_tensor(act_lo[:, j, chunk(c)].rearrange("p a n -> p (a n)"), gate_sum[:, jj % 2, c, :],
                                        act_hi[:, j, chunk(c)].rearrange("p a n -> p (a n)").bitcast(F32), ALU.subtract).then_inc(act_ready, 1)

            tile_lo(named["ffn1 gate/up a"], 0, 0)
            for ph in phases:
                if ph.prep != "dequant":
                    continue

                def step(i, jj, nxt, ni, njj, ph=ph):
                    finish = ph.kind == "gate_up" and (not isinstance(i, int) or 2 * i + jj > 0)
                    if finish:
                        unit_lo(ph, i, jj - 1, 0)
                    if nxt is not None:
                        tile_lo(nxt, ni, njj)
                    if finish:
                        unit_lo(ph, i, jj - 1, 1)

                tile_steps(pool, ph, step, peeled=1)
                if ph.kind == "gate_up":
                    for c in range(CH):
                        unit_lo(ph, ph.tiles // 2, 0, c)

        @block.scalar
        def _(act):
            def integers(ph, i, jj):
                s, n = slot(ph, jj, i), q_cols(ph)
                act.wait_ge(raw_in[s], raw_count(ph, i, jj))
                nc.scalar.activation(w_hi[:, s, n], w_raw[:, s, n].bitcast(I32), ACT.Copy)

            def tile_hi(ph, i, jj):
                s, n = slot(ph, jj, i), slice(0, columns(ph))
                if ph.prep == "split":
                    act.wait_ge(raw_in[s], raw_count(ph, i, jj))
                else:
                    act.wait_ge(w_prod, w_prod_count(ph, i, jj))
                if ph.prep == "dequant":
                    n = dq_cols(ph)
                nc.scalar.activation(w_hi[:, s, n], w_raw[:, s, n], ACT.Copy).then_inc(w_hi_done, 1)

            def hi_of_b(p):
                cols = slice(p * BP, min((p + 1) * BP, BW))
                n = cols.stop - cols.start
                for c in range(CH):
                    if p == 0:
                        act.wait_ge(b_in[c], 16 * BC)
                    else:
                        act.wait_ge(b_ready, CH * (p - 1) + c + 1)
                    nc.scalar.activation(b_hi[RB:2 * RB, c, 0:n], b_raw[RB:2 * RB, c, cols], ACT.Copy)
                    nc.scalar.activation(b_split[0:RB, c, cols], b_raw[RB:2 * RB, c, cols], ACT.Copy).then_inc(b_hi_done, 1)

            def hi_of_t(base, c, nets):
                act.wait_ge(t_masked, base + c + 1)
                for g in range(nets):
                    rows = slice(g * RB, (g + 1) * RB)
                    nc.scalar.activation(t_hi[0:RB, g, chunk(c)], gated[rows, c, :], ACT.Copy)
                    last = nc.scalar.activation(t_hi[RB:2 * RB, g, chunk(c)], gated[rows, c, :], ACT.Copy)
                last.then_inc(t_hi_done, 1)

            def hi_of_a_dn():
                act.wait_ge(a_dn_in, 16 * 2 * NB)
                for c in range(CH):
                    for rows, k0, k1 in ((P, 0, NKD - 1), (F0_TAIL, NKD - 1, NKD)):
                        nc.scalar.activation(a_dn[0:rows, k0:k1, c, 0:RB].rearrange("p k (b r) -> p k b r", r=R),
                                             a_dn_raw[0:rows, c * BC:(c + 1) * BC, k0 * R:k1 * R].rearrange("p b (k r) -> p k b r", r=R),
                                             ACT.Copy).then_inc(a_dn_hi_done, 1)

            def hi_of_pack():
                act.wait_ge(pack_in, 16 * 12)
                nc.scalar.activation(pack_long[:, :], pack_raw[:, 0:F1], ACT.Copy).then_inc(pack_hi_done, 1)
                nc.scalar.activation(short_hi[:, :], pack_raw[:, F1:PACK], ACT.Copy).then_inc(pack_hi_done, 1)

            def gate_up_tile(ph, i, jj):
                m = widths(ph, i, jj)
                for c in range(CH):
                    n = ph.g0 + CH * (2 * i + jj) + c
                    act.wait_ge(gate_ready, n + 1)
                    if not isinstance(i, int) or n >= CH:
                        act.wait_ge(act_ready, n - 1)
                    nc.scalar.activation(gated[0:m, c, :], unit_banks(ph, i, jj, c)[0][0:m, :], ACT.Silu).then_inc(silu_done, 1)
                    act.wait_ge(prod_done, n + 1)
                    nc.scalar.activation(act_hi[0:m, ds(2 * i + jj, 1), chunk(c)].rearrange("p a n -> p (a n)"),
                                         gated[0:m, c, :], ACT.Copy).then_inc(act_hi_done, 1)

            def unit_hi(ph, i, jj, c):
                act.wait_ge(prod_done, ph.g0 + CH * (2 * i + jj) + c + 1)
                nc.scalar.activation(act_hi[:, ds(2 * i + jj, 1), chunk(c)].rearrange("p a n -> p (a n)"),
                                     gate_sum[:, jj % 2, c, :], ACT.Copy).then_inc(act_hi_done, 1)

            def group_tile(ph, i, jj, nxt, ni, njj):
                s, begun = slot(ph, jj, i), not isinstance(i, int) or 2 * i + jj > 0
                for c in range(CH):
                    u = CH * (2 * i + jj) + c
                    act.wait_ge(group_ready, ph.q0 + GQ * u + 1)
                    act.wait_ge(act_ready, ph.g0 + u - 3 if begun else ph.g0)
                    nc.scalar.activation(gate_sum[:, jj % 2, c, :], group_banks[0], ACT.Copy, scale=s_group[:, s, 0:1]).then_inc(first_scaled, 1)
                    if begun:
                        unit_hi(ph, i, jj - 1, c)
                    act.wait_ge(group_ready, ph.q0 + GQ * u + GQ)
                    nc.scalar.activation(up_sum[:, jj % 2, c, :], ps_down[c][:, :], ACT.Copy, scale=s_group[:, s, HK:GQ]).then_inc(up_scaled, 1)
                    if c == 0:
                        if begun:
                            act.wait_ge(up_ready, ph.g0 + CH * (2 * i + jj))
                        integers(nxt, ni, njj)
                        tile_hi(nxt, ni, njj)
                    act.wait_ge(group_added, ph.a0 + (HK - 1) * (u + 1))
                    nc.scalar.activation(gate_sum[:, jj % 2, c, :], gate_sum[:, jj % 2, c, :], ACT.Silu).then_inc(silu_done, 1)

            def down_tile(ph, o):
                for c in range(CH):
                    if ph.name in ("cond down b", "ffn0 down b"):
                        act.wait_ge(sum_done, ph.d0 + CH * o + c + 1)
                        nc.scalar.activation(h_hi[:, o, chunk(c)], xp[:, o, chunk(c)], ACT.Copy).then_inc(h_hi_done, 1)
                    elif ph.name == "cond1":
                        act.wait_ge(sum_done, ph.d0 + CH * o + c + 1)
                        nc.scalar.activation(y_hi[:, o, chunk(c)], gated[:, c, :], ACT.Copy).then_inc(h_hi_done, 1)

            def small_t(base, scale):
                for c in range(CH):
                    act.wait_ge(t_sums, base + c + 1)
                    nc.scalar.activation(gated[0:RB, c, :], ps_m[RB:2 * RB, chunk(c)], ACT.Copy, scale=scale).then_inc(t_lo_rows, 1)
                for c in range(CH):
                    hi_of_t(base, c, 1)

            for item in start:
                if item[0] == "w":
                    half = slice(item[1] * HK * P, (item[1] + 1) * HK * P)
                    act.wait_ge(w_first_in[item[1]], 16)
                    nc.scalar.activation(w_hi[:, 0, half], w_raw[:, 0, half], ACT.Copy).then_inc(start_hi, 1)
                else:
                    _, c, k = item
                    act.wait_ge(x_in[c][k], 16)
                    nc.scalar.activation(h_hi[:, k, chunk(c)], xp[:, k, chunk(c)], ACT.Copy).then_inc(start_hi, 1)
            for c in range(CH):
                act.wait_ge(a_gu_in[c], 16 * BC)
                for g in range(2):
                    nc.scalar.activation(a_gu_hi[:, :, c, g], a_gu_raw[:, c * BC:(c + 1) * BC, :].rearrange(
                        "p b (k g r) -> p g k b r", g=2, r=R)[:, g], ACT.Copy).then_inc(a_gu_hi_done, 1)
            tile_hi(phases[0], 0, 1)
            hi_of_b(0)
            for c in range(CH):
                hi_of_t(0, c, 2)

            for ph in phases:
                if ph.name == "ffn0 down b":
                    act.wait_ge(a1_in, 16 * NB)
                    for c in range(CH):
                        nc.scalar.activation(a1[:, :, c, 0:RB].rearrange("p k (b r) -> p k b r", r=R),
                                             a1_raw[:, c * BC:(c + 1) * BC, :].rearrange("p b (k r) -> p k b r", r=R),
                                             ACT.Copy).then_inc(a1_hi_done, 1)
                    act.wait_ge(b1_in, 16 * NB)
                    nc.scalar.activation(b1_split[0:RB, :, :], b1_raw[RB:2 * RB, :, :], ACT.Copy)
                    nc.scalar.activation(b1_split[RB:2 * RB, :, :], b1_raw[RB:2 * RB, :, :], ACT.Copy).then_inc(b1_hi_done, 1)
                def step(i, jj, nxt, ni, njj, ph=ph):
                    if ph.kind == "gate_up" and ph.prep == "dequant":
                        group_tile(ph, i, jj, nxt, ni, njj)
                        return
                    if nxt is not None and ph.kind == "gate_up" and (not isinstance(i, int) or 2 * i + jj > 0):
                        act.wait_ge(up_ready, ph.g0 + CH * (2 * i + jj))
                    if nxt is not None and nxt.prep == "dequant":
                        integers(nxt, ni, njj)
                    if nxt is not None and not (ph is phases[0] and 2 * i + jj == 0):
                        tile_hi(nxt, ni, njj)
                    if ph.kind == "gate_up":
                        gate_up_tile(ph, i, jj)
                        if ph is phases[0]:
                            between_tiles(2 * i + jj)
                    else:
                        if ph.name == "cond down b" and 2 * i + jj == 0:
                            small_t(CH, 0.5)
                        if ph.name == "cond1" and 2 * i + jj == 0:
                            small_t(2 * CH, 2.0)
                        down_tile(ph, 2 * i + jj)

                def between_tiles(j):
                    hi_of_b(j + 1)
                    if j == 3:
                        hi_of_pack()
                    if j == 5:
                        hi_of_a_dn()

                if ph.kind == "gate_up" and ph.d0 > 0:
                    act.wait_ge(down_ready, ph.d0)
                    if ph.q0 > 0:
                        act.wait_ge(group_ready, ph.q0)
                if ph.kind == "down":
                    def step_down(i, jj, nxt, ni, njj, ph=ph, step=step):
                        o = 2 * i + jj
                        if o == 0:
                            if ph.name != "cond1":
                                act.wait_ge(up_ready, ph.g0)
                            else:
                                act.wait_ge(down_ready, ph.d0)
                        elif ph.prep == "dequant":
                            act.wait_ge(group_ready, ph.q0 + KQ * CH * o)
                        else:
                            act.wait_ge(down_ready, ph.d0 + CH * o)
                        step(i, jj, nxt, ni, njj)
                    tile_steps(act, ph, step_down)
                else:
                    tile_steps(act, ph, step, in_loop=ph is not phases[0], peeled=1 if ph.prep == "dequant" else 0)
                    if ph.prep == "dequant":
                        for c in range(CH):
                            unit_hi(ph, ph.tiles // 2, 0, c)

        @block.vector
        def _(dve):
            chain = [0]

            def link(ins):
                chain[0] += 1
                ins.then_inc(sel_step, 1)
                dve.wait_ge(sel_step, chain[0])

            def lo(out_, value, hi):
                return nc.vector.tensor_tensor(out_, value, hi.bitcast(F32), ALU.subtract)

            def tile_product(ph, i, jj):
                s, n = slot(ph, jj, i), columns(ph)
                dve.wait_ge(raw_in[s], raw_count(ph, i, jj))
                if ph.prep == "scale":
                    dve.wait_ge(m_ready, ph.m0 + 2 * i + jj + 1)
                    nc.vector.tensor_tensor(w_raw[:, s, 0:n], w_raw[:, s, 0:n], ps_m[:, 0:n], ALU.mult).then_inc(w_prod, 1)
                else:
                    n = dq_cols(ph)
                    if ph.kind == "gate_up":
                        nc.vector.tensor_copy(s_group[:, s, :], s_group_in[:, s, :])
                    nc.vector.tensor_tensor(w_raw[:, s, n], w_raw[:, s, n].bitcast(I32), s_bc[s][:, :], ALU.mult).then_inc(w_prod, 1)

            def tile_lo(ph, i, jj):
                s, n = slot(ph, jj, i), slice(0, columns(ph))
                dve.wait_ge(w_hi_done, ph.t0 + 2 * i + jj)
                lo(w_lo[:, s, n], w_raw[:, s, n], w_hi[:, s, n]).then_inc(w_ready, 1)

            def lo_of_b(p):
                cols = slice(p * BP, min((p + 1) * BP, BW))
                for c in range(CH):
                    dve.wait_ge(b_hi_done, CH * p + c + 1)
                    lo(b_split[RB:2 * RB, c, cols], b_raw[RB:2 * RB, c, cols],
                       b_hi[RB:2 * RB, c, 0:cols.stop - cols.start]).then_inc(b_ready, 1)

            def lo_of_t(base, c, nets):
                dve.wait_ge(t_hi_done, base + c + 1)
                for g in range(nets):
                    rows = slice(g * RB, (g + 1) * RB)
                    for to in range(2):
                        last = lo(t_lo[to * RB:(to + 1) * RB, g, chunk(c)], gated[rows, c, :], t_hi[rows, g, chunk(c)])
                last.then_inc(t_lo_done, 1)

            def lo_of_a_dn():
                n = 0
                for c in range(CH):
                    for rows, k0, k1 in ((P, 0, NKD - 1), (F0_TAIL, NKD - 1, NKD)):
                        n += 1
                        dve.wait_ge(a_dn_hi_done, n)
                        hi, low = (a_dn[0:rows, k0:k1, c, x * RB:(x + 1) * RB].rearrange("p k (b r) -> p k b r", r=R) for x in range(2))
                        lo(low, a_dn_raw[0:rows, c * BC:(c + 1) * BC, k0 * R:k1 * R].rearrange("p b (k r) -> p k b r", r=R),
                           hi).then_inc(a_dn_ready, 1)

            def pack_rows():
                dve.wait_ge(rows_ready, 1)
                link(nc.vector.tensor_scalar(row_id[:, 1:2], row_id[:, 0:1], 2, 1, ALU.logical_shift_right, ALU.bitwise_and))
                link(nc.vector.tensor_scalar(row_id[:, 2:3], row_id[:, 0:1], 3, 1, ALU.logical_shift_right, ALU.bitwise_and))
                link(nc.vector.tensor_scalar(row_id[:, 3:4], row_id[:, 0:1], 5, None, ALU.logical_shift_right))
                link(nc.vector.tensor_copy(sel[:, 0:1], row_id[:, 1:2]))
                link(nc.vector.tensor_copy(sel[:, 2:3], row_id[:, 2:3]))
                link(nc.vector.tensor_copy(sel[:, 10:11], row_id[:, 3:4]))
                for a in (0, 2):
                    link(nc.vector.tensor_scalar(sel[:, a + 1:a + 2], sel[:, a:a + 1], -2.0, 1.0, ALU.mult, ALU.add))
                for q in range(3):
                    link(nc.vector.tensor_scalar(sel[:, 11:12], sel[:, 10:11], float(q), None, ALU.is_equal))
                    for a in range(2):
                        link(nc.vector.tensor_tensor(sel[:, 4 + 2 * q + a:5 + 2 * q + a], sel[:, 2 + a:3 + a], sel[:, 11:12], ALU.mult))

            def pack_long_factors():
                dve.wait_ge(pack_hi_done, 2)
                nc.vector.tensor_scalar(pack_raw[:, 0:F1], pack_raw[:, 0:F1], sel[:, 0:1], None, ALU.mult).then_inc(pack_step, 1)
                dve.wait_ge(pack_step, 1)
                nc.vector.scalar_tensor_tensor(out=pack_long[:, :], in0=pack_long[:, :].bitcast(F32), scalar=sel[:, 1:2],
                                               in1=pack_raw[:, 0:F1], op0=ALU.mult, op1=ALU.add).then_inc(pack_ready, 1)

            def pack_short_factors():
                for q in range(3):
                    a = 4 + 2 * q
                    dve.wait_ge(pack_ready, q + 1)
                    nc.vector.tensor_scalar(short_part[:, :], pack_raw[:, F1:PACK], sel[:, a:a + 1], None, ALU.mult).then_inc(pack_step, 1)
                    dve.wait_ge(pack_step, q + 2)
                    nc.vector.scalar_tensor_tensor(out=pack_short[:, q, :], in0=short_hi[:, :].bitcast(F32), scalar=sel[:, a + 1:a + 2],
                                                   in1=short_part[:, :], op0=ALU.mult, op1=ALU.add).then_inc(pack_ready, 1)

            def gate_up_tile(ph, i, jj):
                m = widths(ph, i, jj)
                for c in range(CH):
                    n = ph.g0 + CH * (2 * i + jj) + c
                    dve.wait_ge(silu_done, n + 1)
                    dve.wait_ge(up_ready, n + 1)
                    nc.vector.tensor_tensor(gated[0:m, c, :], gated[0:m, c, :], unit_banks(ph, i, jj, c)[1][0:m, :], ALU.mult).then_inc(prod_done, 1)
                    dve.wait_ge(act_hi_done, n + 1)
                    j = ds(2 * i + jj, 1)
                    lo(act_lo[0:m, j, chunk(c)].rearrange("p a n -> p (a n)"), gated[0:m, c, :],
                       act_hi[0:m, j, chunk(c)].rearrange("p a n -> p (a n)")).then_inc(act_ready, 1)

            def unit_product(ph, i, jj, c):
                n, u = ph.g0 + CH * (2 * i + jj) + c, CH * (2 * i + jj) + c
                dve.wait_ge(silu_done, n + 1)
                dve.wait_ge(up_ready, n + 1)
                gate, up = gate_sum[:, jj % 2, c, :], up_sum[:, jj % 2, c, :]
                nc.vector.tensor_tensor(up, up, ps_up[c][:, :], ALU.add).then_inc(up_added, 1)
                dve.wait_ge(up_added, ph.f0 + u + 1)
                nc.vector.tensor_tensor(gate, gate, up, ALU.mult).then_inc(prod_done, 1)

            def group_tile(ph, i, jj, nxt, ni, njj):
                for c in range(CH):
                    u = CH * (2 * i + jj) + c
                    dve.wait_ge(first_scaled, ph.f0 + u + 1)
                    for k in range(1, HK):
                        dve.wait_ge(group_ready, ph.q0 + GQ * u + k + 1)
                        if k > 1:
                            dve.wait_ge(group_added, ph.a0 + (HK - 1) * u + k - 1)
                        gate = gate_sum[:, jj % 2, c, :]
                        nc.vector.scalar_tensor_tensor(out=gate, in0=group_banks[k], scalar=s_group[:, slot(ph, jj, i), k:k + 1], in1=gate, op0=ALU.mult, op1=ALU.add).then_inc(group_added, 1)
                        if k == 1 and c == 0:
                            tile_product(nxt, ni, njj)
                    if c > 0:
                        unit_product(ph, i, jj, 0)
                    elif not isinstance(i, int) or 2 * i + jj > 0:
                        unit_product(ph, i, jj - 1, CH - 1)

            def down_tile(ph, o):
                for c in range(CH):
                    n = ph.d0 + CH * o + c
                    here = xp[:, o, chunk(c)]
                    dve.wait_ge(down_ready, n + 1)
                    if ph.name == "cond down a":
                        nc.vector.tensor_copy(here, ps_down[c][:, :]).then_inc(sum_done, 1)
                    elif ph.name == "cond1":
                        nc.vector.tensor_scalar(gated[:, c, :], ps_down[c][:, :], bias[:, o:o + 1], None, ALU.add).then_inc(sum_done, 1)
                    else:
                        nc.vector.tensor_tensor(here, here, ps_down[c][:, :], ALU.add).then_inc(sum_done, 1)
                    hs = h_seen(ph) + CH * o + c + 1
                    if ph.name in ("cond down b", "ffn0 down b"):
                        dve.wait_ge(h_hi_done, hs)
                        lo(h_lo[:, o, chunk(c)], here, h_hi[:, o, chunk(c)]).then_inc(h_ready, 1)
                    elif ph.name == "cond1":
                        dve.wait_ge(h_hi_done, hs)
                        lo(y_lo[:, o, chunk(c)], gated[:, c, :], y_hi[:, o, chunk(c)]).then_inc(h_ready, 1)
                if ph.prep == "dequant":
                    for k in range(KQ):
                        for c in range(CH):
                            m = down_group(o, k, c)
                            here = xp[:, o, chunk(c)]
                            col = o * (F1 // P) + ph.first + DQ // P + k
                            if k > 0:
                                dve.wait_ge(group_added, ph.a0 + m - CH + 1)
                            else:
                                dve.wait_ge(sum_done, ph.d0 + CH * o + c + 1)
                            dve.wait_ge(group_ready, ph.q0 + m + 1)
                            nc.vector.scalar_tensor_tensor(out=here, in0=group_banks[m % len(group_banks)], scalar=s_down[:, col:col + 1],
                                                           in1=here, op0=ALU.mult, op1=ALU.add).then_inc(group_added, 1)

            def small_t(base, scale):
                n = base - CH
                for c in range(CH):
                    dve.wait_ge(t_lo_rows, n + c + 1)
                    nc.vector.scalar_tensor_tensor(out=gated[0:RB, c, :], in0=ps_m[0:RB, chunk(c)], scalar=scale,
                                                   in1=gated[0:RB, c, :], op0=ALU.mult, op1=ALU.add).then_inc(t_added, 1)
                    dve.wait_ge(t_added, n + c + 1)
                    nc.vector.tensor_tensor(gated[0:RB, c, :], gated[0:RB, c, :], seg_mask[0:RB, :], ALU.mult).then_inc(t_masked, 1)
                for c in range(CH):
                    lo_of_t(base, c, 1)

            for n, item in enumerate(start):
                dve.wait_ge(start_hi, n + 1)
                if item[0] == "w":
                    half = slice(item[1] * HK * P, (item[1] + 1) * HK * P)
                    lo(w_lo[:, 0, half], w_raw[:, 0, half], w_hi[:, 0, half]).then_inc(start_lo, 1)
                else:
                    _, c, k = item
                    lo(h_lo[:, k, chunk(c)], xp[:, k, chunk(c)], h_hi[:, k, chunk(c)]).then_inc(start_lo, 1)
            for c in range(CH):
                for g in range(2):
                    dve.wait_ge(a_gu_hi_done, 2 * c + g + 1)
                    lo(a_gu_lo[:, :, c, g], a_gu_raw[:, c * BC:(c + 1) * BC, :].rearrange("p b (k g r) -> p g k b r", g=2, r=R)[:, g],
                       a_gu_hi[:, :, c, g]).then_inc(a_gu_ready, 1)
            tile_lo(phases[0], 0, 1)
            lo_of_b(0)
            dve.wait_ge(mask_ready, 2)
            for c in range(CH):
                dve.wait_ge(t_sums, c + 1)
                nc.vector.scalar_tensor_tensor(out=gated[:, c, :], in0=ps_m[:, chunk(c)], scalar=0.5, in1=seg_mask[:, :],
                                               op0=ALU.mult, op1=ALU.mult).then_inc(t_masked, 1)
                lo_of_t(0, c, 2)

            for ph in phases:
                if ph.name == "ffn0 down b":
                    for c in range(CH):
                        dve.wait_ge(a1_hi_done, c + 1)
                        hi, low = (a1[:, :, c, x * RB:(x + 1) * RB].rearrange("p k (b r) -> p k b r", r=R) for x in range(2))
                        lo(low, a1_raw[:, c * BC:(c + 1) * BC, :].rearrange("p b (k r) -> p k b r", r=R), hi).then_inc(a1_ready, 1)
                    dve.wait_ge(b1_hi_done, 1)
                    lo(b1_split[RB:2 * RB, :, :], b1_raw[RB:2 * RB, :, :], b1_split[RB:2 * RB, :, :]).then_inc(b1_ready, 1)
                if ph.name == "cond down a":
                    dve.wait_ge(a_dn_ready, 4)
                    dve.wait_ge(pack_ready, 4)
                if ph.name == "ffn0 down a":
                    dve.wait_ge(x_again, 16)
                if ph.name == "cond1":
                    dve.wait_ge(bias_in, 16)

                if ph.name == "ffn1 down a":
                    dve.wait_ge(s_in, 16)

                def step(i, jj, nxt, ni, njj, ph=ph):
                    if ph.kind == "gate_up" and ph.prep == "dequant":
                        group_tile(ph, i, jj, nxt, ni, njj)
                        return
                    if nxt is not None and nxt.prep != "split":
                        tile_product(nxt, ni, njj)
                    if nxt is not None and nxt.prep != "dequant" and not (ph is phases[0] and 2 * i + jj == 0):
                        tile_lo(nxt, ni, njj)
                    if ph.kind == "gate_up":
                        gate_up_tile(ph, i, jj)
                        if ph is phases[0]:
                            j = 2 * i + jj
                            lo_of_b(j + 1)
                            if j == 2:
                                pack_rows()
                            if j == 3:
                                pack_long_factors()
                            if j == 4:
                                pack_short_factors()
                            if j == 5:
                                lo_of_a_dn()
                    else:
                        if ph.name == "cond down b" and 2 * i + jj == 0:
                            small_t(CH, 0.5)
                        if ph.name == "cond1" and 2 * i + jj == 0:
                            small_t(2 * CH, 2.0)
                        down_tile(ph, 2 * i + jj)

                tile_steps(dve, ph, step, in_loop=ph is not phases[0], peeled=1 if ph.prep == "dequant" else 0)
                if ph.kind == "gate_up" and ph.prep == "dequant":
                    unit_product(ph, ph.tiles // 2, 0, CH - 1)

        @block.tensor
        def _(pe):
            def sums(ps, m, s, col, ks, rhs_hi, rhs_lo, rows=lambda k: P, before=lambda k: None, start=True, stop=False):
                last = None
                for n, k in enumerate(ks):
                    before(k)
                    r = rows(k)
                    cols = slice(col + k * P, col + k * P + m)
                    nc.tensor.matmul(ps[0:m, :], w_hi[0:r, s, cols], rhs_hi(k, r), start=start and n == 0, stop=False)
                    nc.tensor.matmul(ps[0:m, :], w_hi[0:r, s, cols], rhs_lo(k, r), start=False, stop=False)
                    last = nc.tensor.matmul(ps[0:m, :], w_lo[0:r, s, cols], rhs_hi(k, r), start=False,
                                            stop=stop and n == len(ks) - 1)
                return last

            def adapters(ps, m, b, g, c):
                nc.tensor.matmul(ps[0:m, :], b, t_hi[:, g, chunk(c)], start=False, stop=False)
                return nc.tensor.matmul(ps[0:m, :], b, t_lo[:, g, chunk(c)], start=False, stop=True)

            def adapter_t(c, a_cols, ks, rhs_hi, rhs_lo, rows=lambda k: P, start=True, stop=True):
                last = None
                for n, k in enumerate(ks):
                    r = rows(k)
                    nc.tensor.matmul(ps_m[:, chunk(c)], a_cols(k)[0:r, :], rhs_hi(k, r), start=start and n == 0, stop=False)
                    last = nc.tensor.matmul(ps_m[:, chunk(c)], a_cols(k)[0:r, :], rhs_lo(k, r), start=False,
                                            stop=stop and n == len(ks) - 1)
                return last

            def scales(ph, i, jj):
                n = ph.m0 + 2 * i + jj
                if not (isinstance(i, int) and n == 0):
                    pe.wait_ge(w_prod, n)
                else:
                    pe.wait_ge(pack_ready, 4)
                last = None
                if ph.kind == "gate_up":
                    for g in range(2):
                        for k in range(HK):
                            q = g * HK + k
                            last = nc.tensor.matmul(ps_m[:, q * P:(q + 1) * P], pack_short[:, g, k * P:(k + 1) * P],
                                                    pack_long[:, ds((ph.first + 2 * i + jj) * P, P)], start=True, stop=True)
                else:
                    o = 2 * i + jj
                    for k in range(k_count(ph)):
                        last = nc.tensor.matmul(ps_m[:, k * P:(k + 1) * P], pack_long[:, (ph.first + k) * P:(ph.first + k + 1) * P],
                                                pack_short[:, 2, o * P:(o + 1) * P], start=True, stop=True)
                last.then_inc(m_ready, 1)

            def net_input(ph):
                return (y_hi, y_lo) if ph.layer == "ffn1" else (h_hi, h_lo)

            def gate_up_tile(ph, i, jj, chunks):
                s, m = slot(ph, jj, i), widths(ph, i, jj)
                hi, lo = net_input(ph)
                pe.wait_ge(w_ready, ph.t0 + 2 * i + jj)
                for c in chunks:
                    n = ph.g0 + CH * (2 * i + jj) + c
                    for g, (ps, read, ready) in enumerate(((ps_gate, silu_done, gate_ready), (ps_up, prod_done, up_ready))):
                        if not isinstance(i, int) or n >= CH:
                            pe.wait_ge(read, n - 1)

                        def input_ready(k, c=c, g=g):
                            if g == 0 and ph.name == "ffn0 gate/up a" and jj == 0 and isinstance(i, int) and i == 0:
                                pe.wait_ge(h_ready, CH * k + c + 1)

                        last = sums(ps[c], m, s, g * HK * P, range(HK), lambda k, r, c=c: hi[0:r, k, chunk(c)],
                                    lambda k, r, c=c: lo[0:r, k, chunk(c)], before=input_ready, stop=ph.layer != "cond")
                        if ph.layer == "cond":
                            last = gate_up_adapters(ps[c], m, ph, 2 * i + jj, g, c)
                        last.then_inc(ready, 1)

            def gate_up_adapters(ps, m, ph, j, g, c):
                pe.wait_ge(t_lo_done, c + 1)
                pe.wait_ge(b_ready, CH * ((ph.first + j) // 2 + 1))
                b0 = b_col(ph, j, g)
                return adapters(ps, m, b_split[:, c, b0:b0 + m], g, c)

            def unit_base(ph, j, c):
                s = slot(ph, j, 0)
                for g, ps in enumerate(unit_banks(ph, 0, j, c)):
                    def input_ready(k, c=c, g=g):
                        if j == 0:
                            pe.wait_ge(start_lo, max(started("w", g), started("x", c, k)))
                    sums(ps, P, s, g * HK * P, range(HK), lambda k, r, c=c: h_hi[:, k, chunk(c)],
                         lambda k, r, c=c: h_lo[:, k, chunk(c)], before=input_ready)

            def first_tiles(ph):
                for c in range(CH):
                    unit_base(ph, 0, c)
                for c in range(CH):
                    pe.wait_ge(a_gu_ready, 2 * (c + 1))
                    for k in range(HK):
                        a_h, a_l = (a[:, k, c].rearrange("p g b r -> p (g b r)") for a in (a_gu_hi, a_gu_lo))
                        for n, (a, x) in enumerate(((a_h, h_hi), (a_h, h_lo), (a_l, h_hi))):
                            last = nc.tensor.matmul(ps_m[:, chunk(c)], a, x[:, k, chunk(c)], start=k == 0 and n == 0,
                                                    stop=k == HK - 1 and n == 2)
                    last.then_inc(t_sums, 1)
                pe.wait_ge(w_ready, 1)
                unit_base(ph, 1, 0)
                for j, c in ((0, 0), (0, 1), (1, 0)):
                    unit_adapters(ph, j, c)

            def unit_adapters(ph, j, c):
                for g, (ps, ready) in enumerate(zip(unit_banks(ph, 0, j, c), (gate_ready, up_ready))):
                    gate_up_adapters(ps, P, ph, j, g, c).then_inc(ready, 1)

            def group(ps, s, col, hi, lo):
                nc.tensor.matmul(ps, w_hi[:, s, col:col + P], hi, start=True, stop=False)
                nc.tensor.matmul(ps, w_hi[:, s, col:col + P], lo, start=False, stop=True).then_inc(group_ready, 1)

            def group_tile(ph, i, jj):
                s = slot(ph, jj, i)
                first = isinstance(i, int) and 2 * i + jj == 0
                pe.wait_ge(w_ready, ph.t0 + 2 * i + jj)
                for c in range(CH):
                    u = CH * (2 * i + jj) + c
                    for k in range(HK):
                        if first and ph.part == 0:
                            pe.wait_ge(h_ready, 2 * CH * HK + CH * k + c + 1)
                        if first and c == 0:
                            if ph.part:
                                pe.wait_ge(group_added, last_down_use(ph, k))
                        elif k == 0:
                            pe.wait_ge(first_scaled, ph.f0 + u)
                        else:
                            pe.wait_ge(group_added, ph.a0 + (HK - 1) * (u - 1) + k)
                        group(group_banks[k], s, k * P, y_hi[:, k, chunk(c)], y_lo[:, k, chunk(c)])
                    if not first:
                        pe.wait_ge(up_scaled, ph.f0 + u - 1)
                        pe.wait_ge(up_added, ph.f0 + u - 1)
                    else:
                        pe.wait_ge(sum_done, ph.d0 - 1 + c)
                        if ph.part:
                            pe.wait_ge(group_added, last_down_use(ph, HK + c))
                    group(ps_down[c][:, :], s, HK * P, y_hi[:, 0, chunk(c)], y_lo[:, 0, chunk(c)])
                    sums(ps_up[c], P, s, HK * P, range(UQ, HK), lambda k, r, c=c: y_hi[:, k, chunk(c)],
                         lambda k, r, c=c: y_lo[:, k, chunk(c)], stop=True).then_inc(up_ready, 1)

            def last_down_use(ph, bank):
                groups = KQ * CH * HK
                return ph.a0 - groups + max(n for n in range(groups) if n % len(group_banks) == bank) + 1

            def down_groups(ph, o):
                s = slot(ph, o, 0)
                g0 = ph.g0 - CH * ACT_TILES
                for n in range(KQ):
                    for c in range(CH):
                        k, m = DQ // P + n, down_group(o, n, c)
                        if m >= len(group_banks):
                            pe.wait_ge(group_added, ph.a0 + m - len(group_banks) + 1)
                        else:
                            pe.wait_ge(first_scaled, ph.f0)
                            pe.wait_ge(group_added, ph.a0)
                            pe.wait_ge(up_added, ph.f0)
                        if o == 0:
                            pe.wait_ge(act_ready, g0 + CH * k + c + 1)
                        group(group_banks[m % len(group_banks)], s, k * P, act_hi[:, k, chunk(c)], act_lo[:, k, chunk(c)])

            def down_base(ph, o, c):
                n, s = ph.d0 + CH * o + c, slot(ph, o, 0)
                if c == 0:
                    pe.wait_ge(w_ready, ph.t0 + o)
                if ph.prep == "dequant" and o == 0:
                    pe.wait_ge(up_scaled, ph.f0 - 1 + c)
                elif n >= 2:
                    pe.wait_ge(sum_done, n - 1)
                g0 = ph.g0 - CH * k_count(ph)
                ks = range(DQ // P if ph.prep == "dequant" else k_count(ph))

                def input_ready(k):
                    if o > 0:
                        return
                    if ph.layer == "cond1":
                        pe.wait_ge(h_ready, CH * HK + CH * k + c + 1)
                    else:
                        pe.wait_ge(act_ready, g0 + CH * k + c + 1)

                hi, lo = (h_hi, h_lo) if ph.layer == "cond1" else (act_hi, act_lo)
                return sums(ps_down[c], P, s, 0, ks, lambda k, r: hi[0:r, k, chunk(c)],
                            lambda k, r: lo[0:r, k, chunk(c)], rows=lambda k: k_rows(ph, k), before=input_ready,
                            stop=not has_adapters(ph))

            def has_adapters(ph):
                return ph.name in ("cond down b", "cond1")

            def down_adapters(ph, o, c):
                if ph.name == "cond1":
                    pe.wait_ge(b1_ready, 1)
                    pe.wait_ge(t_lo_done, 2 * CH + c + 1)
                    return adapters(ps_down[c], P, b1_split[:, c, o * P:(o + 1) * P], 0, c)
                pe.wait_ge(t_lo_done, CH + c + 1)
                return adapters(ps_down[c], P, b_split[:, c, 2 * F0 + o * P:2 * F0 + (o + 1) * P], 0, c)

            def t_down(ph, c):
                ks = range(k_count(ph))
                pe.wait_ge(a_dn_ready, 4)
                pe.wait_ge(act_ready, ph.g0 - CH + c + 1)
                last = adapter_t(c, lambda k: a_dn[:, ph.first + k, c, :], ks, lambda k, r: act_hi[0:r, k, chunk(c)],
                                 lambda k, r: act_lo[0:r, k, chunk(c)], rows=lambda k: k_rows(ph, k), start=ph.part == 0, stop=ph.part == 1)
                if ph.part == 1:
                    last.then_inc(t_sums, 1)

            for ph in phases:
                if ph.name == "cond1":
                    pe.wait_ge(a1_ready, CH)
                    for c in range(CH):
                        pe.wait_ge(h_ready, 2 * CH * HK - CH + c + 1)
                        adapter_t(c, lambda k, c=c: a1[:, k, c, :], range(HK), lambda k, r, c=c: h_hi[:, k, chunk(c)],
                                  lambda k, r, c=c: h_lo[:, k, chunk(c)]).then_inc(t_sums, 1)

                def step(i, jj, nxt, ni, njj, ph=ph):
                    if nxt is not None and nxt.prep == "scale":
                        scales(nxt, ni, njj)
                    if ph.kind == "gate_up" and ph.prep == "dequant":
                        group_tile(ph, i, jj)
                        return
                    if ph is phases[0] and 2 * i + jj == 0:
                        first_tiles(ph)
                        return
                    if ph.kind == "gate_up":
                        begun = ph is phases[0] and isinstance(i, int) and 2 * i + jj == 1
                        gate_up_tile(ph, i, jj, chunks=range(1 if begun else 0, CH))
                        return
                    o = 2 * i + jj
                    if ph.prep == "dequant":
                        for c in range(CH):
                            down_base(ph, o, c).then_inc(down_ready, 1)
                        down_groups(ph, o)
                        return
                    if not has_adapters(ph):
                        for c in range(CH):
                            down_base(ph, o, c).then_inc(down_ready, 1)
                    elif o == 0:
                        down_base(ph, o, 0)
                        if ph.name == "cond down b":
                            for c in range(CH):
                                t_down(ph, c)
                        down_base(ph, o, 1)
                        for c in range(CH):
                            down_adapters(ph, o, c).then_inc(down_ready, 1)
                    else:
                        for c in range(CH):
                            down_base(ph, o, c)
                            down_adapters(ph, o, c).then_inc(down_ready, 1)

                tile_steps(pe, ph, step, in_loop=ph.layer != "cond", peeled=0 if ph.name == "ffn0 gate/up b" else 1)
                if ph.name == "cond down a":
                    for c in range(CH):
                        t_down(ph, c)


def _lay_out(i):
    import numpy as np

    def tiles(w, k, f):
        o, n = w.shape
        return w.T.reshape(n // P, P, o // f, f).transpose(2, 1, 0, 3)

    def gate_up(g, u, f=P):
        return np.concatenate([tiles(g, HK, f), tiles(u, HK, f)], axis=2).reshape(-1, P, 2 * HK * f)

    def down(w, parts):
        return np.stack([tiles(w[:, a:b], 0, P).reshape(HK, P, -1) for a, b in parts])

    full = F0 // P * P
    cut = 6 * P
    half = F1 // 2
    cg, cu, cd = i["L0_cond_W_gate"], i["L0_cond_W_up"], i["L0_cond_W_down"]
    a = np.stack([i["L0_cond_A_gate"][0], i["L0_cond_A_up"][0]], axis=1)
    n_id = a.shape[0]
    a_dn = i["L0_cond_A_down"][0].transpose(0, 2, 1)
    bg, bu = i["L0_cond_B_gate"][0], i["L0_cond_B_up"][0]
    b0 = np.concatenate([b[:, f:f + P] for f in range(0, F0, P) for b in (bg, bu)] + [i["L0_cond_B_down"][0]], axis=1)
    factors = np.stack([
        np.concatenate([i["L0_ffn_gate_su"].T, i["L0_ffn_gate_sv"]], axis=1),
        np.concatenate([i["L0_ffn_up_su"].T, i["L0_ffn_up_sv"]], axis=1),
        np.concatenate([i["L0_ffn_down_sv"], i["L0_ffn_down_su"].T], axis=1)])
    s_up = i["L1_ffn_up_s"].reshape(F1 // P, P, HK).transpose(0, 2, 1)[:, UQ:]
    s_dn = i["L1_ffn_down_s"].reshape(HK, P, 2, ACT_TILES).transpose(2, 0, 3, 1)[:, :, :DQ // P]
    s_group = np.concatenate([i["L1_ffn_gate_s"], i["L1_ffn_up_s"][:, :UQ]], axis=1)
    a1 = i["L1_cond_lora_As"]
    arrays = {
        "x": i["x"].reshape(TOK, H).T.reshape(HK, P, TOK),
        "ids0": i["itok_B_2_6"].reshape(1, NB),
        "ids1": i["itok_B_0_23"].reshape(1, NB),
        "cond_gu": gate_up(cg[:full], cu[:full]),
        "cond_gu_tail": gate_up(cg[full:], cu[full:], F0_TAIL)[0],
        "cond_dn_a": down(cd, [(0, cut)])[0],
        "cond_dn_b": down(cd, [(cut, full)])[0],
        "cond_dn_tail": cd[:, full:].T.reshape(F0_TAIL, HK, P).transpose(1, 0, 2),
        "a_gu": a.reshape(n_id, 2, R, HK, P).transpose(0, 4, 3, 1, 2).reshape(n_id, P, 2 * HK * R),
        "a_dn": a_dn[:, :full].reshape(n_id, full // P, P, R).transpose(0, 2, 1, 3).reshape(n_id, P, -1),
        "a_dn_tail": a_dn[:, full:],
        "b0": b0.transpose(0, 2, 1),
        "factors": factors,
        "ffn0_gu": gate_up(i["L0_ffn_gate_w"], i["L0_ffn_up_w"]),
        "ffn0_dn": down(i["L0_ffn_down_w"], [(0, half), (half, F1)]),
        "cond1_w": tiles(i["L1_cond_W"], HK, P).reshape(HK, P, H),
        "cond1_b": i["L1_cond_b"].reshape(HK, P).T,
        "a1": a1.reshape(-1, HK, P, R).transpose(0, 2, 1, 3).reshape(-1, P, HK * R),
        "b1": i["L1_cond_lora_Bs"],
        "ffn1_gu": gate_up(i["L1_ffn_gate_q"], i["L1_ffn_up_q"]),
        "ffn1_dn": down(i["L1_ffn_down_q"], [(0, half), (half, F1)]),
        "ffn1_up_s": s_up.reshape(F1 // P, DQ),
        "ffn1_dn_s": s_dn.reshape(2, HK, DQ),
        "ffn1_group_s": s_group.reshape(F1 // P, P, GQ),
        "ffn1_down_s": i["L1_ffn_down_s"].reshape(HK, P, F1 // P).transpose(1, 0, 2).reshape(P, -1),
    }
    return {k: np.ascontiguousarray(v) for k, v in arrays.items()}


def kernel(**inputs):
    import numpy as np
    import concourse.bacc as bacc
    from concourse.bass_utils import run_bass_kernel_spmd

    arrays = _lay_out({k: np.asarray(v) for k, v in inputs.items()})
    nc = bacc.Bacc("TRN2", target_bir_lowering=False, num_devices=1)
    d = {k: nc.dram_tensor(f"in_{k}", v.shape, mybir.dt.from_np(v.dtype), kind="ExternalInput").ap() for k, v in arrays.items()}
    out = nc.dram_tensor("out_t", (HK, P, TOK), F32, kind="ExternalOutput").ap()
    adaln_ffn(nc, d, out)
    r = run_bass_kernel_spmd(nc, [{f"in_{k}": v for k, v in arrays.items()}], core_ids=[0])
    got = r.results[0]["out_t"]
    return np.ascontiguousarray(got.reshape(H, TOK).T.reshape(NB, TOK // NB, H))
```

```python
from collections import namedtuple
from contextlib import ExitStack

import concourse.bass as bass
from concourse import mybir

F32 = mybir.dt.float32
F32R = mybir.dt.float32r
I32 = mybir.dt.int32
ALU = mybir.AluOpType
ACT = mybir.ActivationFunctionType

P = 128
H = 512
HK = H // P
TOK = 1024
CT = 512
CH = TOK // CT
NB = 8
BC = NB // CH
R = 16
RB = BC * R
F0 = 1376
F1 = 1792
F0_TAIL = F0 - F0 // P * P
NKD = (F0 + P - 1) // P
SR = 4
WT = 1024
ACT_TILES = 7
UQ = 2
KQ = 5
DQ_UP = (HK - UQ) * P
DQ_DOWN = (ACT_TILES - KQ) * P
GQ = HK + UQ
assert UQ == CH
PACK = F1 + H
CUT = 6
BA = CUT * 2 * P
BB = 2 * F0 + H - BA
BP = 2 * P
NBP = NKD + H // BP
PAIRS = NB // 2
PT = TOK // PAIRS
PR = 2 * R
assert 4 * PR == P
WARM = 12

Phase = namedtuple("Phase", "name kind layer part tiles first t0 g0 d0 m0 q0 a0 f0 raw0 loads prep")


def plan_phases():
    steps = [
        ("cond gate/up a", "gate_up", "cond", 0, CUT, 0, 1, "split"),
        ("cond down a", "down", "cond", 0, HK, 0, 1, "split"),
        ("cond gate/up b", "gate_up", "cond", 1, NKD - CUT, CUT, 1, "split"),
        ("cond down b", "down", "cond", 1, HK, CUT, 2, "split"),
        ("ffn0 gate/up a", "gate_up", "ffn0", 0, 7, 0, 1, "scale"),
        ("ffn0 down a", "down", "ffn0", 0, HK, 0, 1, "scale"),
        ("ffn0 gate/up b", "gate_up", "ffn0", 1, 7, 7, 1, "scale"),
        ("ffn0 down b", "down", "ffn0", 1, HK, 7, 1, "scale"),
        ("cond1", "down", "cond1", 0, HK, 0, 1, "split"),
        ("ffn1 gate/up a", "gate_up", "ffn1", 0, 7, 0, 3, "dequant"),
        ("ffn1 down a", "down", "ffn1", 0, HK, 0, 2, "dequant"),
        ("ffn1 gate/up b", "gate_up", "ffn1", 1, 7, 7, 3, "dequant"),
        ("ffn1 down b", "down", "ffn1", 1, HK, 7, 2, "dequant"),
    ]
    t0, g0, d0, m0, q0, a0, f0, raw0 = 0, 0, 0, 0, 0, 0, 0, [-16, 0]
    phases = []
    for name, kind, layer, part, tiles, first, loads, prep in steps:
        phases.append(Phase(name, kind, layer, part, tiles, first, t0, g0, d0, m0, q0, a0, f0, tuple(raw0), loads, prep))
        for j in range(tiles):
            raw0[(t0 + j) % 2] += 16 * loads
        t0 += tiles
        if kind == "gate_up":
            g0 += CH * tiles
        else:
            d0 += CH * tiles
        if prep == "scale":
            m0 += tiles
        if prep == "dequant" and kind == "gate_up":
            q0 += CH * tiles * GQ
            a0 += CH * tiles * (HK - 1)
            f0 += CH * tiles
        if prep == "dequant" and kind == "down":
            q0 += CH * tiles * KQ
            a0 += CH * tiles * (KQ - 1)
    return phases


def adaln_ffn(nc, d, out):
    phases = plan_phases()
    following = dict(zip(phases, phases[1:]))
    gate_up_before = dict(zip(phases[1:], phases))
    named = {ph.name: ph for ph in phases}
    with ExitStack() as ctx:
        at = {}

        def place(name, shape, dt, offset):
            return nc.alloc_sbuf_tensor_at(name, shape, dt, offset=offset)

        def region(name, size):
            at[name] = at["top"]
            at["top"] += size

        def sem(name):
            return ctx.enter_context(nc.semaphore(name))

        KB = 1024
        at["top"] = (nc.sbuf_base + 63) // 64 * 64
        for name, size in (("h", 32 * KB), ("xp", 16 * KB), ("act_hi", ACT_TILES * 4 * KB), ("act_lo", ACT_TILES * 4 * KB),
                           ("w", 24 * KB), ("gated", 4 * KB), ("lora0", 11 * KB + BB * PAIRS * 4),
                           ("t", 8 * KB), ("t_hi", 4 * KB), ("mask", 2 * KB), ("pack", 4 * (F1 + 3 * H)), ("lora_b1", 8 * KB), ("small", 704)):
            region(name, size)

        h_hi = place("h_hi", [P, HK, TOK], F32R, at["h"])
        h_lo = place("h_lo", [P, HK, TOK], F32R, at["h"] + 16 * KB)
        xp = place("xp", [P, HK, TOK], F32, at["xp"])
        act_hi = place("act_hi", [P, ACT_TILES, TOK], F32R, at["act_hi"])
        act_lo = place("act_lo", [P, ACT_TILES, TOK], F32R, at["act_lo"])
        w_hi = place("w_hi", [P, 2, WT], F32R, at["w"])
        w_lo = place("w_lo", [P, 2, WT], F32R, at["w"] + 8 * KB)
        w_raw = place("w_raw", [P, 2, WT], F32, at["w"] + 16 * KB)
        gated = place("gated", [P, CH, CT], F32, at["gated"])
        warm = place("warm", [P, CT], F32R, at["gated"])
        a_dn = place("a_dn", [P, NKD, CH, 2 * RB], F32R, at["lora0"])
        b_rows = place("b_rows", [P, PAIRS, BB], F32R, at["lora0"] + 11 * KB)
        b_raw = place("b_raw", [P, PAIRS, BB], F32, at["lora0"] + 11 * KB)
        y_hi = place("y_hi", [P, HK, TOK], F32R, at["lora0"])
        y_lo = place("y_lo", [P, HK, TOK], F32R, at["lora0"] + 16 * KB)
        a1 = place("a1", [P, HK, CH, 2 * RB], F32R, at["lora0"] + 32 * KB)
        a1_raw = place("a1_raw", [P, NB, HK * R], F32, at["lora0"])
        b1_hi = place("b1_hi", [P, PAIRS, H], F32R, at["lora0"] + 4 * KB)
        b1_rows = place("b1_rows", [P, PAIRS, H], F32R, at["lora_b1"])
        b1_raw = place("b1_raw", [P, PAIRS, H], F32, at["lora_b1"])
        t_hi = place("t_hi", [P, CH, CT], F32R, at["t_hi"])
        t_rows = place("t_rows", [P, 2, TOK], F32R, at["t"])
        s_bc = [place(f"s_bc{i}", [P, max(DQ_UP, DQ_DOWN)], F32, at["t"] + 4 * KB + 2 * KB * i) for i in range(2)]
        gate_sum = place("gate_sum", [P, 2, CH, CT], F32, at["h"])
        up_sum = place("up_sum", [P, 2, CH, CT], F32, at["h"] + 8 * KB)
        up_more = place("up_more", [P, 2, CH, CT], F32, at["h"] + 24 * KB)
        down_sum = place("down_sum", [P, 2, CH, CT], F32, at["h"] + 16 * KB)
        down_more = place("down_more", [P, 2, CH, CT], F32, at["lora_b1"])
        seg_mask = place("seg_mask", [P, CT], F32, at["mask"])
        pack_long = place("pack_long", [P, F1], F32R, at["pack"])
        pack_short = place("pack_short", [P, 3, H], F32R, at["pack"] + 4 * F1)
        a_dn_raw = place("a_dn_raw", [P, NB, NKD * R], F32, at["xp"])
        pack_raw = place("pack_raw", [P, PACK], F32, at["xp"] + 4 * NB * NKD * R)
        a_gu_raw = place("a_gu_raw", [P, NB, HK * 2 * R], F32, at["act_hi"] + 20 * KB)
        a_gu_hi = place("a_gu_hi", [P, HK, CH, 2, BC, R], F32R, at["act_lo"] + 16 * KB)
        a_gu_lo = place("a_gu_lo", [P, HK, CH, 2, BC, R], F32R, at["act_lo"] + 20 * KB)
        b_hi = place("b_hi", [P, 2, PAIRS, BP], F32R, at["lora_b1"])
        short_hi = place("short_hi", [P, H], F32R, at["act_lo"] + 24 * KB)
        short_part = place("short_part", [P, H], F32, at["act_lo"] + 26 * KB)
        small = at["small"]
        ids0 = place("ids0", [1, NB], I32, small)
        ids1 = place("ids1", [1, NB], I32, small + 32)
        bias = place("bias", [P, HK], F32, small + 64)
        row_id = place("row_id", [P, 4], I32, small + 96)
        sel = place("sel", [P, 12], F32, small + 128)
        s_group_in = place("s_group_in", [P, 2, GQ], F32, small + 192)
        s_group = place("s_group", [P, 2, GQ], F32, small + 256)
        s_down = place("s_down", [P, HK * (F1 // P)], F32, small + 320)
        assert small + 704 <= nc.sbuf_usable_end

        ps_gate = [ctx.enter_context(nc.psum_tensor(f"ps_gate{c}", [P, CT], F32)) for c in range(CH)]
        ps_up = [ctx.enter_context(nc.psum_tensor(f"ps_up{c}", [P, CT], F32)) for c in range(CH)]
        ps_down = [ctx.enter_context(nc.psum_tensor(f"ps_down{c}", [P, CT], F32)) for c in range(CH)]
        ps_m = ctx.enter_context(nc.psum_tensor("ps_m", [P, WT], F32))
        group_banks = [ps_gate[0][:, :], ps_gate[1][:, :], ps_m[:, 0:CT], ps_m[:, CT:WT], ps_up[0][:, :], ps_up[1][:, :]]

        raw_in = [sem(f"raw_in{s}") for s in range(2)]
        warm_zero = sem("warm_zero")
        w_first_in = [sem(f"w_first_in{g}") for g in range(2)]
        x_in = [[sem(f"x_in{c}{k}") for k in range(HK)] for c in range(CH)]
        start_hi, start_lo = sem("start_hi"), sem("start_lo")
        x_again = sem("x_again")
        ids_in = [sem(f"ids_in{layer}") for layer in range(2)]
        bias_in, s_in = sem("bias_in"), sem("s_in")
        a_gu_in, b_in = ([sem(f"{n}{c}") for c in range(CH)] for n in ("a_gu_in", "b_in"))
        a_dn_in, b_again_in = sem("a_dn_in"), sem("b_again_in")
        a1_in, b1_in = sem("a1_in"), sem("b1_in")
        pack_zero, pack_in = sem("pack_zero"), sem("pack_in")
        mask_step, mask_ready = sem("mask_step"), sem("mask_ready")
        rows_ready = sem("rows_ready")
        sel_step = sem("sel_step")
        a_gu_hi_done, a_gu_ready = sem("a_gu_hi_done"), sem("a_gu_ready")
        a_dn_hi_done, a_dn_ready = sem("a_dn_hi_done"), sem("a_dn_ready")
        b_hi_done, b_step, b_ready = sem("b_hi_done"), sem("b_step"), sem("b_ready")
        a1_hi_done, a1_ready = sem("a1_hi_done"), sem("a1_ready")
        b1_hi_done, b1_step, b1_ready = sem("b1_hi_done"), sem("b1_step"), sem("b1_ready")
        pack_hi_done, pack_step, pack_ready = sem("pack_hi_done"), sem("pack_step"), sem("pack_ready")
        m_ready = sem("m_ready")
        w_prod = sem("w_prod")
        w_hi_done, w_ready = sem("w_hi_done"), sem("w_ready")
        gate_ready, up_ready = sem("gate_ready"), sem("up_ready")
        silu_done, prod_done = sem("silu_done"), sem("prod_done")
        act_hi_done, act_ready = sem("act_hi_done"), sem("act_ready")
        down_ready = sem("down_ready")
        base_done = sem("base_done")
        group_ready = sem("group_ready")
        first_scaled = sem("first_scaled")
        group_added = sem("group_added")
        up_scaled, up_added = sem("up_scaled"), sem("up_added")
        up_joined = sem("up_joined")
        down_scaled = sem("down_scaled")
        more_added = sem("more_added")
        sum_done = sem("sum_done")
        stream_done = sem("stream_done")
        h_hi_done, h_ready = sem("h_hi_done"), sem("h_ready")
        t_sums, t_lo_rows, t_masked = sem("t_sums"), sem("t_lo_rows"), sem("t_masked")
        t_added, t_hi_done = sem("t_added"), sem("t_hi_done")
        t_hi_rows, t_lo_rows_done = sem("t_hi_rows"), sem("t_lo_rows_done")
        out_done = sem("out_done")

        def chunk(c):
            return slice(c * CT, (c + 1) * CT)

        def ds(start, size):
            return bass.ds(start, size)

        def widths(ph, i, jj):
            if ph.layer == "cond" and ph.part == 1 and isinstance(i, int) and 2 * i + jj == ph.tiles - 1:
                return F0_TAIL
            return P

        def k_rows(ph, k):
            return F0_TAIL if ph.name == "cond down b" and k == k_count(ph) - 1 else P

        def k_count(ph):
            return {"cond": (CUT, NKD - CUT)[ph.part], "cond1": HK}.get(ph.layer, ACT_TILES)

        def columns(ph):
            return WT if ph.kind == "gate_up" else k_count(ph) * P

        def slot(ph, jj, i):
            return (ph.t0 + jj) % 2

        def raw_count(ph, i, jj):
            return ph.raw0[slot(ph, jj, i)] + 16 * ph.loads * (i + jj // 2 + 1)

        def b_piece(ph, j):
            return ph.first + j

        def piece_cols(p):
            start = (p if p < CUT else p - CUT) * BP
            if p >= NKD:
                start -= 2 * (P - F0_TAIL)
            return slice(start, start + (2 * F0_TAIL if p == NKD - 1 else BP))

        def next_piece(ph, j):
            p = {"cond gate/up a": j + 2, "cond down a": CUT + j - 1, "cond gate/up b": CUT + j + 3}[ph.name]
            first, last = (3, CUT) if ph.name == "cond gate/up a" else (CUT, NBP)
            return p if first <= p < last else None

        def pair_tokens(pair):
            return slice(pair * PT, (pair + 1) * PT)

        def quarter(n):
            return slice(n * PR, (n + 1) * PR)

        def unit_banks(ph, i, jj, c):
            if ph is phases[0] and isinstance(i, int) and 2 * i + jj == 1:
                return [ps[:, :] for ps in ps_down] if c == 0 else [ps_m[:, chunk(g)] for g in range(2)]
            return ps_gate[c], ps_up[c]

        def base_before(ph):
            return {"cond down b": CH, "cond1": CH + CH * HK}[ph.name]

        def ends_with_sums(ph, o):
            return ph is phases[-1] and o == HK - 1

        def down_group(o, k, c):
            return CH * (KQ * o + k) + c

        def down_group_bank(m):
            return (m - KQ * CH * HK) % len(group_banks)

        def groups_added(ph, o, k, c):
            return CH * ((KQ - 1) * o + k - (not ends_with_sums(ph, o))) + c + 1

        def group_read(ph, m):
            o, k, c = m // (CH * KQ), m // CH % KQ, m % CH
            if k == 0 and not ends_with_sums(ph, o):
                return down_scaled, CH * (HK * ph.part + o) + c + 1
            return group_added, ph.a0 + groups_added(ph, o, k, c)

        def group_scale(ph, o, k):
            col = o * (F1 // P) + ph.first + DQ_DOWN // P + k
            return s_down[:, col:col + 1]

        def has_adapters(ph):
            return ph.name in ("cond down b", "cond1")

        def small_t_of(ph):
            return {"cond down b": (CH, 0.5), "cond1": (2 * CH, 2.0)}[ph.name]

        def down_bank(ph, o, c):
            return ps_up[c] if has_adapters(ph) and o % 2 else ps_down[c]

        def q_cols(ph):
            return slice(0, WT - DQ_UP) if ph.kind == "gate_up" else slice(DQ_DOWN, DQ_DOWN + KQ * P)

        def dq_cols(ph):
            return slice(WT - DQ_UP, WT) if ph.kind == "gate_up" else slice(0, DQ_DOWN)

        start = [("w", 0)] + [("x", 0, k) for k in range(HK)] + [("w", 1)] + [("x", 1, k) for k in range(HK)]

        def started(*item):
            return start.index(item) + 1

        def tile_steps(eng, ph, step, in_loop=True, peeled=0):
            if ph.kind == "down":
                peeled, in_loop = 0, False
            looped = (ph.tiles - 1) // 2 if in_loop else peeled
            for j in range(2 * peeled):
                step(j // 2, j % 2, ph, (j + 1) // 2, (j + 1) % 2)
            if looped > peeled:
                with eng.Fori(peeled, looped) as i:
                    for jj in range(2):
                        step(i, jj, ph, i, jj + 1)
            for j in range(2 * looped, ph.tiles):
                if j + 1 < ph.tiles:
                    step(j // 2, j % 2, ph, j // 2, j % 2 + 1)
                else:
                    step(j // 2, j % 2, following.get(ph), 0, 0)

        def w_prod_count(ph, i, jj):
            scaled = sum(p.tiles for p in phases if p.prep == "scale")
            if ph.prep == "scale":
                return ph.m0 + 2 * i + jj + 1
            return scaled + ph.t0 - named["ffn1 gate/up a"].t0 + 2 * i + jj + 1

        def h_seen(ph):
            return {"ffn0 down b": CH * HK, "cond1": 2 * CH * HK}.get(ph.name, 0)

        def ready_together(ph, i, jj):
            return ph is phases[0] and 2 * i + jj < 2

        def first_phase_weights(prepare, j, slot_free=lambda count: None):
            first = phases[0]
            if j == 1:
                slot_free(CH * 2)
                prepare(first, 1, 1)
            elif j > 2:
                slot_free(CH * j)
                prepare(*((first, (j + 1) // 2, (j + 1) % 2) if j + 1 < first.tiles else (following[first], 0, 0)))

        def load_a_gu(eng, b):
            e = eng.value_load(ids0[0:1, b:b + 1], min_val=0, max_val=d["a_gu"].shape[0] - 1)
            eng.dma_start(a_gu_raw[:, b, :], d["a_gu"][ds(e, 1)].rearrange("a p n -> (a p) n")).then_inc(a_gu_in[b // BC], 16)

        def load_b(eng, b, part, done):
            e = eng.value_load(ids0[0:1, b:b + 1], min_val=0, max_val=d["b0"].shape[0] - 1)
            row = 3 * PR + b % 2 * R
            n, start = (BA, 0) if part == 0 else (BB, BA)
            eng.dma_start(b_raw[row:row + R, b // 2, 0:n],
                          d["b0"][ds(e, 1)].rearrange("a r n -> (a r) n")[:, start:start + n]).then_inc(done, 16)

        block = ctx.enter_context(nc.Block())

        @block.sync
        def _(sp):
            def load_tile(ph, i, jj):
                s = slot(ph, jj, i)
                if not isinstance(i, int) or ph.t0 + 2 * i + jj > 2:
                    sp.wait_ge(w_ready, ph.t0 + 2 * i + jj - 2)
                elif ph.t0 + 2 * i + jj == 2:
                    sp.wait_ge(start_lo, started("w", 1))
                n = columns(ph)
                if ph.kind == "gate_up":
                    f = ph.first + 2 * i + jj
                    if widths(ph, i, jj) == F0_TAIL:
                        sp.dma_start(w_raw[:, s, :].rearrange("p (g f) -> p g f", f=P)[:, :, 0:F0_TAIL],
                                     d["cond_gu_tail"].rearrange("p (g f) -> p g f", f=F0_TAIL)).then_inc(raw_in[s], 16)
                        return
                    src = {"cond": d["cond_gu"], "ffn0": d["ffn0_gu"], "ffn1": d["ffn1_gu"]}[ph.layer]
                    dst = w_raw[:, s, :]
                    if ph.prep == "dequant":
                        dst = dst.bitcast(I32)
                    sp.dma_start(dst, src[ds(f, 1)].rearrange("a p n -> (a p) n")).then_inc(raw_in[s], 16)
                    if ph.prep == "dequant":
                        sp.dma_start(s_group_in[:, s, :], d["ffn1_group_s"][ds(f, 1)].rearrange("a p n -> (a p) n")).then_inc(raw_in[s], 16)
                        sp.dma_start(s_bc[s][:, 0:DQ_UP], d["ffn1_up_s"][ds(f, 1), :].partition_broadcast(P)).then_inc(raw_in[s], 16)
                    return
                o = 2 * i + jj
                if ph.layer == "cond":
                    src = d[("cond_dn_a", "cond_dn_b")[ph.part]]
                    main = src.shape[2]
                    sp.dma_start(w_raw[:, s, 0:main], src[o]).then_inc(raw_in[s], 16)
                    if ph.part:
                        sp.dma_start(w_raw[0:F0_TAIL, s, main:n], d["cond_dn_tail"][o]).then_inc(raw_in[s], 16)
                elif ph.layer == "cond1":
                    sp.dma_start(w_raw[:, s, 0:n], d["cond1_w"][o]).then_inc(raw_in[s], 16)
                elif ph.layer == "ffn0":
                    sp.dma_start(w_raw[:, s, 0:n], d["ffn0_dn"][ph.part, o]).then_inc(raw_in[s], 16)
                else:
                    sp.dma_start(w_raw[:, s, 0:n].bitcast(I32), d["ffn1_dn"][ph.part, o]).then_inc(raw_in[s], 16)
                    sp.dma_start(s_bc[s][:, 0:DQ_DOWN], d["ffn1_dn_s"][ph.part, o:o + 1, :].partition_broadcast(P)).then_inc(raw_in[s], 16)

            for n, item in enumerate(start):
                if n == 2:
                    sp.dma_start(ids0[:, :], d["ids0"]).then_inc(ids_in[0], 16)
                if item[0] == "w":
                    half = slice(item[1] * HK * P, (item[1] + 1) * HK * P)
                    sp.dma_start(w_raw[:, 0, half], d["cond_gu"][0][:, half]).then_inc(w_first_in[item[1]], 16)
                else:
                    _, c, k = item
                    sp.dma_start(xp[:, k, chunk(c)], d["x"][k][:, chunk(c)]).then_inc(x_in[c][k], 16)
            sp.wait_ge(ids_in[0], 16)
            for b in range(BC, NB):
                load_a_gu(sp, b)
            load_tile(phases[0], 0, 1)
            for b in range(BC, NB):
                load_b(sp, b, 0, b_in[b // BC])
            sp.dma_start(ids1[:, :], d["ids1"]).then_inc(ids_in[1], 16)
            for ph in phases:
                if ph.name == "cond1":
                    sp.dma_start(bias[:, :], d["cond1_b"]).then_inc(bias_in, 16)
                    sp.dma_start(s_down[:, :], d["ffn1_down_s"]).then_inc(s_in, 16)
                if ph.name == "ffn0 down a":
                    sp.wait_ge(h_ready, CH * HK)
                    sp.dma_start(xp[:, :, :], d["x"].rearrange("k p n -> p k n")).then_inc(x_again, 16)
                unloaded = 0
                if ph is phases[0]:
                    for j in range(2, 4):
                        load_tile(ph, j // 2, j % 2)
                    unloaded = 2
                pairs = ph.tiles // 2
                if ph.kind == "gate_up":
                    with sp.Fori(unloaded, pairs) as i:
                        load_tile(ph, i, 0)
                        load_tile(ph, i, 1)
                    if ph.tiles % 2:
                        load_tile(ph, pairs, 0)
                else:
                    for o in range(ph.tiles):
                        load_tile(ph, o // 2, o % 2)
            last = phases[-1]
            for o in range(HK):
                for c in range(CH):
                    if not ends_with_sums(last, o):
                        sp.wait_ge(stream_done, CH * (HK + o) + c + 1)
                    else:
                        sp.wait_ge(sum_done, last.d0 + CH * o + c + 1)
                    sp.dma_start(out[o][:, chunk(c)], xp[:, o, chunk(c)]).then_inc(out_done, 16)
            sp.wait_ge(out_done, 16 * CH * HK)

        @block.gpsimd
        def _(pool):
            pool.wait_ge(ids_in[0], 16)
            for b in range(BC):
                load_a_gu(pool, b)
            for b in range(BC):
                load_b(pool, b, 0, b_in[b // BC])
            nc.gpsimd.memset(seg_mask[:, :], 1.0).then_inc(mask_step, 1)
            pool.wait_ge(mask_step, 1)
            for n in range(2):
                segs = seg_mask[n * RB:(n + 1) * RB, :].rearrange("p (s n) -> p s n", s=BC)
                nc.gpsimd.affine_select(out=segs, in_=segs, compare_op=ALU.is_ge, fill=0.0, base=0,
                                        pattern=[[-R, BC], [0, P]], channel_multiplier=1).then_inc(mask_step, 1)
                pool.wait_ge(mask_step, n + 2)
                nc.gpsimd.affine_select(out=segs, in_=segs, compare_op=ALU.is_ge, fill=0.0, base=R - 1,
                                        pattern=[[R, BC], [0, P]], channel_multiplier=-1).then_inc(mask_ready, 1)
                pool.wait_ge(mask_ready, n + 1)
            nc.gpsimd.iota(row_id[:, 0:1], [[0, 1]], base=0, channel_multiplier=1).then_inc(rows_ready, 1)
            pool.wait_ge(start_lo, len(start))
            for b in range(NB):
                e = pool.value_load(ids0[0:1, b:b + 1], min_val=0, max_val=d["a_dn"].shape[0] - 1)
                full = (NKD - 1) * R
                pool.dma_start(a_dn_raw[:, b, 0:full], d["a_dn"][ds(e, 1)].rearrange("a p n -> (a p) n")).then_inc(a_dn_in, 16)
                pool.dma_start(a_dn_raw[0:F0_TAIL, b, full:full + R],
                               d["a_dn_tail"][ds(e, 1)].rearrange("a p n -> (a p) n")).then_inc(a_dn_in, 16)
            nc.gpsimd.memset(pack_raw[:, :], 0.0).then_inc(pack_zero, 1)
            pool.wait_ge(pack_zero, 1)
            for q in range(3):
                for v in range(4):
                    row = 32 * q + SR * v
                    pool.dma_start(pack_raw[row:row + SR, :], d["factors"][q]).then_inc(pack_in, 16)
            pool.wait_ge(up_ready, CH * CUT)
            for b in range(NB):
                load_b(pool, b, 1, b_again_in)
            pool.wait_ge(ids_in[1], 16)
            pool.wait_ge(down_ready, 2 * CH * HK)
            for b in range(NB):
                e = pool.value_load(ids1[0:1, b:b + 1], min_val=0, max_val=d["a1"].shape[0] - 1)
                pool.dma_start(a1_raw[:, b, :], d["a1"][ds(e, 1)].rearrange("a p n -> (a p) n")).then_inc(a1_in, 16)
                row = 3 * PR + b % 2 * R
                pool.dma_start(b1_raw[row:row + R, b // 2, :], d["b1"][ds(e, 1)].rearrange("a r n -> (a r) n")).then_inc(b1_in, 16)

            def tile_lo(ph, i, jj):
                s, n = slot(ph, jj, i), dq_cols(ph)
                pool.wait_ge(w_hi_done, ph.t0 + 2 * i + jj)
                nc.gpsimd.tensor_tensor(w_lo[:, s, n], w_raw[:, s, n], w_hi[:, s, n].bitcast(F32), ALU.subtract).then_inc(w_ready, 1)

            def unit_lo(ph, i, jj, c):
                pool.wait_ge(act_hi_done, ph.g0 + CH * (2 * i + jj) + c + 1)
                j = ds(2 * i + jj, 1)
                nc.gpsimd.tensor_tensor(act_lo[:, j, chunk(c)].rearrange("p a n -> p (a n)"), gate_sum[:, jj % 2, c, :],
                                        act_hi[:, j, chunk(c)].rearrange("p a n -> p (a n)").bitcast(F32), ALU.subtract).then_inc(act_ready, 1)

            tile_lo(named["ffn1 gate/up a"], 0, 0)
            for ph in phases:
                if ph.prep != "dequant":
                    continue

                def join(i, jj, c, ph=ph):
                    u = CH * (2 * i + jj) + c
                    pool.wait_ge(up_scaled, UQ * (ph.f0 + u + 1))
                    nc.gpsimd.tensor_tensor(up_sum[:, jj % 2, c, :], up_sum[:, jj % 2, c, :], up_more[:, jj % 2, c, :],
                                            ALU.add).then_inc(up_joined, 1)

                def step(i, jj, nxt, ni, njj, ph=ph):
                    finish = ph.kind == "gate_up" and (not isinstance(i, int) or 2 * i + jj > 0)
                    if finish:
                        unit_lo(ph, i, jj - 1, 0)
                    if ph.kind == "gate_up":
                        join(i, jj, 0)
                    if nxt is not None:
                        tile_lo(nxt, ni, njj)
                    if finish:
                        unit_lo(ph, i, jj - 1, 1)
                    if ph.kind == "gate_up":
                        join(i, jj, 1)
                    if ph.kind == "down":
                        o = 2 * i + jj
                        chunks = range(0 if ends_with_sums(ph, o) else CH)
                        for c in chunks:
                            pool.wait_ge(down_scaled, CH * (HK * ph.part + o) + c + 1)
                            nc.gpsimd.tensor_tensor(xp[:, o, chunk(c)], xp[:, o, chunk(c)], down_more[:, o % 2, c, :],
                                                    ALU.add).then_inc(more_added, 1)
                        for c in chunks:
                            pool.wait_ge(more_added, CH * (HK * ph.part + o) + c + 1)
                            pool.wait_ge(group_added, ph.a0 + groups_added(ph, o, KQ - 1, c))
                            nc.gpsimd.tensor_tensor(xp[:, o, chunk(c)], xp[:, o, chunk(c)], down_sum[:, o % 2, c, :],
                                                    ALU.add).then_inc(stream_done, 1)

                tile_steps(pool, ph, step, peeled=1)
                if ph.kind == "gate_up":
                    for c in range(CH):
                        unit_lo(ph, ph.tiles // 2, 0, c)

        @block.scalar
        def _(act):
            def integers(ph, i, jj):
                s, n = slot(ph, jj, i), q_cols(ph)
                act.wait_ge(raw_in[s], raw_count(ph, i, jj))
                nc.scalar.activation(w_hi[:, s, n], w_raw[:, s, n].bitcast(I32), ACT.Copy)

            def tile_hi(ph, i, jj):
                s, n = slot(ph, jj, i), slice(0, columns(ph))
                if ph.prep == "split":
                    act.wait_ge(raw_in[s], raw_count(ph, i, jj))
                else:
                    act.wait_ge(w_prod, w_prod_count(ph, i, jj))
                if ph.prep == "dequant":
                    n = dq_cols(ph)
                nc.scalar.activation(w_hi[:, s, n], w_raw[:, s, n], ACT.Copy).then_inc(w_hi_done, 1)

            def hi_of_b(p):
                cols = piece_cols(p)
                n = cols.stop - cols.start
                if p == 0:
                    for c in range(CH):
                        act.wait_ge(b_in[c], 16 * BC)
                elif p > 1:
                    act.wait_ge(b_ready, p - 1)
                if p == CUT:
                    act.wait_ge(b_again_in, 16 * NB)
                raw = b_raw[quarter(3), :, cols]
                nc.scalar.activation(b_hi[quarter(3), p % 2, :, 0:n], raw, ACT.Copy)
                nc.scalar.activation(b_rows[quarter(0), :, cols], raw, ACT.Copy)
                nc.scalar.activation(b_rows[quarter(2), :, cols], raw, ACT.Copy).then_inc(b_hi_done, 1)

            def hi_of_t(base, c, nets):
                n = nets * RB
                act.wait_ge(t_masked, base + c + 1)
                nc.scalar.activation(t_hi[0:n, c, :], gated[0:n, c, :], ACT.Copy).then_inc(t_hi_done, 1)
                for g in range(nets):
                    for half in range(2):
                        for row in (0, 1):
                            last = nc.scalar.activation(t_rows[quarter(row), g, pair_tokens(2 * c + half)],
                                                        gated[quarter(2 * g + half), c, pair_tokens(half)], ACT.Copy)
                last.then_inc(t_hi_rows, 1)

            def hi_of_b1(pair):
                act.wait_ge(b1_in, 16 * NB)
                raw = b1_raw[quarter(3), pair, :]
                nc.scalar.activation(b1_hi[quarter(3), pair, :], raw, ACT.Copy)
                nc.scalar.activation(b1_rows[quarter(0), pair, :], raw, ACT.Copy)
                nc.scalar.activation(b1_rows[quarter(2), pair, :], raw, ACT.Copy).then_inc(b1_hi_done, 1)

            def hi_of_a_dn():
                act.wait_ge(a_dn_in, 16 * 2 * NB)
                for c in range(CH):
                    for rows, k0, k1 in ((P, 0, NKD - 1), (F0_TAIL, NKD - 1, NKD)):
                        nc.scalar.activation(a_dn[0:rows, k0:k1, c, 0:RB].rearrange("p k (b r) -> p k b r", r=R),
                                             a_dn_raw[0:rows, c * BC:(c + 1) * BC, k0 * R:k1 * R].rearrange("p b (k r) -> p k b r", r=R),
                                             ACT.Copy).then_inc(a_dn_hi_done, 1)

            def hi_of_pack():
                act.wait_ge(pack_in, 16 * 12)
                nc.scalar.activation(pack_long[:, :], pack_raw[:, 0:F1], ACT.Copy).then_inc(pack_hi_done, 1)
                nc.scalar.activation(short_hi[:, :], pack_raw[:, F1:PACK], ACT.Copy).then_inc(pack_hi_done, 1)

            def gate_up_tile(ph, i, jj):
                m = widths(ph, i, jj)
                for c in range(CH):
                    n = ph.g0 + CH * (2 * i + jj) + c
                    act.wait_ge(gate_ready, n + 1)
                    if not isinstance(i, int) or n >= CH:
                        act.wait_ge(act_ready, n - 1)
                    nc.scalar.activation(gated[0:m, c, :], unit_banks(ph, i, jj, c)[0][0:m, :], ACT.Silu).then_inc(silu_done, 1)
                    if not ready_together(ph, i, jj):
                        gate_up_hi(ph, i, jj, c)
                if ready_together(ph, i, jj):
                    for c in range(CH):
                        gate_up_hi(ph, i, jj, c)

            def gate_up_hi(ph, i, jj, c):
                m = widths(ph, i, jj)
                act.wait_ge(prod_done, ph.g0 + CH * (2 * i + jj) + c + 1)
                nc.scalar.activation(act_hi[0:m, ds(2 * i + jj, 1), chunk(c)].rearrange("p a n -> p (a n)"),
                                     gated[0:m, c, :], ACT.Copy).then_inc(act_hi_done, 1)

            def unit_hi(ph, i, jj, c):
                act.wait_ge(prod_done, ph.g0 + CH * (2 * i + jj) + c + 1)
                nc.scalar.activation(act_hi[:, ds(2 * i + jj, 1), chunk(c)].rearrange("p a n -> p (a n)"),
                                     gate_sum[:, jj % 2, c, :], ACT.Copy).then_inc(act_hi_done, 1)

            def group_tile(ph, i, jj, nxt, ni, njj):
                s, begun = slot(ph, jj, i), not isinstance(i, int) or 2 * i + jj > 0
                for c in range(CH):
                    u = CH * (2 * i + jj) + c
                    act.wait_ge(group_ready, ph.q0 + GQ * u + 1)
                    act.wait_ge(act_ready, ph.g0 + u - 3 if begun else ph.g0)
                    nc.scalar.activation(gate_sum[:, jj % 2, c, :], group_banks[0], ACT.Copy, scale=s_group[:, s, 0:1]).then_inc(first_scaled, 1)
                    if begun:
                        unit_hi(ph, i, jj - 1, c)
                    for n, up in enumerate((up_sum, up_more)):
                        act.wait_ge(group_ready, ph.q0 + GQ * u + HK + n + 1)
                        nc.scalar.activation(up[:, jj % 2, c, :], ps_down[n][:, :], ACT.Copy, scale=s_group[:, s, HK + n:HK + n + 1]).then_inc(up_scaled, 1)
                    if c == 0:
                        if begun:
                            act.wait_ge(up_ready, ph.g0 + CH * (2 * i + jj))
                        integers(nxt, ni, njj)
                        tile_hi(nxt, ni, njj)
                    act.wait_ge(group_added, ph.a0 + (HK - 1) * (u + 1))
                    nc.scalar.activation(gate_sum[:, jj % 2, c, :], gate_sum[:, jj % 2, c, :], ACT.Silu).then_inc(silu_done, 1)

            def down_tile(ph, o, chunks=range(CH)):
                for c in chunks:
                    if ph.name in ("cond down b", "ffn0 down b"):
                        act.wait_ge(sum_done, ph.d0 + CH * o + c + 1)
                        nc.scalar.activation(h_hi[:, o, chunk(c)], xp[:, o, chunk(c)], ACT.Copy).then_inc(h_hi_done, 1)
                    elif ph.name == "cond1":
                        act.wait_ge(sum_done, ph.d0 + CH * o + c + 1)
                        nc.scalar.activation(y_hi[:, o, chunk(c)], gated[:, c, :], ACT.Copy).then_inc(h_hi_done, 1)
                    elif ph.prep == "dequant" and not ends_with_sums(ph, o):
                        n = CH * o + c
                        act.wait_ge(down_ready, ph.d0 + n + 1)
                        if ph.part or o > 1:
                            act.wait_ge(stream_done, CH * HK * ph.part + n - 2 * CH + 1)
                        nc.scalar.activation(down_sum[:, o % 2, c, :], ps_down[c][:, :], ACT.Copy).then_inc(sum_done, 1)

            def down_first_group(ph, o):
                for c in range(CH):
                    n = CH * (HK * ph.part + o) + c
                    act.wait_ge(group_ready, ph.q0 + down_group(o, 0, c) + 1)
                    if n >= 2 * CH:
                        act.wait_ge(more_added, n - 2 * CH + 1)
                    nc.scalar.activation(down_more[:, o % 2, c, :], group_banks[down_group_bank(down_group(o, 0, c))], ACT.Copy,
                                         scale=group_scale(ph, o, 0)).then_inc(down_scaled, 1)

            def small_t(base, scale):
                for c in range(CH):
                    act.wait_ge(t_sums, base + c + 1)
                    nc.scalar.activation(gated[0:RB, c, :], ps_m[RB:2 * RB, chunk(c)], ACT.Copy, scale=scale).then_inc(t_lo_rows, 1)
                for c in range(CH):
                    hi_of_t(base, c, 1)

            for item in start:
                if item[0] == "w":
                    half = slice(item[1] * HK * P, (item[1] + 1) * HK * P)
                    act.wait_ge(w_first_in[item[1]], 16)
                    nc.scalar.activation(w_hi[:, 0, half], w_raw[:, 0, half], ACT.Copy).then_inc(start_hi, 1)
                else:
                    _, c, k = item
                    act.wait_ge(x_in[c][k], 16)
                    nc.scalar.activation(h_hi[:, k, chunk(c)], xp[:, k, chunk(c)], ACT.Copy).then_inc(start_hi, 1)
            for c in range(CH):
                act.wait_ge(a_gu_in[c], 16 * BC)
                for g in range(2):
                    nc.scalar.activation(a_gu_hi[:, :, c, g], a_gu_raw[:, c * BC:(c + 1) * BC, :].rearrange(
                        "p b (k g r) -> p g k b r", g=2, r=R)[:, g], ACT.Copy).then_inc(a_gu_hi_done, 1)
            tile_hi(phases[0], 0, 1)
            hi_of_b(0)
            act.wait_ge(base_done, CH)
            tile_hi(phases[0], 1, 0)
            for c in range(CH):
                hi_of_t(0, c, 2)
            hi_of_b(1)
            hi_of_b(2)

            for ph in phases:
                if ph.name == "ffn0 down b":
                    act.wait_ge(a1_in, 16 * NB)
                    for c in range(CH):
                        nc.scalar.activation(a1[:, :, c, 0:RB].rearrange("p k (b r) -> p k b r", r=R),
                                             a1_raw[:, c * BC:(c + 1) * BC, :].rearrange("p b (k r) -> p k b r", r=R),
                                             ACT.Copy).then_inc(a1_hi_done, 1)

                def step(i, jj, nxt, ni, njj, ph=ph):
                    if ph.kind == "gate_up" and ph.prep == "dequant":
                        group_tile(ph, i, jj, nxt, ni, njj)
                        return
                    if ph.kind == "down" and ph.prep == "dequant":
                        group_down_step(ph, 2 * i + jj, nxt)
                        return
                    if has_adapters(ph):
                        adapters_step(ph, 2 * i + jj)
                        return
                    if nxt is not None and ph.kind == "gate_up" and ph is not phases[0] and (not isinstance(i, int) or 2 * i + jj > 0):
                        act.wait_ge(up_ready, ph.g0 + CH * (2 * i + jj))
                    if nxt is not None and nxt.prep == "dequant":
                        integers(nxt, ni, njj)
                    if ph is phases[0]:
                        first_phase_weights(tile_hi, 2 * i + jj, lambda count: act.wait_ge(up_ready, count))
                    elif nxt is not None:
                        tile_hi(nxt, ni, njj)
                    if ph.kind == "gate_up":
                        gate_up_tile(ph, i, jj)
                        if ph.layer == "cond":
                            between_tiles(ph, 2 * i + jj)
                    else:
                        down_tile(ph, 2 * i + jj)
                        if ph.name == "cond down a":
                            between_tiles(ph, 2 * i + jj)
                        if ph.name == "ffn0 down a":
                            hi_of_b1(2 * i + jj)

                def group_down_step(ph, o, nxt):
                    for c in range(CH):
                        down_tile(ph, o, range(c, c + 1))
                        if o == 0:
                            unit_hi(gate_up_before[ph], ACT_TILES // 2, 0, c)
                        elif c == 0 and nxt is not None:
                            integers(nxt, (o + 1) // 2 % (HK // 2), (o + 1) % 2)
                            tile_hi(nxt, (o + 1) // 2 % (HK // 2), (o + 1) % 2)
                    if not ends_with_sums(ph, o):
                        down_first_group(ph, o)
                    if o == 0:
                        integers(nxt, 0, 1)
                        tile_hi(nxt, 0, 1)

                def adapters_step(ph, o):
                    if o == 0:
                        tile_hi(ph, 0, 1)
                        small_t(*small_t_of(ph))
                    if o + 2 < HK:
                        act.wait_ge(base_done, base_before(ph) + CH * (o + 1))
                        tile_hi(ph, o // 2 + 1, o % 2)
                    down_tile(ph, o)
                    if o == HK - 2:
                        act.wait_ge(base_done, base_before(ph) + CH * (o + 1))
                        nxt = following[ph]
                        if nxt.prep == "dequant":
                            integers(nxt, 0, 0)
                        tile_hi(nxt, 0, 0)

                def between_tiles(ph, j):
                    p = next_piece(ph, j)
                    if p is not None:
                        hi_of_b(p)
                    if ph is phases[0] and j == 3:
                        hi_of_a_dn()
                    if ph is phases[0] and j == 4:
                        hi_of_pack()

                if ph.name == "ffn1 down a":
                    act.wait_ge(s_in, 16)
                if ph.kind == "gate_up" and ph.d0 > 0:
                    act.wait_ge(down_ready, ph.d0)
                    if ph.q0 > 0:
                        act.wait_ge(group_ready, ph.q0)
                if ph.kind == "down":
                    def step_down(i, jj, nxt, ni, njj, ph=ph, step=step):
                        o = 2 * i + jj
                        if o == 0:
                            if ph.name != "cond1":
                                act.wait_ge(up_ready, ph.g0)
                            else:
                                act.wait_ge(down_ready, ph.d0)
                        elif ph.prep == "dequant":
                            act.wait_ge(group_ready, ph.q0 + KQ * CH * o)
                        elif not has_adapters(ph):
                            act.wait_ge(down_ready, ph.d0 + CH * o)
                        step(i, jj, nxt, ni, njj)
                    tile_steps(act, ph, step_down)
                else:
                    tile_steps(act, ph, step, in_loop=ph.layer != "cond", peeled=1 if ph.prep == "dequant" else 0)

        @block.vector
        def _(dve):
            chain = [0]

            def link(ins):
                chain[0] += 1
                ins.then_inc(sel_step, 1)
                dve.wait_ge(sel_step, chain[0])

            def lo(out_, value, hi):
                return nc.vector.tensor_tensor(out_, value, hi.bitcast(F32), ALU.subtract)

            def tile_product(ph, i, jj):
                s, n = slot(ph, jj, i), columns(ph)
                dve.wait_ge(raw_in[s], raw_count(ph, i, jj))
                if ph.prep == "scale":
                    dve.wait_ge(m_ready, ph.m0 + 2 * i + jj + 1)
                    nc.vector.tensor_tensor(w_raw[:, s, 0:n], w_raw[:, s, 0:n], ps_m[:, 0:n], ALU.mult).then_inc(w_prod, 1)
                else:
                    n = dq_cols(ph)
                    if ph.kind == "gate_up":
                        nc.vector.tensor_copy(s_group[:, s, :], s_group_in[:, s, :])
                    nc.vector.tensor_tensor(w_raw[:, s, n], w_raw[:, s, n].bitcast(I32), s_bc[s][:, 0:n.stop - n.start], ALU.mult).then_inc(w_prod, 1)

            def tile_lo(ph, i, jj):
                s, n = slot(ph, jj, i), slice(0, columns(ph))
                dve.wait_ge(w_hi_done, ph.t0 + 2 * i + jj)
                lo(w_lo[:, s, n], w_raw[:, s, n], w_hi[:, s, n]).then_inc(w_ready, 1)

            def lo_of_b(p):
                cols = piece_cols(p)
                dve.wait_ge(b_hi_done, p + 1)
                raw, hi = b_raw[quarter(3), :, cols], b_hi[quarter(3), p % 2, :, 0:cols.stop - cols.start]
                lo(b_rows[quarter(1), :, cols], raw, hi).then_inc(b_step, 1)
                dve.wait_ge(b_step, p + 1)
                lo(b_rows[quarter(3), :, cols], raw, hi).then_inc(b_ready, 1)

            def lo_of_t(base, c, nets):
                dve.wait_ge(t_hi_done, base + c + 1)
                for g in range(nets):
                    for half in range(2):
                        rows, cols = quarter(2 * g + half), pair_tokens(half)
                        for row in (2, 3):
                            last = lo(t_rows[quarter(row), g, pair_tokens(2 * c + half)], gated[rows, c, cols], t_hi[rows, c, cols])
                last.then_inc(t_lo_rows_done, 1)

            def lo_of_b1(pair):
                dve.wait_ge(b1_hi_done, pair + 1)
                raw, hi = b1_raw[quarter(3), pair, :], b1_hi[quarter(3), pair, :]
                lo(b1_rows[quarter(1), pair, :], raw, hi).then_inc(b1_step, 1)
                dve.wait_ge(b1_step, pair + 1)
                lo(b1_rows[quarter(3), pair, :], raw, hi).then_inc(b1_ready, 1)

            def lo_of_a_dn():
                n = 0
                for c in range(CH):
                    for rows, k0, k1 in ((P, 0, NKD - 1), (F0_TAIL, NKD - 1, NKD)):
                        n += 1
                        dve.wait_ge(a_dn_hi_done, n)
                        hi, low = (a_dn[0:rows, k0:k1, c, x * RB:(x + 1) * RB].rearrange("p k (b r) -> p k b r", r=R) for x in range(2))
                        lo(low, a_dn_raw[0:rows, c * BC:(c + 1) * BC, k0 * R:k1 * R].rearrange("p b (k r) -> p k b r", r=R),
                           hi).then_inc(a_dn_ready, 1)

            def pack_rows():
                dve.wait_ge(rows_ready, 1)
                link(nc.vector.tensor_scalar(row_id[:, 1:2], row_id[:, 0:1], 2, 1, ALU.logical_shift_right, ALU.bitwise_and))
                link(nc.vector.tensor_scalar(row_id[:, 2:3], row_id[:, 0:1], 3, 1, ALU.logical_shift_right, ALU.bitwise_and))
                link(nc.vector.tensor_scalar(row_id[:, 3:4], row_id[:, 0:1], 5, None, ALU.logical_shift_right))
                link(nc.vector.tensor_copy(sel[:, 0:1], row_id[:, 1:2]))
                link(nc.vector.tensor_copy(sel[:, 2:3], row_id[:, 2:3]))
                link(nc.vector.tensor_copy(sel[:, 10:11], row_id[:, 3:4]))
                for a in (0, 2):
                    link(nc.vector.tensor_scalar(sel[:, a + 1:a + 2], sel[:, a:a + 1], -2.0, 1.0, ALU.mult, ALU.add))
                for q in range(3):
                    link(nc.vector.tensor_scalar(sel[:, 11:12], sel[:, 10:11], float(q), None, ALU.is_equal))
                    for a in range(2):
                        link(nc.vector.tensor_tensor(sel[:, 4 + 2 * q + a:5 + 2 * q + a], sel[:, 2 + a:3 + a], sel[:, 11:12], ALU.mult))

            def pack_long_factors():
                dve.wait_ge(pack_hi_done, 2)
                nc.vector.tensor_scalar(pack_raw[:, 0:F1], pack_raw[:, 0:F1], sel[:, 0:1], None, ALU.mult).then_inc(pack_step, 1)
                dve.wait_ge(pack_step, 1)
                nc.vector.scalar_tensor_tensor(out=pack_long[:, :], in0=pack_long[:, :].bitcast(F32), scalar=sel[:, 1:2],
                                               in1=pack_raw[:, 0:F1], op0=ALU.mult, op1=ALU.add).then_inc(pack_ready, 1)

            def pack_short_factors():
                for q in range(3):
                    a = 4 + 2 * q
                    dve.wait_ge(pack_ready, q + 1)
                    nc.vector.tensor_scalar(short_part[:, :], pack_raw[:, F1:PACK], sel[:, a:a + 1], None, ALU.mult).then_inc(pack_step, 1)
                    dve.wait_ge(pack_step, q + 2)
                    nc.vector.scalar_tensor_tensor(out=pack_short[:, q, :], in0=short_hi[:, :].bitcast(F32), scalar=sel[:, a + 1:a + 2],
                                                   in1=short_part[:, :], op0=ALU.mult, op1=ALU.add).then_inc(pack_ready, 1)

            def gate_up_tile(ph, i, jj):
                m = widths(ph, i, jj)
                for c in range(CH):
                    n = ph.g0 + CH * (2 * i + jj) + c
                    dve.wait_ge(silu_done, n + 1)
                    dve.wait_ge(up_ready, n + 1)
                    nc.vector.tensor_tensor(gated[0:m, c, :], gated[0:m, c, :], unit_banks(ph, i, jj, c)[1][0:m, :], ALU.mult).then_inc(prod_done, 1)
                    if not ready_together(ph, i, jj):
                        gate_up_lo(ph, i, jj, c)
                if ready_together(ph, i, jj):
                    for c in range(CH):
                        gate_up_lo(ph, i, jj, c)

            def gate_up_lo(ph, i, jj, c):
                m, j = widths(ph, i, jj), ds(2 * i + jj, 1)
                dve.wait_ge(act_hi_done, ph.g0 + CH * (2 * i + jj) + c + 1)
                lo(act_lo[0:m, j, chunk(c)].rearrange("p a n -> p (a n)"), gated[0:m, c, :],
                   act_hi[0:m, j, chunk(c)].rearrange("p a n -> p (a n)")).then_inc(act_ready, 1)

            def unit_product(ph, i, jj, c):
                n, u = ph.g0 + CH * (2 * i + jj) + c, CH * (2 * i + jj) + c
                dve.wait_ge(silu_done, n + 1)
                dve.wait_ge(up_ready, n + 1)
                dve.wait_ge(up_joined, ph.f0 + u + 1)
                gate, up = gate_sum[:, jj % 2, c, :], up_sum[:, jj % 2, c, :]
                nc.vector.tensor_tensor(up, up, ps_up[c][:, :], ALU.add).then_inc(up_added, 1)
                dve.wait_ge(up_added, ph.f0 + u + 1)
                nc.vector.tensor_tensor(gate, gate, up, ALU.mult).then_inc(prod_done, 1)

            def group_tile(ph, i, jj, nxt, ni, njj):
                for c in range(CH):
                    u = CH * (2 * i + jj) + c
                    dve.wait_ge(first_scaled, ph.f0 + u + 1)
                    for k in range(1, HK):
                        dve.wait_ge(group_ready, ph.q0 + GQ * u + k + 1)
                        if k > 1:
                            dve.wait_ge(group_added, ph.a0 + (HK - 1) * u + k - 1)
                        gate = gate_sum[:, jj % 2, c, :]
                        nc.vector.scalar_tensor_tensor(out=gate, in0=group_banks[k], scalar=s_group[:, slot(ph, jj, i), k:k + 1], in1=gate, op0=ALU.mult, op1=ALU.add).then_inc(group_added, 1)
                        if k == 1 and c == 0:
                            tile_product(nxt, ni, njj)
                    if c > 0:
                        unit_product(ph, i, jj, 0)
                    elif not isinstance(i, int) or 2 * i + jj > 0:
                        unit_product(ph, i, jj - 1, CH - 1)

            def down_tile(ph, o):
                for c in range(0 if ph.prep == "dequant" else CH):
                    n = ph.d0 + CH * o + c
                    here = xp[:, o, chunk(c)]
                    dve.wait_ge(down_ready, n + 1)
                    if ph.name == "cond down a":
                        nc.vector.tensor_copy(here, ps_down[c][:, :]).then_inc(sum_done, 1)
                    elif ph.name == "cond1":
                        if o > 0:
                            dve.wait_ge(h_ready, h_seen(ph) + CH * (o - 1) + c + 1)
                        nc.vector.tensor_scalar(gated[:, c, :], down_bank(ph, o, c)[:, :], bias[:, o:o + 1], None, ALU.add).then_inc(sum_done, 1)
                    else:
                        nc.vector.tensor_tensor(here, here, down_bank(ph, o, c)[:, :], ALU.add).then_inc(sum_done, 1)
                for c in range(0 if ph.prep == "dequant" else CH):
                    here = xp[:, o, chunk(c)]
                    hs = h_seen(ph) + CH * o + c + 1
                    if ph.name in ("cond down b", "ffn0 down b"):
                        dve.wait_ge(h_hi_done, hs)
                        lo(h_lo[:, o, chunk(c)], here, h_hi[:, o, chunk(c)]).then_inc(h_ready, 1)
                    elif ph.name == "cond1":
                        dve.wait_ge(h_hi_done, hs)
                        lo(y_lo[:, o, chunk(c)], gated[:, c, :], y_hi[:, o, chunk(c)]).then_inc(h_ready, 1)
                if ph.prep == "dequant":
                    final = ends_with_sums(ph, o)

                    def stream_sum(c):
                        here = xp[:, o, chunk(c)]
                        dve.wait_ge(down_ready, ph.d0 + CH * o + c + 1)
                        nc.vector.tensor_tensor(here, here, ps_down[c][:, :], ALU.add).then_inc(sum_done, 1)

                    if final:
                        dve.wait_ge(stream_done, CH * HK)
                    for k in range(0 if final else 1, KQ):
                        for c in range(CH):
                            m = down_group(o, k, c)
                            here = xp[:, o, chunk(c)] if final else down_sum[:, o % 2, c, :]
                            if k > (not final):
                                dve.wait_ge(group_added, ph.a0 + groups_added(ph, o, k - 1, c))
                            elif not final:
                                dve.wait_ge(sum_done, ph.d0 + CH * o + c + 1)
                            dve.wait_ge(group_ready, ph.q0 + m + 1)
                            nc.vector.scalar_tensor_tensor(out=here, in0=group_banks[down_group_bank(m)], scalar=group_scale(ph, o, k),
                                                           in1=here, op0=ALU.mult, op1=ALU.add).then_inc(group_added, 1)
                    if final:
                        for c in range(CH):
                            dve.wait_ge(group_added, ph.a0 + groups_added(ph, o, KQ - 1, c))
                            stream_sum(c)

            def small_t(base, scale):
                n = base - CH
                for c in range(CH):
                    dve.wait_ge(t_lo_rows, n + c + 1)
                    nc.vector.scalar_tensor_tensor(out=gated[0:RB, c, :], in0=ps_m[0:RB, chunk(c)], scalar=scale,
                                                   in1=gated[0:RB, c, :], op0=ALU.mult, op1=ALU.add).then_inc(t_added, 1)
                    dve.wait_ge(t_added, n + c + 1)
                    nc.vector.tensor_tensor(gated[0:RB, c, :], gated[0:RB, c, :], seg_mask[0:RB, :], ALU.mult).then_inc(t_masked, 1)
                for c in range(CH):
                    lo_of_t(base, c, 1)

            nc.vector.memset(warm[:, :].bitcast(F32), 0.0).then_inc(warm_zero, 1)
            for n, item in enumerate(start):
                dve.wait_ge(start_hi, n + 1)
                if item[0] == "w":
                    half = slice(item[1] * HK * P, (item[1] + 1) * HK * P)
                    lo(w_lo[:, 0, half], w_raw[:, 0, half], w_hi[:, 0, half]).then_inc(start_lo, 1)
                else:
                    _, c, k = item
                    lo(h_lo[:, k, chunk(c)], xp[:, k, chunk(c)], h_hi[:, k, chunk(c)]).then_inc(start_lo, 1)
            for c in range(CH):
                for g in range(2):
                    dve.wait_ge(a_gu_hi_done, 2 * c + g + 1)
                    lo(a_gu_lo[:, :, c, g], a_gu_raw[:, c * BC:(c + 1) * BC, :].rearrange("p b (k g r) -> p g k b r", g=2, r=R)[:, g],
                       a_gu_hi[:, :, c, g]).then_inc(a_gu_ready, 1)
            tile_lo(phases[0], 0, 1)
            pack_rows()
            dve.wait_ge(mask_ready, 2)
            for c in range(CH):
                dve.wait_ge(t_sums, c + 1)
                nc.vector.scalar_tensor_tensor(out=gated[:, c, :], in0=ps_m[:, chunk(c)], scalar=0.5, in1=seg_mask[:, :],
                                               op0=ALU.mult, op1=ALU.mult).then_inc(t_masked, 1)
                if c == 0:
                    lo_of_b(0)
            tile_lo(phases[0], 1, 0)
            for c in range(CH):
                lo_of_t(0, c, 2)
            lo_of_b(1)
            lo_of_b(2)

            for ph in phases:
                if ph.name == "ffn0 down b":
                    for c in range(CH):
                        dve.wait_ge(a1_hi_done, c + 1)
                        hi, low = (a1[:, :, c, x * RB:(x + 1) * RB].rearrange("p k (b r) -> p k b r", r=R) for x in range(2))
                        lo(low, a1_raw[:, c * BC:(c + 1) * BC, :].rearrange("p b (k r) -> p k b r", r=R), hi).then_inc(a1_ready, 1)
                if ph.name == "ffn0 down a":
                    dve.wait_ge(x_again, 16)
                if ph.name == "cond1":
                    dve.wait_ge(bias_in, 16)

                if ph.name == "ffn1 down a":
                    dve.wait_ge(s_in, 16)

                def step(i, jj, nxt, ni, njj, ph=ph):
                    if ph.kind == "gate_up" and ph.prep == "dequant":
                        group_tile(ph, i, jj, nxt, ni, njj)
                        return
                    if has_adapters(ph):
                        adapters_step(ph, 2 * i + jj)
                        return
                    if nxt is not None and nxt.prep != "split":
                        tile_product(nxt, ni, njj)
                    if ph is phases[0]:
                        first_phase_weights(tile_lo, 2 * i + jj)
                    elif nxt is not None and nxt.prep != "dequant":
                        tile_lo(nxt, ni, njj)
                    if ph.kind == "gate_up":
                        gate_up_tile(ph, i, jj)
                        if ph.layer == "cond":
                            between_tiles(ph, 2 * i + jj)
                    else:
                        down_tile(ph, 2 * i + jj)
                        if ph.name == "cond down a":
                            between_tiles(ph, 2 * i + jj)
                        if ph.name == "ffn0 down a":
                            lo_of_b1(2 * i + jj)

                def adapters_step(ph, o):
                    nxt = following[ph]
                    if o == 0:
                        tile_lo(ph, 0, 1)
                        small_t(*small_t_of(ph))
                    if o + 2 < HK:
                        tile_lo(ph, o // 2 + 1, o % 2)
                    if o == HK - 2:
                        tile_product(nxt, 0, 0)
                    down_tile(ph, o)
                    if o == HK - 2 and nxt.prep != "dequant":
                        tile_lo(nxt, 0, 0)

                def between_tiles(ph, j):
                    p = next_piece(ph, j)
                    if p is not None:
                        lo_of_b(p)
                    if ph is phases[0] and j == 3:
                        lo_of_a_dn()
                    if ph is phases[0] and j == 4:
                        pack_long_factors()
                    if ph is phases[0] and j == 5:
                        pack_short_factors()

                tile_steps(dve, ph, step, in_loop=ph.layer != "cond", peeled=1 if ph.prep == "dequant" else 0)
                if ph.kind == "gate_up" and ph.prep == "dequant":
                    unit_product(ph, ph.tiles // 2, 0, CH - 1)

        @block.tensor
        def _(pe):
            def sums(ps, m, s, col, ks, rhs_hi, rhs_lo, rows=lambda k: P, before=lambda k: None, start=True, stop=False):
                last = None
                for n, k in enumerate(ks):
                    before(k)
                    r = rows(k)
                    cols = slice(col + k * P, col + k * P + m)
                    nc.tensor.matmul(ps[0:m, :], w_hi[0:r, s, cols], rhs_hi(k, r), start=start and n == 0, stop=False)
                    nc.tensor.matmul(ps[0:m, :], w_hi[0:r, s, cols], rhs_lo(k, r), start=False, stop=False)
                    last = nc.tensor.matmul(ps[0:m, :], w_lo[0:r, s, cols], rhs_hi(k, r), start=False,
                                            stop=stop and n == len(ks) - 1)
                return last

            def adapters(ps, m, b, col, g, c):
                for half in range(2):
                    pair = 2 * c + half
                    last = nc.tensor.matmul(ps[0:m, pair_tokens(half)], b[:, pair, col:col + m], t_rows[:, g, pair_tokens(pair)],
                                            start=False, stop=half == 1)
                return last

            def adapter_t(c, a_cols, ks, rhs_hi, rhs_lo, rows=lambda k: P, start=True, stop=True):
                last = None
                for n, k in enumerate(ks):
                    r = rows(k)
                    nc.tensor.matmul(ps_m[:, chunk(c)], a_cols(k)[0:r, :], rhs_hi(k, r), start=start and n == 0, stop=False)
                    last = nc.tensor.matmul(ps_m[:, chunk(c)], a_cols(k)[0:r, :], rhs_lo(k, r), start=False,
                                            stop=stop and n == len(ks) - 1)
                return last

            def scales(ph, i, jj):
                n = ph.m0 + 2 * i + jj
                if not (isinstance(i, int) and n == 0):
                    pe.wait_ge(w_prod, n)
                else:
                    pe.wait_ge(pack_ready, 4)
                last = None
                if ph.kind == "gate_up":
                    for g in range(2):
                        for k in range(HK):
                            q = g * HK + k
                            last = nc.tensor.matmul(ps_m[:, q * P:(q + 1) * P], pack_short[:, g, k * P:(k + 1) * P],
                                                    pack_long[:, ds((ph.first + 2 * i + jj) * P, P)], start=True, stop=True)
                else:
                    o = 2 * i + jj
                    for k in range(k_count(ph)):
                        last = nc.tensor.matmul(ps_m[:, k * P:(k + 1) * P], pack_long[:, (ph.first + k) * P:(ph.first + k + 1) * P],
                                                pack_short[:, 2, o * P:(o + 1) * P], start=True, stop=True)
                last.then_inc(m_ready, 1)

            def net_input(ph):
                return (y_hi, y_lo) if ph.layer == "ffn1" else (h_hi, h_lo)

            def gate_up_tile(ph, i, jj):
                s, m = slot(ph, jj, i), widths(ph, i, jj)
                hi, lo = net_input(ph)
                pe.wait_ge(w_ready, ph.t0 + 2 * i + jj)
                for c in range(CH):
                    n = ph.g0 + CH * (2 * i + jj) + c
                    for g, (ps, read, ready) in enumerate(((ps_gate, silu_done, gate_ready), (ps_up, prod_done, up_ready))):
                        if not isinstance(i, int) or n >= CH:
                            pe.wait_ge(read, n - 3 if ph is phases[0] and 2 * i + jj == 2 else n - 1)

                        def input_ready(k, c=c, g=g):
                            if g == 0 and ph.name == "ffn0 gate/up a" and jj == 0 and isinstance(i, int) and i == 0:
                                pe.wait_ge(h_ready, CH * k + c + 1)

                        last = sums(ps[c], m, s, g * HK * P, range(HK), lambda k, r, c=c: hi[0:r, k, chunk(c)],
                                    lambda k, r, c=c: lo[0:r, k, chunk(c)], before=input_ready, stop=ph.layer != "cond")
                        if ph.layer == "cond":
                            last = gate_up_adapters(ps[c], m, ph, 2 * i + jj, g, c)
                        last.then_inc(ready, 1)

            def gate_up_adapters(ps, m, ph, j, g, c):
                pe.wait_ge(t_hi_rows, c + 1)
                pe.wait_ge(t_lo_rows_done, c + 1)
                pe.wait_ge(b_ready, b_piece(ph, j) + 1)
                return adapters(ps, m, b_rows, piece_cols(b_piece(ph, j)).start + g * m, g, c)

            def unit_base(ph, j, c):
                s = slot(ph, j, 0)
                for g, ps in enumerate(unit_banks(ph, 0, j, c)):
                    def input_ready(k, c=c, g=g):
                        if j == 0:
                            pe.wait_ge(start_lo, max(started("w", g), started("x", c, k)))
                    last = sums(ps, P, s, g * HK * P, range(HK), lambda k, r, c=c: h_hi[:, k, chunk(c)],
                                lambda k, r, c=c: h_lo[:, k, chunk(c)], before=input_ready)
                if j == 0:
                    last.then_inc(base_done, 1)

            def first_tiles(ph):
                for c in range(CH):
                    unit_base(ph, 0, c)
                for c in range(CH):
                    pe.wait_ge(a_gu_ready, 2 * (c + 1))
                    for k in range(HK):
                        a_h, a_l = (a[:, k, c].rearrange("p g b r -> p (g b r)") for a in (a_gu_hi, a_gu_lo))
                        for n, (a, x) in enumerate(((a_h, h_hi), (a_h, h_lo), (a_l, h_hi))):
                            last = nc.tensor.matmul(ps_m[:, chunk(c)], a, x[:, k, chunk(c)], start=k == 0 and n == 0,
                                                    stop=k == HK - 1 and n == 2)
                    last.then_inc(t_sums, 1)
                pe.wait_ge(w_ready, 1)
                unit_base(ph, 1, 0)
                pe.wait_ge(t_masked, CH)
                unit_base(ph, 1, 1)
                for j in range(2):
                    for c in range(CH):
                        unit_adapters(ph, j, c)

            def unit_adapters(ph, j, c):
                for g, (ps, ready) in enumerate(zip(unit_banks(ph, 0, j, c), (gate_ready, up_ready))):
                    gate_up_adapters(ps, P, ph, j, g, c).then_inc(ready, 1)

            def group(ps, s, col, hi, lo):
                nc.tensor.matmul(ps, w_hi[:, s, col:col + P], hi, start=True, stop=False)
                nc.tensor.matmul(ps, w_hi[:, s, col:col + P], lo, start=False, stop=True).then_inc(group_ready, 1)

            def group_tile(ph, i, jj):
                s = slot(ph, jj, i)
                first = isinstance(i, int) and 2 * i + jj == 0
                pe.wait_ge(w_ready, ph.t0 + 2 * i + jj)
                for c in range(CH):
                    u = CH * (2 * i + jj) + c
                    for k in range(HK):
                        if first and ph.part == 0:
                            pe.wait_ge(h_ready, 2 * CH * HK + CH * k + c + 1)
                        if first and c == 0:
                            if ph.part:
                                pe.wait_ge(*last_down_use(k))
                        elif k == 0:
                            pe.wait_ge(first_scaled, ph.f0 + u)
                        else:
                            pe.wait_ge(group_added, ph.a0 + (HK - 1) * (u - 1) + k)
                        group(group_banks[k], s, k * P, y_hi[:, k, chunk(c)], y_lo[:, k, chunk(c)])
                    for n in range(UQ):
                        if first and c == 0:
                            pe.wait_ge(sum_done, ph.d0 - 1 + n)
                        else:
                            pe.wait_ge(up_scaled, UQ * (ph.f0 + u - 1) + n + 1)
                        group(ps_down[n][:, :], s, (HK + n) * P, y_hi[:, n, chunk(c)], y_lo[:, n, chunk(c)])
                    if not first:
                        pe.wait_ge(up_added, ph.f0 + u - 1)
                    elif ph.part:
                        pe.wait_ge(*last_down_use(HK + c))
                    sums(ps_up[c], P, s, HK * P, range(UQ, HK), lambda k, r, c=c: y_hi[:, k, chunk(c)],
                         lambda k, r, c=c: y_lo[:, k, chunk(c)], stop=True).then_inc(up_ready, 1)

            def last_down_use(bank):
                return group_read(named["ffn1 down a"], max(m for m in range(KQ * CH * HK) if down_group_bank(m) == bank))

            def down_groups(ph, o):
                s = slot(ph, o, 0)
                g0 = ph.g0 - CH * ACT_TILES
                for n in range(KQ):
                    for c in range(CH):
                        k, m = DQ_DOWN // P + n, down_group(o, n, c)
                        if m >= len(group_banks):
                            pe.wait_ge(*group_read(ph, m - len(group_banks)))
                        else:
                            bank = down_group_bank(m)
                            if bank == 0:
                                pe.wait_ge(first_scaled, ph.f0)
                            elif bank < HK:
                                pe.wait_ge(group_added, ph.a0 - (HK - 1) + bank)
                            else:
                                pe.wait_ge(up_added, ph.f0 - (len(group_banks) - 1 - bank))
                        if o == 0:
                            pe.wait_ge(act_ready, g0 + CH * k + c + 1)
                        group(group_banks[down_group_bank(m)], s, k * P, act_hi[:, k, chunk(c)], act_lo[:, k, chunk(c)])

            def down_base(ph, o, c):
                n, s = ph.d0 + CH * o + c, slot(ph, o, 0)
                if c == 0:
                    pe.wait_ge(w_ready, ph.t0 + o)
                if ph.prep == "dequant" and o == 0:
                    pe.wait_ge(up_scaled, UQ * (ph.f0 - 1) + c + 1)
                elif has_adapters(ph) and o == 1:
                    pe.wait_ge(prod_done, ph.g0)
                elif n >= 2:
                    pe.wait_ge(sum_done, n - 1 if o == 0 or not has_adapters(ph) else n - 3)
                g0 = ph.g0 - CH * k_count(ph)
                ks = range(DQ_DOWN // P if ph.prep == "dequant" else k_count(ph))

                def input_ready(k):
                    if o > 0:
                        return
                    if ph.layer == "cond1":
                        pe.wait_ge(h_ready, CH * HK + CH * k + c + 1)
                    else:
                        pe.wait_ge(act_ready, g0 + CH * k + c + 1)

                hi, lo = (h_hi, h_lo) if ph.layer == "cond1" else (act_hi, act_lo)
                return sums(down_bank(ph, o, c), P, s, 0, ks, lambda k, r: hi[0:r, k, chunk(c)],
                            lambda k, r: lo[0:r, k, chunk(c)], rows=lambda k: k_rows(ph, k), before=input_ready,
                            stop=not has_adapters(ph))

            def down_adapters(ph, o, c):
                if ph.name == "cond1":
                    pe.wait_ge(b1_ready, PAIRS)
                    pe.wait_ge(t_hi_rows, 2 * CH + c + 1)
                    pe.wait_ge(t_lo_rows_done, 2 * CH + c + 1)
                    return adapters(down_bank(ph, o, c), P, b1_rows, o * P, 0, c)
                pe.wait_ge(b_ready, NBP)
                pe.wait_ge(t_hi_rows, CH + c + 1)
                pe.wait_ge(t_lo_rows_done, CH + c + 1)
                return adapters(down_bank(ph, o, c), P, b_rows, piece_cols(NKD).start + o * P, 0, c)

            def t_of(ph, c):
                if ph.name == "cond down b":
                    t_down(ph, c)
                    return
                pe.wait_ge(a1_ready, CH)
                pe.wait_ge(h_ready, 2 * CH * HK - CH + c + 1)
                adapter_t(c, lambda k: a1[:, k, c, :], range(HK), lambda k, r: h_hi[:, k, chunk(c)],
                          lambda k, r: h_lo[:, k, chunk(c)]).then_inc(t_sums, 1)

            def t_down(ph, c):
                ks = range(k_count(ph))
                pe.wait_ge(a_dn_ready, 4)
                pe.wait_ge(act_ready, ph.g0 - CH + c + 1)
                last = adapter_t(c, lambda k: a_dn[:, ph.first + k, c, :], ks, lambda k, r: act_hi[0:r, k, chunk(c)],
                                 lambda k, r: act_lo[0:r, k, chunk(c)], rows=lambda k: k_rows(ph, k), start=ph.part == 0, stop=ph.part == 1)
                if ph.part == 1:
                    last.then_inc(t_sums, 1)

            pe.wait_ge(warm_zero, 1)
            for n in range(WARM):
                nc.tensor.matmul(ps_m[:, 0:CT], warm[:, 0:P], warm[:, :], start=n == 0, stop=n == WARM - 1)

            for ph in phases:
                def step(i, jj, nxt, ni, njj, ph=ph):
                    if nxt is not None and nxt.prep == "scale" and not has_adapters(ph):
                        scales(nxt, ni, njj)
                    if ph.name == "cond down b" and 2 * i + jj == HK - 2:
                        scales(following[ph], 0, 0)
                    if ph.kind == "gate_up" and ph.prep == "dequant":
                        group_tile(ph, i, jj)
                        return
                    if ph is phases[0] and 2 * i + jj == 0:
                        first_tiles(ph)
                        return
                    if ph is phases[0] and 2 * i + jj == 1:
                        return
                    if ph.kind == "gate_up":
                        gate_up_tile(ph, i, jj)
                        return
                    o = 2 * i + jj
                    if ph.prep == "dequant":
                        if ends_with_sums(ph, o):
                            pe.wait_ge(w_ready, ph.t0 + o)
                            down_groups(ph, o)
                        for c in range(CH):
                            down_base(ph, o, c).then_inc(down_ready, 1)
                        if not ends_with_sums(ph, o):
                            down_groups(ph, o)
                        return
                    if not has_adapters(ph):
                        for c in range(CH):
                            down_base(ph, o, c).then_inc(down_ready, 1)
                        return
                    if o == 0:
                        if ph.name == "cond1":
                            down_base(ph, o, 0).then_inc(base_done, 1)
                        t_of(ph, 0)
                        if ph.name != "cond1":
                            down_base(ph, o, 0).then_inc(base_done, 1)
                        t_of(ph, 1)
                        down_base(ph, o, 1).then_inc(base_done, 1)
                        return
                    for c in range(CH):
                        down_base(ph, o, c).then_inc(base_done, 1)
                        if o > 1:
                            down_adapters(ph, o, c).then_inc(down_ready, 1)
                    if o == 1:
                        for oo in range(2):
                            for c in range(CH):
                                down_adapters(ph, oo, c).then_inc(down_ready, 1)

                tile_steps(pe, ph, step, in_loop=ph.layer != "cond", peeled=0 if ph.name == "ffn0 gate/up b" else 1)
                if ph.name == "cond down a":
                    for c in range(CH):
                        t_down(ph, c)


def _lay_out(i):
    import numpy as np

    def tiles(w, k, f):
        o, n = w.shape
        return w.T.reshape(n // P, P, o // f, f).transpose(2, 1, 0, 3)

    def gate_up(g, u, f=P):
        return np.concatenate([tiles(g, HK, f), tiles(u, HK, f)], axis=2).reshape(-1, P, 2 * HK * f)

    def down(w, parts):
        return np.stack([tiles(w[:, a:b], 0, P).reshape(HK, P, -1) for a, b in parts])

    full = F0 // P * P
    cut = CUT * P
    half = F1 // 2
    cg, cu, cd = i["L0_cond_W_gate"], i["L0_cond_W_up"], i["L0_cond_W_down"]
    a = np.stack([i["L0_cond_A_gate"][0], i["L0_cond_A_up"][0]], axis=1)
    n_id = a.shape[0]
    a_dn = i["L0_cond_A_down"][0].transpose(0, 2, 1)
    bg, bu = i["L0_cond_B_gate"][0], i["L0_cond_B_up"][0]
    b0 = np.concatenate([b[:, f:f + P] for f in range(0, F0, P) for b in (bg, bu)] + [i["L0_cond_B_down"][0]], axis=1)
    factors = np.stack([
        np.concatenate([i["L0_ffn_gate_su"].T, i["L0_ffn_gate_sv"]], axis=1),
        np.concatenate([i["L0_ffn_up_su"].T, i["L0_ffn_up_sv"]], axis=1),
        np.concatenate([i["L0_ffn_down_sv"], i["L0_ffn_down_su"].T], axis=1)])
    s_up = i["L1_ffn_up_s"].reshape(F1 // P, P, HK).transpose(0, 2, 1)[:, UQ:]
    s_dn = i["L1_ffn_down_s"].reshape(HK, P, 2, ACT_TILES).transpose(2, 0, 3, 1)[:, :, :DQ_DOWN // P]
    s_group = np.concatenate([i["L1_ffn_gate_s"], i["L1_ffn_up_s"][:, :UQ]], axis=1)
    a1 = i["L1_cond_lora_As"]
    arrays = {
        "x": i["x"].reshape(TOK, H).T.reshape(HK, P, TOK),
        "ids0": i["itok_B_2_6"].reshape(1, NB),
        "ids1": i["itok_B_0_23"].reshape(1, NB),
        "cond_gu": gate_up(cg[:full], cu[:full]),
        "cond_gu_tail": gate_up(cg[full:], cu[full:], F0_TAIL)[0],
        "cond_dn_a": down(cd, [(0, cut)])[0],
        "cond_dn_b": down(cd, [(cut, full)])[0],
        "cond_dn_tail": cd[:, full:].T.reshape(F0_TAIL, HK, P).transpose(1, 0, 2),
        "a_gu": a.reshape(n_id, 2, R, HK, P).transpose(0, 4, 3, 1, 2).reshape(n_id, P, 2 * HK * R),
        "a_dn": a_dn[:, :full].reshape(n_id, full // P, P, R).transpose(0, 2, 1, 3).reshape(n_id, P, -1),
        "a_dn_tail": a_dn[:, full:],
        "b0": b0.transpose(0, 2, 1),
        "factors": factors,
        "ffn0_gu": gate_up(i["L0_ffn_gate_w"], i["L0_ffn_up_w"]),
        "ffn0_dn": down(i["L0_ffn_down_w"], [(0, half), (half, F1)]),
        "cond1_w": tiles(i["L1_cond_W"], HK, P).reshape(HK, P, H),
        "cond1_b": i["L1_cond_b"].reshape(HK, P).T,
        "a1": a1.reshape(-1, HK, P, R).transpose(0, 2, 1, 3).reshape(-1, P, HK * R),
        "b1": i["L1_cond_lora_Bs"],
        "ffn1_gu": gate_up(i["L1_ffn_gate_q"], i["L1_ffn_up_q"]),
        "ffn1_dn": down(i["L1_ffn_down_q"], [(0, half), (half, F1)]),
        "ffn1_up_s": s_up.reshape(F1 // P, DQ_UP),
        "ffn1_dn_s": s_dn.reshape(2, HK, DQ_DOWN),
        "ffn1_group_s": s_group.reshape(F1 // P, P, GQ),
        "ffn1_down_s": i["L1_ffn_down_s"].reshape(HK, P, F1 // P).transpose(1, 0, 2).reshape(P, -1),
    }
    return {k: np.ascontiguousarray(v) for k, v in arrays.items()}


def kernel(**inputs):
    import numpy as np
    import concourse.bacc as bacc
    from concourse.bass_utils import run_bass_kernel_spmd

    arrays = _lay_out({k: np.asarray(v) for k, v in inputs.items()})
    nc = bacc.Bacc("TRN2", target_bir_lowering=False, num_devices=1)
    d = {k: nc.dram_tensor(f"in_{k}", v.shape, mybir.dt.from_np(v.dtype), kind="ExternalInput").ap() for k, v in arrays.items()}
    out = nc.dram_tensor("out_t", (HK, P, TOK), F32, kind="ExternalOutput").ap()
    adaln_ffn(nc, d, out)
    r = run_bass_kernel_spmd(nc, [{f"in_{k}": v for k, v in arrays.items()}], core_ids=[0])
    got = r.results[0]["out_t"]
    return np.ascontiguousarray(got.reshape(H, TOK).T.reshape(NB, TOK // NB, H))
```
